# Optimizing a Trainium2 kernel written in Bass

```python
import numpy as np
import jax
import jax.numpy as jnp

def _softmax(x, axis=-1):
    return jax.nn.softmax(x, axis=axis)

def _gelu(x):
    return jax.nn.gelu(x, approximate=True)

def _silu(x):
    return jax.nn.silu(x)

def _sigmoid(x):
    return jax.nn.sigmoid(x)

def _layernorm(x, axis=-1, eps=1e-05):
    m = jnp.mean(x, axis=axis, keepdims=True)
    v = jnp.var(x, axis=axis, keepdims=True)
    return (x - m) / jnp.sqrt(v + eps)

def _scatter_add(tgt, idx, src, axis=0):
    return tgt.at[idx].add(src)

def _segment_sum(src, seg, n):
    return jax.ops.segment_sum(src, seg, n)
kernel_name = 'mk_decoder_preln_d1_seqx_r4_3dbcfa'

def setup_inputs(seed: int=0):
    np.random.seed(seed)
    _w = jnp.asarray

    def _rec_inputs():
        import jax
        import jax.numpy as jnp
        _rk = jax.random.key(seed)
        x = 7.22e-05 + 1 * jax.random.normal(jax.random.fold_in(_rk, 1), (8, 256, 512), jnp.float32)
        _lenS = 256 - jax.random.randint(jax.random.fold_in(_rk, 7), (8,), 0, max(1, 256 // 4) + 1, jnp.int32)
        _lenS2 = 256 - jax.random.randint(jax.random.fold_in(_rk, 8), (8,), 0, max(1, 256 // 4) + 1, jnp.int32)
        _ctx_2048P = jax.random.normal(jax.random.fold_in(_rk, 11), (8, 16, 512), jnp.float32)
        _ctx_2048c = jax.random.dirichlet(jax.random.fold_in(_rk, 511), 0.3 * jnp.ones((16,), jnp.float32), (8, 256))
        _ctx_2048t = jnp.einsum('bsk,bkd->bsd', _ctx_2048c, _ctx_2048P)
        _ctx_2048t = _ctx_2048t * jax.lax.rsqrt(jnp.mean(jnp.square(_ctx_2048t)) + 1e-12) * 0.953939
        ctx_2048 = 4.13588e-05 + 0.999923 * (_ctx_2048t + 0.3 * jax.random.normal(jax.random.fold_in(_rk, 611), (8, 256, 512), jnp.float32))
        return (x, ctx_2048)
    x, ctx_2048 = _rec_inputs()

    def _L0_attn_setup():
        import jax, jax.numpy as jnp
        import numpy as np
        EPS = 1e-06

        def rms_norm(x, scale):
            x32 = x.astype(jnp.float32)
            mean2 = jnp.mean(jnp.square(x32), axis=-1, keepdims=True)
            return x32 * jax.lax.rsqrt(mean2 + EPS) * scale
        key = jax.random.key(seed)
        ks = jax.random.split(key, 7)
        B, S, E, H, D = (2, 512, 512, 16, 128)
        w_std = 1.0 / np.sqrt(E)
        x = jax.random.normal(ks[0], (B, S, E), jnp.float32)
        wq = jax.random.normal(ks[1], (E, H, D), jnp.float32) * w_std
        wk = jax.random.normal(ks[2], (E, H, D), jnp.float32) * w_std
        wv = jax.random.normal(ks[3], (E, H, D), jnp.float32) * w_std
        wo = jax.random.normal(ks[4], (H, D, E), jnp.float32) * (1.0 / np.sqrt(H * D))
        q_scale = jnp.ones((D,), jnp.float32)
        k_scale = jnp.ones((D,), jnp.float32)
        return {'x': x, 'wq': wq, 'wk': wk, 'wv': wv, 'wo': wo, 'q_scale': q_scale, 'k_scale': k_scale}
    _L0_attn_all = _L0_attn_setup()
    _L0_attn_in = {k: v for k, v in _L0_attn_all.items() if k in ('wq', 'wk', 'wv', 'wo', 'q_scale', 'k_scale')}
    del _L0_attn_all

    def _L0_xattn_setup():
        import jax, jax.numpy as jnp
        import numpy as np
        B, S, DIM, HD = (4, 256, 512, 128)
        H = DIM // HD
        GN_EPS = 0.001

        def _decay_masks(n_heads, seq_len):
            gam = 1.0 - 2.0 ** (-5.0 - jnp.arange(n_heads, dtype=jnp.float32))
            idx = jnp.arange(seq_len, dtype=jnp.float32)
            expo = idx[None, :] - idx[:, None]
            D = jnp.where(expo[None, :, :] <= 0, gam[:, None, None] ** expo[None, :, :], 0.0)
            return D / jnp.sqrt(D.sum(axis=-1))[:, None, :]
        key = jax.random.key(seed)
        ks = jax.random.split(key, 8)
        x = jax.random.normal(ks[0], (B, S, DIM), dtype=jnp.float32)
        k = jax.random.normal(ks[1], (B, S, DIM), dtype=jnp.float32)
        v = jax.random.normal(ks[2], (B, S, DIM), dtype=jnp.float32)
        Wh = jax.random.normal(ks[3], (H, HD, HD), dtype=jnp.float32) / np.sqrt(HD)
        wg_w = jax.random.normal(ks[4], (DIM, DIM), dtype=jnp.float32) / np.sqrt(DIM)
        wo_w = jax.random.normal(ks[5], (DIM, DIM), dtype=jnp.float32) / np.sqrt(DIM)
        gn_gamma = jnp.ones((DIM,), dtype=jnp.float32)
        gn_beta = jnp.zeros((DIM,), dtype=jnp.float32)
        return {'x': x, 'k': k, 'v': v, 'Wh': Wh, 'wg_w': wg_w, 'wo_w': wo_w, 'gn_gamma': gn_gamma, 'gn_beta': gn_beta}
    _L0_xattn_all = _L0_xattn_setup()
    _L0_xattn_in = {k: v for k, v in _L0_xattn_all.items() if k in ('Wh', 'wg_w', 'wo_w', 'gn_gamma', 'gn_beta')}
    del _L0_xattn_all

    def _L0_ffn_setup():
        import jax, jax.numpy as jnp
        import numpy as np
        B, S, H = (2, 512, 512)
        E, K = (16, 4)
        I_MOE, I_SH = (352, 1408)
        key = jax.random.key(seed)
        ks = jax.random.split(key, 9)

        def w(k, shape, fan_in):
            return jax.random.normal(k, shape, jnp.float32) * fan_in ** (-0.5)
        return {'hidden_states': jax.random.normal(ks[0], (B, S, H), jnp.float32), 'router_w': w(ks[1], (E, H), H), 'w_gate': w(ks[2], (E, H, I_MOE), H), 'w_up': w(ks[3], (E, H, I_MOE), H), 'w_down': w(ks[4], (E, I_MOE, H), I_MOE), 'sh_gate': w(ks[5], (H, I_SH), H), 'sh_up': w(ks[6], (H, I_SH), H), 'sh_down': w(ks[7], (I_SH, H), I_SH), 'sh_gate_w': w(ks[8], (H, 1), H)}
    _L0_ffn_all = _L0_ffn_setup()
    _L0_ffn_in = {k: v for k, v in _L0_ffn_all.items() if k in ('router_w', 'w_gate', 'w_up', 'w_down', 'sh_gate', 'sh_up', 'sh_down', 'sh_gate_w')}
    del _L0_ffn_all
    return {'x': x, 'ctx_2048': ctx_2048, 'L0_attn_wq': _L0_attn_in['wq'], 'L0_attn_wk': _L0_attn_in['wk'], 'L0_attn_wv': _L0_attn_in['wv'], 'L0_attn_wo': _L0_attn_in['wo'], 'L0_attn_q_scale': _L0_attn_in['q_scale'], 'L0_attn_k_scale': _L0_attn_in['k_scale'], 'L0_xattn_Wh': _L0_xattn_in['Wh'], 'L0_xattn_wg_w': _L0_xattn_in['wg_w'], 'L0_xattn_wo_w': _L0_xattn_in['wo_w'], 'L0_xattn_gn_gamma': _L0_xattn_in['gn_gamma'], 'L0_xattn_gn_beta': _L0_xattn_in['gn_beta'], 'L0_ffn_router_w': _L0_ffn_in['router_w'], 'L0_ffn_w_gate': _L0_ffn_in['w_gate'], 'L0_ffn_w_up': _L0_ffn_in['w_up'], 'L0_ffn_w_down': _L0_ffn_in['w_down'], 'L0_ffn_sh_gate': _L0_ffn_in['sh_gate'], 'L0_ffn_sh_up': _L0_ffn_in['sh_up'], 'L0_ffn_sh_down': _L0_ffn_in['sh_down'], 'L0_ffn_sh_gate_w': _L0_ffn_in['sh_gate_w']}

def reference(x, ctx_2048, L0_attn_wq, L0_attn_wk, L0_attn_wv, L0_attn_wo, L0_attn_q_scale, L0_attn_k_scale, L0_xattn_Wh, L0_xattn_wg_w, L0_xattn_wo_w, L0_xattn_gn_gamma, L0_xattn_gn_beta, L0_ffn_router_w, L0_ffn_w_gate, L0_ffn_w_up, L0_ffn_w_down, L0_ffn_sh_gate, L0_ffn_sh_up, L0_ffn_sh_down, L0_ffn_sh_gate_w):
    import jax
    import jax.numpy as jnp

    def _L0_attn_ref(x, wq, wk, wv, wo, q_scale, k_scale):
        import jax, jax.numpy as jnp
        import numpy as np
        EPS = 1e-06

        def rms_norm(x, scale):
            x32 = x.astype(jnp.float32)
            mean2 = jnp.mean(jnp.square(x32), axis=-1, keepdims=True)
            return x32 * jax.lax.rsqrt(mean2 + EPS) * scale
        q = jnp.einsum('bse,ehd->bshd', x, wq)
        k = jnp.einsum('bse,ehd->bshd', x, wk)
        v = jnp.einsum('bse,ehd->bshd', x, wv)
        qn = rms_norm(q, q_scale)
        kn = rms_norm(k, k_scale)
        scores = jnp.einsum('bqhd,bkhd->bhqk', qn, kn)
        attn = jax.nn.softmax(scores, axis=-1)
        out = jnp.einsum('bhqk,bkhd->bqhd', attn, v)
        return jnp.einsum('bqhd,hde->bqe', out, wo)

    def _L0_xattn_ref(x, k, v, Wh, wg_w, wo_w, gn_gamma, gn_beta):
        import jax, jax.numpy as jnp
        import numpy as np
        B, S, DIM, HD = (4, 256, 512, 128)
        H = DIM // HD
        GN_EPS = 0.001

        def _decay_masks(n_heads, seq_len):
            gam = 1.0 - 2.0 ** (-5.0 - jnp.arange(n_heads, dtype=jnp.float32))
            idx = jnp.arange(seq_len, dtype=jnp.float32)
            expo = idx[None, :] - idx[:, None]
            D = jnp.where(expo[None, :, :] <= 0, gam[:, None, None] ** expo[None, :, :], 0.0)
            return D / jnp.sqrt(D.sum(axis=-1))[:, None, :]
        b, s, dim = x.shape
        h, hd, _ = Wh.shape
        xh = x.reshape(b, s, h, hd)
        kh = k.reshape(b, s, h, hd)
        vh = v.reshape(b, s, h, hd)
        Q = jnp.einsum('bshd,hde->bshe', xh, Wh)
        K = jnp.einsum('bshd,hde->bshe', kh, Wh)
        V = jnp.einsum('bshd,hde->bshe', vh, Wh)
        scores = jnp.einsum('bshe,bthe->bhst', Q, K) / jnp.sqrt(jnp.float32(hd))
        Dn = _decay_masks(h, s)
        masked = scores * Dn[None, :, :, :]
        A = jnp.maximum(jnp.abs(masked.sum(axis=0)), 1.0)
        O = jnp.einsum('hst,bthe->bshe', A, V).reshape(b, s, dim)
        mu = O.mean(axis=-1, keepdims=True)
        var = O.var(axis=-1, keepdims=True)
        Y = (O - mu) / jnp.sqrt(var + GN_EPS) * gn_gamma + gn_beta
        W = jax.nn.relu(x @ wg_w)
        return W * Y @ wo_w

    def _L0_ffn_ref(hidden_states, router_w, w_gate, w_up, w_down, sh_gate, sh_up, sh_down, sh_gate_w):
        import jax, jax.numpy as jnp
        import numpy as np
        B, S, H = (2, 512, 512)
        E, K = (16, 4)
        I_MOE, I_SH = (352, 1408)
        orig = hidden_states.shape
        h = hidden_states.reshape(-1, orig[-1])
        N = h.shape[0]
        logits = h @ router_w.T
        probs = jax.nn.softmax(logits.astype(jnp.float32), axis=-1)
        top_vals, top_idx = jax.lax.top_k(probs, K)
        top_vals = top_vals / jnp.maximum(top_vals.sum(-1, keepdims=True), 1e-09)
        top_vals = top_vals.astype(h.dtype)
        comb = jnp.zeros((N, E), h.dtype).at[jnp.arange(N)[:, None], top_idx].add(top_vals)
        g = jnp.einsum('nh,ehi->eni', h, w_gate)
        u = jnp.einsum('nh,ehi->eni', h, w_up)
        y = jnp.einsum('eni,eih->enh', jax.nn.silu(g) * u, w_down)
        routed = jnp.einsum('enh,ne->nh', y, comb)
        shared = jax.nn.silu(h @ sh_gate) * (h @ sh_up) @ sh_down
        sg = jax.nn.sigmoid(h @ sh_gate_w)
        return (routed + sg * shared).reshape(orig)
    x = x + _L0_attn_ref(_layernorm(x, axis=-1), L0_attn_wq, L0_attn_wk, L0_attn_wv, L0_attn_wo, L0_attn_q_scale, L0_attn_k_scale)
    x = x + _L0_xattn_ref(_layernorm(x, axis=-1), ctx_2048, ctx_2048, L0_xattn_Wh, L0_xattn_wg_w, L0_xattn_wo_w, L0_xattn_gn_gamma, L0_xattn_gn_beta)
    x = x + _L0_ffn_ref(_layernorm(x, axis=-1), L0_ffn_router_w, L0_ffn_w_gate, L0_ffn_w_up, L0_ffn_w_down, L0_ffn_sh_gate, L0_ffn_sh_up, L0_ffn_sh_down, L0_ffn_sh_gate_w)
    return x

_drawn_inputs = setup_inputs


def setup_inputs(seed=0):
    import zlib

    import numpy as np

    out = dict(_drawn_inputs(seed))
    spreads = {'L0_attn_q_scale': (1.0, 0.2),
     'L0_attn_k_scale': (1.0, 0.2),
     'L0_xattn_gn_gamma': (1.0, 0.2),
     'L0_xattn_gn_beta': (0.0, 0.1)}
    factors = {}
    for name, (base, spread) in spreads.items():
        noise = np.random.default_rng([zlib.crc32(name.encode()), seed]).standard_normal(out[name].shape)
        drawn = base * np.exp(spread * noise) if base else spread * noise
        out[name] = jnp.asarray(drawn.astype(out[name].dtype))
    for name, factor in factors.items():
        out[name] = (out[name] * factor).astype(out[name].dtype)
    return out
```

```python
from contextlib import ExitStack

import concourse.bass as bass
from concourse import mybir
import numpy as np

F32 = mybir.dt.float32
F32R = mybir.dt.float32r
BF16 = mybir.dt.bfloat16
I32 = mybir.dt.int32
U32 = mybir.dt.uint32
ALU = mybir.AluOpType
ACT = mybir.ActivationFunctionType
AX_X = mybir.AxisListType.X

P = 128
B, S, E = 8, 256, 512
N = B * S
NT = N // P
EC = E // P
H = 16
HG = 4
G = H // HG
ROUNDS = G * B
LN_EPS = 1e-5
RMS_EPS = 1e-6
XP = 16
TOPK = 4
WI = 352
SHARED = 4
TS = 256
ROUTED = N * TOPK // TS + XP
SLOTS = ROUTED * TS
SHARED_STEPS = SHARED * (N // TS)
STEPS = SHARED_STEPS + ROUTED
ZERO_ROWS = 4
CLEARS = SLOTS // (P * ZERO_ROWS)
HI, LO = 0, 1


class Space:

    def __init__(self, nc, prefix):
        self.nc, self.prefix, self.ctx = nc, prefix, ExitStack()

    def __enter__(self):
        return self

    def __exit__(self, *a):
        return self.ctx.__exit__(*a)

    def sb(self, name, shape, dt=F32):
        return self.ctx.enter_context(self.nc.sbuf_tensor(f"{self.prefix}_{name}", shape, dt))

    def bank(self, name, shape=(P, 512), dt=F32):
        return self.ctx.enter_context(self.nc.psum_tensor(f"{self.prefix}_{name}", list(shape), dt))

    def sem(self, name):
        return self.ctx.enter_context(self.nc.semaphore(f"{self.prefix}_{name}"))

    def block(self):
        return self.ctx.enter_context(self.nc.Block())


def matmul3(nc, out, a_hi, a_lo, b_hi, b_lo, start, stop):
    nc.tensor.matmul(out, a_hi, b_lo, start=start, stop=False)
    nc.tensor.matmul(out, a_lo, b_hi, start=False, stop=False)
    return nc.tensor.matmul(out, a_hi, b_hi, start=False, stop=stop)


def make_constants(nc, sp, ident, neg_half):
    with Space(nc, "const") as s:
        cleared = s.sem("cleared")
        done = s.sem("done")
        block = s.block()

        @block.gpsimd
        def _(pool):
            nc.gpsimd.memset(ident[:, :], 0.0).then_inc(cleared, 1)
            pool.wait_ge(cleared, 1)
            nc.gpsimd.affine_select(out=ident[:, :], in_=ident[:, :], compare_op=ALU.not_equal, fill=1.0,
                                    base=0, pattern=[[-1, P]], channel_multiplier=1).then_inc(done, 1)
            nc.gpsimd.memset(neg_half[:, :], -0.5).then_inc(done, 1)
            pool.wait_ge(done, 2)


def token_moments(nc, dve, src, tiles, stats, mean, half, var, eps, step, done):
    with dve.Fori(0, tiles) as t:
        nc.vector.bn_stats(stats[:, bass.ds(t, 1), :].rearrange("p a s -> p (a s)"),
                           src[:, bass.ds(t, 1), :].rearrange("p a e -> p (a e)")).then_inc(step, 1)
    dve.wait_ge(step, tiles)
    nc.vector.tensor_tensor(mean[:, :], stats[:, :, 1], stats[:, :, 4], ALU.add).then_inc(step, 1)
    nc.vector.tensor_tensor(half[:, :], stats[:, :, 1], stats[:, :, 4], ALU.subtract).then_inc(step, 1)
    nc.vector.tensor_tensor(var[:, :], stats[:, :, 2], stats[:, :, 5], ALU.add).then_inc(step, 1)
    dve.wait_ge(step, tiles + 3)
    nc.vector.tensor_scalar(mean[:, :], mean[:, :], 0.5, None, ALU.mult).then_inc(step, 1)
    nc.vector.tensor_scalar(var[:, :], var[:, :], 1.0 / E, eps, ALU.mult, ALU.add).then_inc(step, 1)
    nc.vector.scalar_tensor_tensor(half[:, :], half[:, :], 0.25, half[:, :], ALU.mult, ALU.mult).then_inc(step, 1)
    dve.wait_ge(step, tiles + 6)
    nc.vector.tensor_tensor(var[:, :], var[:, :], half[:, :], ALU.add).then_inc(done, 1)


def layernorm_transpose(nc, prefix, x, xT, ident, neg_half, x_dram=None, xt_dram=None, rows=None, rows_dram=None):
    with Space(nc, prefix) as s:
        stats = s.sb("stats", [P, NT, 6])
        mean = s.sb("mean", [P, NT])
        half = s.sb("half", [P, NT])
        var = s.sb("var", [P, NT])
        rstd = s.sb("rstd", [P, NT])
        xn = s.sb("xn", [P, 2, E])
        flip = [s.bank(f"flip{k}") for k in range(2)]
        loaded = s.sem("loaded")
        step = s.sem("step")
        var_ready = s.sem("var_ready")
        rstd_ready = s.sem("rstd_ready")
        xn_ready = s.sem("xn_ready")
        flipped = s.sem("flipped")
        hi_ready = s.sem("hi_ready")
        lo_ready = s.sem("lo_ready")
        row_kept = s.sem("row_kept")
        stored = s.sem("stored")
        block = s.block()

        @block.sync
        def _(sp):
            if x_dram is not None:
                xv = x_dram.rearrange("b (t p) e -> p (b t) e", p=P)
                for q in range(4):
                    sp.dma_start(x[:, q * 4:q * 4 + 4, :], xv[:, q * 4:q * 4 + 4, :]).then_inc(loaded, 16)
            if xt_dram is not None:
                with sp.Fori(0, B) as b:
                    sp.wait_ge(lo_ready, 2 * b + 2)
                    for part in (HI, LO):
                        sp.dma_start(xt_dram[bass.ds(b, 1), :, part, :, :].rearrange("b p c s -> (b p) c s"),
                                     xT[:, part, :, bass.ds(b * S, S)].bitcast(F32)).then_inc(stored, 16)
                sp.wait_ge(stored, 16 * 2 * B)
            if rows is not None:
                sp.wait_ge(row_kept, NT)
                sp.dma_start(rows_dram[0:N, :].rearrange("(t p) e -> p t e", p=P), rows[:, :, :]).then_inc(stored, 16)
                sp.wait_ge(stored, 16)

        @block.vector
        def _(dve):
            if x_dram is not None:
                dve.wait_ge(loaded, 64)
            token_moments(nc, dve, x, NT, stats, mean, half, var, LN_EPS, step, var_ready)
            dve.wait_ge(rstd_ready, 1)

            def normalise(t, k):
                nc.vector.tensor_scalar(xn[:, k, :], x[:, bass.ds(t, 1), :].rearrange("p a e -> p (a e)"),
                                        mean[:, bass.ds(t, 1)], rstd[:, bass.ds(t, 1)],
                                        ALU.subtract, ALU.mult).then_inc(xn_ready, 1)

            def low(t, k):
                dve.wait_ge(hi_ready, t + 1)
                nc.vector.tensor_tensor(xT[:, LO, :, bass.ds(t * P, P)],
                                        flip[k][:, :].rearrange("p (c n) -> p c n", c=EC),
                                        xT[:, HI, :, bass.ds(t * P, P)], ALU.subtract).then_inc(lo_ready, 1)

            normalise(0, 0)
            normalise(1, 1)
            with dve.Fori(0, NT // 2 - 1) as m:
                for k in range(2):
                    low(2 * m + k, k)
                    if rows is not None:
                        dve.wait_ge(row_kept, 2 * m + (k + 1))
                    normalise(2 * m + (k + 2), k)
            low(NT - 2, 0)
            low(NT - 1, 1)

        @block.gpsimd
        def _(pool):
            pool.wait_ge(var_ready, 1)
            nc.gpsimd.tensor_tensor(rstd[:, :], var[:, :], neg_half[:, 0:NT], ALU.pow).then_inc(rstd_ready, 1)

        @block.tensor
        def _(pe):
            def flips(t, k):
                pe.wait_ge(xn_ready, t + 1)
                if not isinstance(t, int):
                    pe.wait_ge(lo_ready, t - 1)
                for c in range(EC):
                    last = nc.tensor.transpose(flip[k][:, c * P:(c + 1) * P], xn[:, k, c * P:(c + 1) * P],
                                               ident[:, :])
                last.then_inc(flipped, 1)

            flips(0, 0)
            flips(1, 1)
            with pe.Fori(1, NT // 2) as m:
                for k in range(2):
                    flips(2 * m + k, k)

        @block.scalar
        def _(act):
            nc.scalar.preload_act_table(ACT.Exp)
            with act.Fori(0, NT // 2) as m:
                for k in range(2):
                    act.wait_ge(flipped, 2 * m + (k + 1))
                    nc.scalar.activation(xT[:, HI, :, bass.ds(m * (2 * P) + k * P, P)],
                                         flip[k][:, :].rearrange("p (c n) -> p c n", c=EC),
                                         ACT.Copy).then_inc(hi_ready, 1)
                    if rows is not None:
                        nc.scalar.activation(rows[:, bass.ds(2 * m + k, 1), :].rearrange("p a e -> p (a e)"),
                                             xn[:, k, :], ACT.Copy).then_inc(row_kept, 1)


def attention(nc, x, ident, neg_half, xt_dram, wqkv, wo, q_scale, k_scale, slot_rows):
    D = P
    QK = 4
    with Space(nc, "attn") as s:
        xt = s.sb("xt", [P, 2, EC, S], F32R)
        w_raw = s.sb("w_raw", [P, 2, EC * HG * D])
        w = s.sb("w", [P, 4, 2, EC * HG * D], F32R)
        squares = s.sb("squares", [P, 2, HG, D + 1])
        sums = s.sb("sums", [P, QK, HG])
        rms = s.sb("rms", [P, QK, HG])
        qk = s.sb("qk", [P, QK, HG * D])
        v = s.sb("v", [P, 2, 2, HG * D], F32R)
        qT = s.sb("qT", [P, HG, 2, S], F32R)
        kT = s.sb("kT", [P, HG, 2, S], F32R)
        scale_in = s.sb("scale_in", [P, 2])
        scale = s.sb("scale", [P, 1])
        neg_max = s.sb("neg_max", [P, HG, 2])
        row_sum = s.sb("row_sum", [P, HG, 2])
        inv_sum = s.sb("inv_sum", [P, HG, 2])
        probs = s.sb("probs", [P, 2, 2, S])
        pT = s.sb("pT", [P, 2, 2, 2, S], F32R)
        oT = s.sb("oT", [P, HG, 2, S], F32R)
        bank = [s.bank(f"bank{k}") for k in range(8)]
        proj_bank = bank[0:2]
        score_bank = bank[2:4]
        pT_bank = bank[4]
        oT_bank = bank[5]
        flip_bank = [bank[2], bank[3], bank[6], bank[7]]
        out_bank = [bank[4], bank[6]]

        xt_loaded = s.sem("xt_loaded")
        raw_loaded = [s.sem(f"raw_loaded{k}") for k in range(2)]
        w_hi = s.sem("w_hi")
        w_ready = s.sem("w_ready")
        scales_loaded = s.sem("scales_loaded")
        scale_ready = s.sem("scale_ready")
        ones_ready = s.sem("ones_ready")
        projected = s.sem("projected")
        squared = s.sem("squared")
        summed = s.sem("summed")
        rms_ready = s.sem("rms_ready")
        qk_ready = s.sem("qk_ready")
        v_hi = s.sem("v_hi")
        v_ready = s.sem("v_ready")
        flipped = s.sem("flipped")
        qkT_hi = s.sem("qkT_hi")
        qkT_ready = s.sem("qkT_ready")
        scored = s.sem("scored")
        max_ready = s.sem("max_ready")
        exp_ready = s.sem("exp_ready")
        inv_ready = s.sem("inv_ready")
        probs_ready = s.sem("probs_ready")
        p_flipped = s.sem("p_flipped")
        pT_hi = s.sem("pT_hi")
        pT_ready = s.sem("pT_ready")
        o_done = s.sem("o_done")
        oT_hi = s.sem("oT_hi")
        oT_ready = s.sem("oT_ready")
        out_done = s.sem("out_done")
        added = s.sem("added")
        zeros = s.sb("zeros", [P, ZERO_ROWS * E])
        zeros_ready = s.sem("zeros_ready")
        slots_cleared = s.sem("slots_cleared")
        block = s.block()

        def rounds(eng, first, body, refill_qkv, refill_out):
            first()
            with eng.Fori(0, G - 1) as g:
                with eng.Fori(0, B - 1) as b:
                    body(g * B + b, b, True)
                refill_qkv(g + 1)
                body(g * B + (B - 1), B - 1, True)
                refill_out(g + 1)
            with eng.Fori(0, B - 1) as b:
                body(b + (G - 1) * B, b, True)
            body(G * B - 1, B - 1, False)

        def nothing(*a):
            pass

        @block.sync
        def _(sp):
            def load_raw(g, c):
                if not isinstance(g, int):
                    sp.wait_ge(w_ready, 4 * g + (c - 1))
                elif c >= 2:
                    sp.wait_ge(w_ready, c - 1)
                if c < 3:
                    src = wqkv[bass.ds(g, 1), c, :, :].rearrange("g p n -> (g p) n")
                    sp.dma_start(w_raw[:, c % 2, :], src).then_inc(raw_loaded[c % 2], 16)
                else:
                    src = wo[bass.ds(g, 1), :, :, :].rearrange("g h d e -> d (g h) e")
                    sp.dma_start(w_raw[:, c % 2, :].rearrange("p (h e) -> p h e", h=HG),
                                 src).then_inc(raw_loaded[c % 2], 16)

            def load_xt(j, b):
                if not isinstance(j, int) or j > 0:
                    sp.wait_ge(projected, 6 * j)
                sp.dma_start(xt[:, :, :, :].bitcast(F32), xt_dram[bass.ds(b, 1), :, :, :, :].rearrange(
                    "b p l c s -> (b p) l c s")).then_inc(xt_loaded, 16)

            load_raw(0, 0)
            load_raw(0, 1)
            sp.dma_start(scale_in[:, 0:1], q_scale.rearrange("(p a) -> p a", a=1)).then_inc(scales_loaded, 16)
            sp.dma_start(scale_in[:, 1:2], k_scale.rearrange("(p a) -> p a", a=1)).then_inc(scales_loaded, 16)
            load_xt(0, 0)
            load_raw(0, 2)
            load_raw(0, 3)
            sp.wait_ge(zeros_ready, 1)
            for n in range(CLEARS):
                sp.dma_start(slot_rows[n * P * ZERO_ROWS:(n + 1) * P * ZERO_ROWS, :].rearrange(
                    "(p r) e -> p (r e)", p=P), zeros[:, :]).then_inc(slots_cleared, 16)
            with sp.Fori(0, G - 1) as g:
                load_raw(g + 1, 0)
                load_raw(g + 1, 1)
                with sp.Fori(0, B - 1) as b:
                    load_xt(g * B + b + 1, b + 1)
                load_xt(g * B + B, 0)
                load_raw(g + 1, 2)
                load_raw(g + 1, 3)
            with sp.Fori(0, B - 1) as b:
                load_xt(b + ((G - 1) * B + 1), b + 1)
            sp.wait_ge(slots_cleared, 16 * CLEARS)

        @block.tensor
        def _(pe):
            def project(j, n, g=None):
                c, tile = ((n % 2, n // 2) if n < QK else (2, n - QK))
                if n == 0:
                    pe.wait_ge(xt_loaded, 16 * (j + 1))
                if g is not None and n in (0, 1, 4):
                    pe.wait_ge(w_ready, 4 * g + (c + 1))
                if n >= 2:
                    pe.wait_ge(qk_ready, QK * j + (n - 1))
                elif not isinstance(j, int) or j > 0:
                    pe.wait_ge(v_ready, 2 * j + (n - 1))
                for e in range(EC):
                    cols = slice(e * HG * D, (e + 1) * HG * D)
                    toks = slice(tile * P, tile * P + P)
                    last = matmul3(nc, proj_bank[n % 2][:, :], xt[:, HI, e, toks], xt[:, LO, e, toks],
                                   w[:, c, HI, cols], w[:, c, LO, cols], e == 0, e == EC - 1)
                last.then_inc(projected, 1)

            def flip(j):
                pe.wait_ge(qk_ready, QK * j + QK)
                if not isinstance(j, int) or j > 0:
                    pe.wait_ge(exp_ready, HG * j)
                    pe.wait_ge(added, 2 * j - 2)
                for u in range(HG):
                    for c in range(2):
                        for tile in range(2):
                            last = nc.tensor.transpose(flip_bank[u][:, (2 * c + tile) * P:(2 * c + tile + 1) * P],
                                                       qk[:, 2 * tile + c, u * D:(u + 1) * D], ident[:, :])
                    last.then_inc(flipped, 1)

            def score(i, u):
                pe.wait_ge(qkT_ready, HG * i + (u + 1))
                if u >= 2:
                    pe.wait_ge(exp_ready, HG * i + (u - 1))
                for tile in range(2):
                    toks = slice(tile * P, tile * P + P)
                    last = matmul3(nc, score_bank[u % 2][:, tile * S:(tile + 1) * S], qT[:, u, HI, toks],
                                   qT[:, u, LO, toks], kT[:, u, HI, :], kT[:, u, LO, :], True, True)
                last.then_inc(scored, 1)

            def flip_probs(i, u):
                pe.wait_ge(probs_ready, HG * i + (u + 1))
                if u == 0:
                    pe.wait_ge(added, 2 * i)
                else:
                    pe.wait_ge(pT_ready, HG * i + u)
                for kt in range(2):
                    for tile in range(2):
                        last = nc.tensor.transpose(pT_bank[:, kt * S + tile * P:kt * S + (tile + 1) * P],
                                                   probs[:, u % 2, tile, kt * P:(kt + 1) * P], ident[:, :])
                last.then_inc(p_flipped, 1)

            def weigh(i, u):
                pe.wait_ge(pT_ready, HG * i + (u + 1))
                if u == 0:
                    pe.wait_ge(v_ready, 2 * i + 2)
                else:
                    pe.wait_ge(oT_ready, HG * i + u)
                for kt in range(2):
                    last = matmul3(nc, oT_bank[:, 0:S], v[:, kt, HI, u * D:(u + 1) * D],
                                   v[:, kt, LO, u * D:(u + 1) * D], pT[:, u % 2, HI, kt, :],
                                   pT[:, u % 2, LO, kt, :], kt == 0, kt == 1)
                last.then_inc(o_done, 1)

            def output(i, more):
                pe.wait_ge(oT_ready, HG * i + HG)
                for tile in range(2):
                    if tile == 1 and more:
                        pe.wait_ge(qkT_ready, HG * i + (HG + 3))
                    for u in range(HG):
                        toks = slice(tile * P, tile * P + P)
                        cols = slice(u * E, (u + 1) * E)
                        last = matmul3(nc, out_bank[tile][:, :], oT[:, u, HI, toks], oT[:, u, LO, toks],
                                       w[:, 3, HI, cols], w[:, 3, LO, cols], u == 0, u == HG - 1)
                    last.then_inc(out_done, 1)

            def body(i, b, more, g=None):
                j = i + 1
                score(i, 0)
                if more:
                    project(j, 0, g)
                score(i, 1)
                if more:
                    project(j, 1, g)
                flip_probs(i, 0)
                score(i, 2)
                if more:
                    project(j, 2, g)
                weigh(i, 0)
                flip_probs(i, 1)
                score(i, 3)
                if more:
                    project(j, 3, g)
                weigh(i, 1)
                flip_probs(i, 2)
                if more:
                    project(j, 4, g)
                weigh(i, 2)
                flip_probs(i, 3)
                if more:
                    project(j, 5, g)
                weigh(i, 3)
                if more:
                    flip(j)
                output(i, more)

            for n in range(6):
                project(0, n, 0)
            flip(0)
            pe.wait_ge(w_ready, 4)
            with pe.Fori(0, G - 1) as g:
                with pe.Fori(0, B - 1) as b:
                    body(g * B + b, b, True)
                body(g * B + (B - 1), B - 1, True, g + 1)
                pe.wait_ge(w_ready, 4 * g + 8)
            with pe.Fori(0, B - 1) as b:
                body(b + (G - 1) * B, b, True)
            body(G * B - 1, B - 1, False)

        @block.scalar
        def _(act):
            def split_hi(g, c):
                act.wait_ge(raw_loaded[c % 2], 32 * g + 16 * (c // 2 + 1))
                if not isinstance(g, int):
                    if c < 3:
                        act.wait_ge(projected, 6 * B * g)
                    else:
                        act.wait_ge(out_done, 2 * B * g)
                nc.scalar.activation(w[:, c, HI, :], w_raw[:, c % 2, :], ACT.Copy).then_inc(w_hi, 1)

            def square(j, n):
                act.wait_ge(projected, 6 * j + (n + 1))
                if not (isinstance(j, int) and n < 2):
                    act.wait_ge(summed, QK * j + (n - 1))
                nc.scalar.activation(squares[:, n % 2, :, 0:D],
                                     proj_bank[n % 2][:, :].rearrange("p (h d) -> p h d", h=HG),
                                     ACT.Square).then_inc(squared, 1)

            def v_high(j, tile):
                act.wait_ge(projected, 6 * j + (QK + tile + 1))
                if not isinstance(j, int):
                    act.wait_ge(o_done, HG * j)
                nc.scalar.activation(v[:, tile, HI, :], proj_bank[tile][:, :], ACT.Copy).then_inc(v_hi, 1)

            def qkT_high(j, u):
                act.wait_ge(flipped, HG * j + (u + 1))
                nc.scalar.activation(qT[:, u, HI, :], flip_bank[u][:, 0:S], ACT.Copy, scale=scale[:, 0:1])
                nc.scalar.activation(kT[:, u, HI, :], flip_bank[u][:, S:2 * S], ACT.Copy).then_inc(qkT_hi, 1)

            def exponentials(i, u):
                act.wait_ge(max_ready, HG * i + (u + 1))
                if u >= 2:
                    act.wait_ge(p_flipped, HG * i + (u - 1))
                for tile in range(2):
                    last = nc.scalar.activation(probs[:, u % 2, tile, :], score_bank[u % 2][:, tile * S:(tile + 1) * S],
                                                ACT.Exp, bias=neg_max[:, u, tile:tile + 1],
                                                accum_out=row_sum[:, u, tile:tile + 1])
                last.then_inc(exp_ready, 1)

            def pT_high(i, u):
                act.wait_ge(p_flipped, HG * i + (u + 1))
                nc.scalar.activation(pT[:, u % 2, HI, :, :].rearrange("p k s -> p (k s)"), pT_bank[:, :],
                                     ACT.Copy).then_inc(pT_hi, 1)

            def oT_high(i, u):
                act.wait_ge(o_done, HG * i + (u + 1))
                nc.scalar.activation(oT[:, u, HI, :], oT_bank[:, 0:S], ACT.Copy).then_inc(oT_hi, 1)

            def body(i, b, more):
                j = i + 1
                exponentials(i, 0)
                if more:
                    square(j, 0)
                exponentials(i, 1)
                if more:
                    square(j, 1)
                pT_high(i, 0)
                exponentials(i, 2)
                if more:
                    square(j, 2)
                oT_high(i, 0)
                pT_high(i, 1)
                exponentials(i, 3)
                if more:
                    square(j, 3)
                oT_high(i, 1)
                pT_high(i, 2)
                oT_high(i, 2)
                pT_high(i, 3)
                oT_high(i, 3)
                if more:
                    for u in range(HG):
                        qkT_high(j, u)
                    v_high(j, 0)
                    v_high(j, 1)

            def first():
                split_hi(0, 0)
                split_hi(0, 1)
                split_hi(0, 2)
                act.wait_ge(ones_ready, 1)
                act.wait_ge(scale_ready, 1)
                for n in range(QK):
                    square(0, n)
                v_high(0, 0)
                v_high(0, 1)
                for u in range(HG):
                    qkT_high(0, u)
                split_hi(0, 3)

            rounds(act, first, body, lambda g: [split_hi(g, c) for c in range(3)], lambda g: split_hi(g, 3))

        @block.vector
        def _(dve):
            def split_lo(g, c):
                dve.wait_ge(w_hi, 4 * g + (c + 1))
                nc.vector.tensor_tensor(w[:, c, LO, :], w_raw[:, c % 2, :], w[:, c, HI, :],
                                        ALU.subtract).then_inc(w_ready, 1)

            def sum_squares(j, n):
                dve.wait_ge(squared, QK * j + (n + 1))
                nc.vector.reduce_sum(sums[:, n, :], squares[:, n % 2, :, :], AX_X).then_inc(summed, 1)

            def scale_rows(j, n):
                dve.wait_ge(rms_ready, QK * j + (n + 1))
                nc.vector.tensor_tensor(qk[:, n, :].rearrange("p (h d) -> p h d", h=HG),
                                        proj_bank[n % 2][:, :].rearrange("p (h d) -> p h d", h=HG),
                                        rms[:, n, :].unsqueeze(2).to_broadcast([P, HG, D]),
                                        ALU.mult).then_inc(qk_ready, 1)

            def v_low(j, tile):
                dve.wait_ge(v_hi, 2 * j + (tile + 1))
                nc.vector.tensor_tensor(v[:, tile, LO, :], proj_bank[tile][:, :], v[:, tile, HI, :],
                                        ALU.subtract).then_inc(v_ready, 1)

            def qkT_low(j, u):
                dve.wait_ge(qkT_hi, HG * j + (u + 1))
                nc.vector.scalar_tensor_tensor(qT[:, u, LO, :], flip_bank[u][:, 0:S], scale[:, 0:1],
                                               qT[:, u, HI, :], ALU.mult, ALU.subtract)
                nc.vector.tensor_tensor(kT[:, u, LO, :], flip_bank[u][:, S:2 * S], kT[:, u, HI, :],
                                        ALU.subtract).then_inc(qkT_ready, 1)

            def maxima(i, u):
                dve.wait_ge(scored, HG * i + (u + 1))
                nc.vector.tensor_reduce(neg_max[:, u, :], score_bank[u % 2][:, :].rearrange("p (t k) -> p t k", t=2),
                                        AX_X, ALU.max, negate=True).then_inc(max_ready, 1)

            def invert_sums(i, u):
                dve.wait_ge(exp_ready, HG * i + (u + 1))
                nc.vector.reciprocal(inv_sum[:, u, :], row_sum[:, u, :]).then_inc(inv_ready, 1)

            def pT_low(i, u):
                dve.wait_ge(pT_hi, HG * i + (u + 1))
                nc.vector.tensor_tensor(pT[:, u % 2, LO, :, :].rearrange("p k s -> p (k s)"), pT_bank[:, :],
                                        pT[:, u % 2, HI, :, :].rearrange("p k s -> p (k s)"),
                                        ALU.subtract).then_inc(pT_ready, 1)

            def oT_low(i, u):
                dve.wait_ge(oT_hi, HG * i + (u + 1))
                nc.vector.tensor_tensor(oT[:, u, LO, :], oT_bank[:, 0:S], oT[:, u, HI, :],
                                        ALU.subtract).then_inc(oT_ready, 1)

            def add_output(i, b, tile):
                dve.wait_ge(out_done, 2 * i + (tile + 1))
                rows = x[:, bass.ds(b * 2 + tile, 1), :].rearrange("p a e -> p (a e)")
                nc.vector.tensor_tensor(rows, out_bank[tile][:, :], rows, ALU.add).then_inc(added, 1)

            def body(i, b, more):
                j = i + 1
                maxima(i, 0)
                if more:
                    sum_squares(j, 0)
                invert_sums(i, 0)
                maxima(i, 1)
                if more:
                    scale_rows(j, 0)
                    sum_squares(j, 1)
                invert_sums(i, 1)
                pT_low(i, 0)
                maxima(i, 2)
                if more:
                    scale_rows(j, 1)
                    sum_squares(j, 2)
                invert_sums(i, 2)
                oT_low(i, 0)
                pT_low(i, 1)
                maxima(i, 3)
                if more:
                    scale_rows(j, 2)
                    sum_squares(j, 3)
                invert_sums(i, 3)
                oT_low(i, 1)
                pT_low(i, 2)
                if more:
                    scale_rows(j, 3)
                oT_low(i, 2)
                pT_low(i, 3)
                oT_low(i, 3)
                if more:
                    for u in range(HG):
                        qkT_low(j, u)
                    v_low(j, 0)
                    v_low(j, 1)
                add_output(i, b, 0)
                add_output(i, b, 1)

            def first():
                nc.vector.memset(squares[:, :, :, D:D + 1], RMS_EPS * D).then_inc(ones_ready, 1)
                dve.wait_ge(scales_loaded, 32)
                nc.vector.tensor_scalar(scale[:, :], scale_in[:, 0:1], scale_in[:, 1:2], float(D), ALU.mult,
                                        ALU.mult).then_inc(scale_ready, 1)
                for c in range(3):
                    split_lo(0, c)
                dve.wait_ge(ones_ready, 1)
                for n in range(QK):
                    sum_squares(0, n)
                    scale_rows(0, n)
                v_low(0, 0)
                v_low(0, 1)
                for u in range(HG):
                    qkT_low(0, u)
                split_lo(0, 3)

            rounds(dve, first, body, lambda g: [split_lo(g, c) for c in range(3)], lambda g: split_lo(g, 3))

        @block.gpsimd
        def _(pool):
            def inverse_rms(j, n):
                pool.wait_ge(summed, QK * j + (n + 1))
                nc.gpsimd.tensor_tensor(rms[:, n, :], sums[:, n, :], neg_half[:, 0:HG], ALU.pow).then_inc(rms_ready, 1)

            def normalise(i, u):
                pool.wait_ge(inv_ready, HG * i + (u + 1))
                nc.gpsimd.tensor_tensor(probs[:, u % 2, :, :], probs[:, u % 2, :, :],
                                        inv_sum[:, u, :].unsqueeze(2).to_broadcast([P, 2, S]),
                                        ALU.mult).then_inc(probs_ready, 1)

            def body(i, b, more):
                for u in range(HG):
                    if more:
                        inverse_rms(i + 1, u)
                    normalise(i, u)

            def first():
                nc.gpsimd.memset(zeros[:, :], 0.0).then_inc(zeros_ready, 1)
                for n in range(QK):
                    inverse_rms(0, n)

            rounds(pool, first, body, nothing, nothing)


def retention(nc, x, xT, ident, neg_half, ctxT, head_w, decayT, gate_w, out_w, gamma, beta):
    RH = E // P
    NB = N // 512
    GN_EPS = 1e-3
    with Space(nc, "ret") as keep:
        o = keep.sb("o", [P, NT, E])
        with Space(nc, "heads") as s:
            ctx_raw = s.sb("ctx_raw", [P, 2, 512])
            ctx = s.sb("ctx", [P, 2, 2, 512], F32R)
            hw_raw = s.sb("hw_raw", [P, P])
            hw = s.sb("hw", [P, 2, P], F32R)
            decay = s.sb("decay", [P, 2, S])
            k_full = s.sb("k_full", [P, 2, 512])
            kT = s.sb("kT", [P, 2, N], F32R)
            qT = s.sb("qT", [P, 2, N], F32R)
            v = s.sb("v", [P, 2, 2, B, P], F32R)
            masked = s.sb("masked", [P, 2, S])
            a32 = s.sb("a32", [P, 2, S])
            a = s.sb("a", [P, 2, 2, S], F32R)
            bank = [s.bank(f"bank{k}") for k in range(8)]
            k_bank = bank[0:2]
            v_bank = bank[2:4]
            q_bank = [bank[4], bank[5], bank[4], bank[5]]
            score_bank = bank[6:8]
            o_bank = [bank[0], bank[1], bank[2], bank[3]]
            ctx_loaded = [s.sem(f"ctx_loaded{k}") for k in range(2)]
            head_loaded = s.sem("head_loaded")
            ctx_hi = s.sem("ctx_hi")
            ctx_ready = s.sem("ctx_ready")
            hw_hi = s.sem("hw_hi")
            hw_ready = s.sem("hw_ready")
            k_done = s.sem("k_done")
            k_full_ready = s.sem("k_full_ready")
            k_hi = s.sem("k_hi")
            k_ready = s.sem("k_ready")
            q_done = s.sem("q_done")
            q_hi = s.sem("q_hi")
            q_ready = s.sem("q_ready")
            v_flipped = s.sem("v_flipped")
            v_hi = s.sem("v_hi")
            v_ready = s.sem("v_ready")
            scored = s.sem("scored")
            decayed = s.sem("decayed")
            negated = s.sem("negated")
            a_full = s.sem("a_full")
            a_hi = s.sem("a_hi")
            a_ready = s.sem("a_ready")
            o_done = s.sem("o_done")
            o_read = s.sem("o_read")
            block = s.block()

            @block.sync
            def _(sp):
                with sp.Fori(0, RH) as h:
                    sp.wait_ge(decayed, 2 * h)
                    sp.dma_start(hw_raw[:, :], head_w[bass.ds(h, 1), :, :].rearrange("h d e -> (h d) e")).then_inc(
                        head_loaded, 16)
                    sp.dma_start(decay[:, :, :], decayT[bass.ds(h, 1), :, :, :].rearrange(
                        "h p t s -> (h p) t s")).then_inc(head_loaded, 16)
                    for n in range(NB):
                        if n >= 2:
                            sp.wait_ge(ctx_ready, NB * h + (n - 1))
                        sp.dma_start(ctx_raw[:, n % 2, :], ctxT[bass.ds(h, 1), :, n * 512:(n + 1) * 512].rearrange(
                            "h d n -> (h d) n")).then_inc(ctx_loaded[n % 2], 16)

            @block.tensor
            def _(pe):
                with pe.Fori(0, RH) as h:
                    def keys(n):
                        if n == 0:
                            pe.wait_ge(hw_ready, h + 1)
                            pe.wait_ge(o_read, 4 * h)
                        if n >= 2:
                            pe.wait_ge(k_ready, NB * h + (n - 1))
                        pe.wait_ge(ctx_ready, NB * h + (n + 1))
                        matmul3(nc, k_bank[n % 2][:, :], hw[:, HI, :], hw[:, LO, :], ctx[:, n % 2, HI, :],
                                ctx[:, n % 2, LO, :], True, True).then_inc(k_done, 1)

                    def values(n):
                        pe.wait_ge(k_full_ready, NB * h + (n + 1))
                        if n >= 2:
                            pe.wait_ge(v_ready, NB * h + (n - 1))
                        for q in range(4):
                            last = nc.tensor.transpose(v_bank[n % 2][:, q * P:(q + 1) * P],
                                                       k_full[:, n % 2, q * P:(q + 1) * P], ident[:, :])
                        last.then_inc(v_flipped, 1)

                    def queries(n):
                        if n >= 2:
                            pe.wait_ge(q_ready, NB * h + (n - 1))
                        cols = slice(n * 512, (n + 1) * 512)
                        matmul3(nc, q_bank[n][:, :], hw[:, HI, :], hw[:, LO, :],
                                xT[:, HI, bass.ds(h, 1), cols].rearrange("p a n -> p (a n)"),
                                xT[:, LO, bass.ds(h, 1), cols].rearrange("p a n -> p (a n)"),
                                True, True).then_inc(q_done, 1)

                    keys(0)
                    keys(1)
                    queries(0)
                    values(0)
                    keys(2)
                    queries(1)
                    values(1)
                    keys(3)
                    queries(2)
                    values(2)
                    queries(3)
                    values(3)
                    pe.wait_ge(k_ready, NB * h + NB)
                    pe.wait_ge(q_ready, NB * h + NB)
                    for kt in range(2):
                        for b in range(B):
                            keys_of = slice(b * S + kt * P, b * S + (kt + 1) * P)
                            queries_of = slice(b * S, (b + 1) * S)
                            last = matmul3(nc, score_bank[kt][:, 0:S], kT[:, HI, keys_of], kT[:, LO, keys_of],
                                           qT[:, HI, queries_of], qT[:, LO, queries_of], b == 0, b == B - 1)
                        last.then_inc(scored, 1)
                    pe.wait_ge(a_ready, 2 * h + 2)
                    pe.wait_ge(v_ready, NB * h + NB)
                    for st in range(2):
                        for half in range(2):
                            for kt in range(2):
                                batches = slice(4 * half, 4 * half + 4)
                                last = matmul3(nc, o_bank[2 * st + half][:, :], a[:, HI, kt, st * P:(st + 1) * P],
                                               a[:, LO, kt, st * P:(st + 1) * P], v[:, HI, kt, batches, :],
                                               v[:, LO, kt, batches, :], kt == 0, kt == 1)
                            last.then_inc(o_done, 1)

            def v_view(part, n):
                return v[:, part, :, 2 * n:2 * n + 2, :]

            def v_psum(n):
                return v_bank[n % 2][:, :].rearrange("p (b t e) -> p t b e", b=2, t=2)

            @block.scalar
            def _(act):
                nc.scalar.preload_act_table(ACT.Exp)
                with act.Fori(0, RH) as h:
                    def keys(n):
                        act.wait_ge(k_done, NB * h + (n + 1))
                        if n >= 2:
                            act.wait_ge(v_flipped, NB * h + (n - 1))
                        nc.scalar.activation(k_full[:, n % 2, :], k_bank[n % 2][:, :], ACT.Copy).then_inc(
                            k_full_ready, 1)
                        nc.scalar.activation(kT[:, HI, n * 512:(n + 1) * 512], k_bank[n % 2][:, :],
                                             ACT.Copy).then_inc(k_hi, 1)

                    def queries(n):
                        act.wait_ge(q_done, NB * h + (n + 1))
                        nc.scalar.activation(qT[:, HI, n * 512:(n + 1) * 512], q_bank[n][:, :],
                                             ACT.Copy).then_inc(q_hi, 1)

                    def values(n):
                        act.wait_ge(v_flipped, NB * h + (n + 1))
                        nc.scalar.activation(v_view(HI, n), v_psum(n), ACT.Copy).then_inc(v_hi, 1)

                    keys(0)
                    keys(1)
                    queries(0)
                    values(0)
                    keys(2)
                    queries(1)
                    values(1)
                    keys(3)
                    queries(2)
                    values(2)
                    queries(3)
                    values(3)
                    for kt in range(2):
                        act.wait_ge(a_full, 2 * h + (kt + 1))
                        nc.scalar.activation(a[:, HI, kt, :], a32[:, kt, :], ACT.Copy).then_inc(a_hi, 1)
                    for st in range(2):
                        for half in range(2):
                            act.wait_ge(o_done, 4 * h + (2 * st + half + 1))
                            tiles = o[:, 8 * half:8 * half + 8, bass.ds(h * P, P)].rearrange(
                                "p (b s) e -> p b s e", s=2)[:, :, st, :]
                            nc.scalar.activation(tiles, o_bank[2 * st + half][:, :].rearrange(
                                "p (b e) -> p b e", b=4), ACT.Copy).then_inc(o_read, 1)

            @block.vector
            def _(dve):
                with dve.Fori(0, RH) as h:
                    def context(n):
                        dve.wait_ge(ctx_loaded[n % 2], 8 * NB * h + 16 * (n // 2 + 1))
                        if n >= 2:
                            dve.wait_ge(k_done, NB * h + (n - 1))
                        nc.vector.tensor_copy(ctx[:, n % 2, HI, :], ctx_raw[:, n % 2, :]).then_inc(ctx_hi, 1)
                        dve.wait_ge(ctx_hi, NB * h + (n + 1))
                        nc.vector.tensor_tensor(ctx[:, n % 2, LO, :], ctx_raw[:, n % 2, :], ctx[:, n % 2, HI, :],
                                                ALU.subtract).then_inc(ctx_ready, 1)

                    def keys(n):
                        dve.wait_ge(k_hi, NB * h + (n + 1))
                        nc.vector.tensor_tensor(kT[:, LO, n * 512:(n + 1) * 512], k_bank[n % 2][:, :],
                                                kT[:, HI, n * 512:(n + 1) * 512], ALU.subtract).then_inc(k_ready, 1)

                    def queries(n):
                        dve.wait_ge(q_hi, NB * h + (n + 1))
                        nc.vector.tensor_tensor(qT[:, LO, n * 512:(n + 1) * 512], q_bank[n][:, :],
                                                qT[:, HI, n * 512:(n + 1) * 512], ALU.subtract).then_inc(q_ready, 1)

                    def values(n):
                        dve.wait_ge(v_hi, NB * h + (n + 1))
                        nc.vector.tensor_tensor(v_view(LO, n), v_psum(n), v_view(HI, n),
                                                ALU.subtract).then_inc(v_ready, 1)

                    dve.wait_ge(head_loaded, 32 * h + 32)
                    dve.wait_ge(q_done, NB * h)
                    nc.vector.tensor_copy(hw[:, HI, :], hw_raw[:, :]).then_inc(hw_hi, 1)
                    dve.wait_ge(hw_hi, h + 1)
                    nc.vector.tensor_tensor(hw[:, LO, :], hw_raw[:, :], hw[:, HI, :], ALU.subtract).then_inc(hw_ready, 1)
                    context(0)
                    context(1)
                    keys(0)
                    context(2)
                    keys(1)
                    queries(0)
                    context(3)
                    values(0)
                    keys(2)
                    queries(1)
                    values(1)
                    keys(3)
                    queries(2)
                    values(2)
                    queries(3)
                    values(3)
                    for kt in range(2):
                        dve.wait_ge(scored, 2 * h + (kt + 1))
                        nc.vector.tensor_tensor(masked[:, kt, :], score_bank[kt][:, 0:S], decay[:, kt, :],
                                                ALU.mult).then_inc(decayed, 1)
                        dve.wait_ge(decayed, 2 * h + (kt + 1))
                        nc.vector.tensor_scalar(a32[:, kt, :], masked[:, kt, :], -1.0, 1.0, ALU.mult,
                                                ALU.max).then_inc(negated, 1)
                        dve.wait_ge(negated, 2 * h + (kt + 1))
                        nc.vector.tensor_tensor(a32[:, kt, :], masked[:, kt, :], a32[:, kt, :],
                                                ALU.max).then_inc(a_full, 1)
                    for kt in range(2):
                        dve.wait_ge(a_hi, 2 * h + (kt + 1))
                        nc.vector.tensor_tensor(a[:, LO, kt, :], a32[:, kt, :], a[:, HI, kt, :],
                                                ALU.subtract).then_inc(a_ready, 1)

        with Space(nc, "mix") as s:
            w_raw = s.sb("w_raw", [P, EC, E])
            gw = s.sb("gw", [P, 2, EC, E], F32R)
            ow = s.sb("ow", [P, 2, EC, E], F32R)
            gamma_b = s.sb("gamma_b", [P, E])
            beta_b = s.sb("beta_b", [P, E])
            stats = s.sb("stats", [P, NT, 6])
            mean = s.sb("mean", [P, NT])
            half = s.sb("half", [P, NT])
            var = s.sb("var", [P, NT])
            rstd = s.sb("rstd", [P, NT])
            xs = s.sb("xs", [P, 2, 2, EC, P], F32R)
            y = s.sb("y", [P, 2, E])
            wy = s.sb("wy", [P, 2, E])
            wyT = s.sb("wyT", [P, 2, 2, EC, P], F32R)
            gate_bank = [s.bank(f"gate{k}") for k in range(2)]
            flip_bank = [s.bank(f"flip{k}") for k in range(2)]
            out_bank = [s.bank(f"out{k}") for k in range(2)]
            w_loaded = s.sem("w_loaded")
            affine_loaded = s.sem("affine_loaded")
            w_hi = s.sem("w_hi")
            w_ready = s.sem("w_ready")
            step = s.sem("step")
            var_ready = s.sem("var_ready")
            rstd_ready = s.sem("rstd_ready")
            xs_loaded = [s.sem(f"xs_loaded{k}") for k in range(2)]
            y_normal = s.sem("y_normal")
            y_scaled = s.sem("y_scaled")
            y_ready = s.sem("y_ready")
            gated = s.sem("gated")
            wy_ready = s.sem("wy_ready")
            flipped = s.sem("flipped")
            wyT_hi = s.sem("wyT_hi")
            wyT_ready = s.sem("wyT_ready")
            out_done = s.sem("out_done")
            added = s.sem("added")
            block = s.block()

            @block.sync
            def _(sp):
                sp.dma_start(w_raw[:, :, :], gate_w.rearrange("(c p) n -> p c n", p=P)).then_inc(w_loaded, 16)
                sp.dma_start(gamma_b[:, :], gamma.rearrange("(a e) -> a e", a=1).to_broadcast([P, E])).then_inc(
                    affine_loaded, 16)
                sp.dma_start(beta_b[:, :], beta.rearrange("(a e) -> a e", a=1).to_broadcast([P, E])).then_inc(
                    affine_loaded, 16)

                def tile_in(t, k):
                    first = t * P
                    if not isinstance(t, int):
                        first = sp.snap(first)
                        sp.wait_ge(gated, t - 1)
                    sp.dma_start(xs[:, k, :, :, :].bitcast(F32), xT[:, :, :, bass.ds(first, P)].bitcast(F32)).then_inc(
                        xs_loaded[k], 16)

                tile_in(0, 0)
                tile_in(1, 1)
                sp.wait_ge(w_ready, 1)
                sp.dma_start(w_raw[:, :, :], out_w.rearrange("(c p) n -> p c n", p=P)).then_inc(w_loaded, 16)
                with sp.Fori(1, NT // 2) as m:
                    for k in range(2):
                        tile_in(2 * m + k, k)

            @block.tensor
            def _(pe):
                def gate(m, k):
                    t = 2 * m + k
                    pe.wait_ge(xs_loaded[k], 16 * m + 16)
                    if not isinstance(t, int):
                        pe.wait_ge(wy_ready, t - 1)
                    for c in range(EC):
                        last = matmul3(nc, gate_bank[k][:, :], xs[:, k, HI, c, :], xs[:, k, LO, c, :],
                                       gw[:, HI, c, :], gw[:, LO, c, :], c == 0, c == EC - 1)
                    last.then_inc(gated, 1)

                def flip(t, k):
                    pe.wait_ge(wy_ready, t + 1)
                    if not isinstance(t, int) or t > 1:
                        pe.wait_ge(wyT_ready, t - 1)
                    for c in range(EC):
                        last = nc.tensor.transpose(flip_bank[k][:, c * P:(c + 1) * P], wy[:, k, c * P:(c + 1) * P],
                                                   ident[:, :])
                    last.then_inc(flipped, 1)

                def out(t, k):
                    pe.wait_ge(wyT_ready, t + 1)
                    if not isinstance(t, int) or t > 1:
                        pe.wait_ge(added, t - k)
                    for c in range(EC):
                        last = matmul3(nc, out_bank[k][:, :], wyT[:, k, HI, c, :], wyT[:, k, LO, c, :],
                                       ow[:, HI, c, :], ow[:, LO, c, :], c == 0, c == EC - 1)
                    last.then_inc(out_done, 1)

                pe.wait_ge(w_ready, 1)
                gate(0, 0)
                gate(0, 1)
                flip(0, 0)
                pe.wait_ge(w_ready, 2)
                with pe.Fori(1, NT // 2) as m:
                    gate(m, 0)
                    flip(2 * m - 1, 1)
                    out(2 * m - 2, 0)
                    gate(m, 1)
                    flip(2 * m, 0)
                    out(2 * m - 1, 1)
                flip(NT - 1, 1)
                out(NT - 2, 0)
                out(NT - 1, 1)

            @block.scalar
            def _(act):
                nc.scalar.preload_act_table(ACT.Exp)
                for n, w in enumerate((gw, ow)):
                    act.wait_ge(w_loaded, 16 * (n + 1))
                    nc.scalar.activation(w[:, HI, :, :], w_raw[:, :, :], ACT.Copy).then_inc(w_hi, 1)
                with act.Fori(0, NT // 2) as m:
                    for k in range(2):
                        act.wait_ge(flipped, 2 * m + (k + 1))
                        nc.scalar.activation(wyT[:, k, HI, :, :], flip_bank[k][:, :].rearrange(
                            "p (c n) -> p c n", c=EC), ACT.Copy).then_inc(wyT_hi, 1)

            @block.vector
            def _(dve):
                dve.wait_ge(w_hi, 1)
                nc.vector.tensor_tensor(gw[:, LO, :, :], w_raw[:, :, :], gw[:, HI, :, :], ALU.subtract).then_inc(
                    w_ready, 1)
                token_moments(nc, dve, o, NT, stats, mean, half, var, GN_EPS, step, var_ready)
                dve.wait_ge(rstd_ready, 1)

                def normal(t, k):
                    if not isinstance(t, int):
                        dve.wait_ge(wy_ready, t - 1)
                    nc.vector.tensor_scalar(y[:, k, :], o[:, bass.ds(t, 1), :].rearrange("p a e -> p (a e)"),
                                            mean[:, bass.ds(t, 1)], rstd[:, bass.ds(t, 1)],
                                            ALU.subtract, ALU.mult).then_inc(y_normal, 1)

                def gate_y(t, k):
                    dve.wait_ge(gated, t + 1)
                    dve.wait_ge(y_ready, t + 1)
                    if not isinstance(t, int):
                        dve.wait_ge(flipped, t - 1)
                    nc.vector.scalar_tensor_tensor(wy[:, k, :], gate_bank[k][:, :], 0.0, y[:, k, :], ALU.max,
                                                   ALU.mult).then_inc(wy_ready, 1)

                def low(t, k):
                    dve.wait_ge(wyT_hi, t + 1)
                    nc.vector.tensor_tensor(wyT[:, k, LO, :, :], flip_bank[k][:, :].rearrange(
                        "p (c n) -> p c n", c=EC), wyT[:, k, HI, :, :], ALU.subtract).then_inc(wyT_ready, 1)

                def add(t, k):
                    dve.wait_ge(out_done, t + 1)
                    rows = x[:, bass.ds(t, 1), :].rearrange("p a e -> p (a e)")
                    nc.vector.tensor_tensor(rows, out_bank[k][:, :], rows, ALU.add).then_inc(added, 1)

                normal(0, 0)
                normal(1, 1)
                dve.wait_ge(w_hi, 2)
                nc.vector.tensor_tensor(ow[:, LO, :, :], w_raw[:, :, :], ow[:, HI, :, :], ALU.subtract).then_inc(
                    w_ready, 1)
                gate_y(0, 0)
                gate_y(1, 1)
                low(0, 0)
                with dve.Fori(1, NT // 2) as m:
                    normal(2 * m, 0)
                    normal(2 * m + 1, 1)
                    gate_y(2 * m, 0)
                    low(2 * m - 1, 1)
                    add(2 * m - 2, 0)
                    gate_y(2 * m + 1, 1)
                    low(2 * m, 0)
                    add(2 * m - 1, 1)
                low(NT - 1, 1)
                add(NT - 2, 0)
                add(NT - 1, 1)

            @block.gpsimd
            def _(pool):
                pool.wait_ge(var_ready, 1)
                nc.gpsimd.tensor_tensor(rstd[:, :], var[:, :], neg_half[:, 0:NT], ALU.pow).then_inc(rstd_ready, 1)
                pool.wait_ge(affine_loaded, 32)
                with pool.Fori(0, NT // 2) as m:
                    for k in range(2):
                        pool.wait_ge(y_normal, 2 * m + (k + 1))
                        nc.gpsimd.tensor_tensor(y[:, k, :], y[:, k, :], gamma_b[:, :], ALU.mult).then_inc(y_scaled, 1)
                        pool.wait_ge(y_scaled, 2 * m + (k + 1))
                        nc.gpsimd.tensor_tensor(y[:, k, :], y[:, k, :], beta_b[:, :], ALU.add).then_inc(y_ready, 1)


def route(nc, xT, ident, router, top_w, slot, shared_gate, expert_of):
    W = 32
    NB = N // 512
    with Space(nc, "route") as s:
        rw_raw = s.sb("rw_raw", [P, EC, P])
        rw = s.sb("rw", [P, 2, EC, P], F32R)
        logitsT = s.sb("logitsT", [W, N])
        logits = s.sb("logits", [P, NT, W])
        top = s.sb("top", [P, NT])
        shifted = s.sb("shifted", [P, NT, XP])
        expd = s.sb("expd", [P, NT, XP])
        total = s.sb("total", [P, NT])
        probs = s.sb("probs", [P, NT, XP])
        best = s.sb("best", [P, NT, 8])
        best_at = s.sb("best_at", [P, NT, 8], U32)
        chosen = s.sb("chosen", [P, NT, TOPK])
        top_sum = s.sb("top_sum", [P, NT])
        gate_exp = s.sb("gate_exp", [P, NT])
        expert_ids = s.sb("expert_ids", [P, XP])
        onehot = s.sb("onehot", [P, NT, TOPK, XP])
        member = s.sb("member", [P, NT, XP], BF16)
        before = s.sb("before", [P, P], BF16)
        ones = s.sb("ones", [P, P], BF16)
        in_tile = s.sb("in_tile", [P, NT, XP])
        prior = s.sb("prior", [P, NT, XP])
        count = s.sb("count", [P, XP])
        tile_starts = s.sb("tile_starts", [P, N // TS])
        used = s.sb("used", [P, XP, N // TS])
        tiles = s.sb("tiles", [P, XP])
        one_row = s.sb("one_row", [P, XP])
        tiles_to = s.sb("tiles_to", [P, XP])
        base = s.sb("base", [P, XP])
        place = s.sb("place", [P, NT, XP])
        picked = s.sb("picked", [P, NT, TOPK, XP])
        place_k = s.sb("place_k", [P, NT, TOPK])
        tile_ids = s.sb("tile_ids", [P, ROUTED])
        past = s.sb("past", [P, ROUTED, XP])
        owner = s.sb("owner", [P, ROUTED])
        bank = [s.bank(f"bank{k}") for k in range(NB)]
        flip_bank = s.bank("flip_bank")
        rank_bank = s.bank("rank_bank")
        count_bank = s.bank("count_bank")
        loaded = s.sem("loaded")
        rw_hi = s.sem("rw_hi")
        rw_ready = s.sem("rw_ready")
        logit_done = s.sem("logit_done")
        logit_copied = s.sem("logit_copied")
        flipped = s.sem("flipped")
        step = s.sem("step")
        exp_ready = s.sem("exp_ready")
        made = s.sem("made")
        tables_ready = s.sem("tables_ready")
        member_ready = s.sem("member_ready")
        ranked = s.sem("ranked")
        block = s.block()
        SHIFTED = 3

        @block.sync
        def _(sp):
            sp.dma_start(rw_raw[:, :, :], router).then_inc(loaded, 16)

        @block.gpsimd
        def _(pool):
            nc.gpsimd.memset(before[:, :], 1.0).then_inc(made, 1)
            nc.gpsimd.memset(ones[:, :], 1.0).then_inc(tables_ready, 1)
            nc.gpsimd.memset(one_row[:, :], 1.0).then_inc(tables_ready, 1)
            pool.wait_ge(made, 1)
            nc.gpsimd.affine_select(out=before[:, :], in_=before[:, :], compare_op=ALU.is_gt, fill=0.0, base=0,
                                    pattern=[[1, P]], channel_multiplier=-1).then_inc(tables_ready, 1)
            for table, step_by in ((expert_ids, 1), (tile_starts, TS), (tile_ids, 1)):
                nc.gpsimd.iota(table[:, :], pattern=[[step_by, table.shape[1]]], base=0, channel_multiplier=0,
                               allow_small_or_imprecise_dtypes=True).then_inc(tables_ready, 1)

        @block.tensor
        def _(pe):
            pe.wait_ge(rw_ready, 1)
            for n in range(NB):
                for c in range(EC):
                    cols = slice(n * 512, (n + 1) * 512)
                    last = matmul3(nc, bank[n][:, :], rw[:, HI, c, :], rw[:, LO, c, :], xT[:, HI, c, cols],
                                   xT[:, LO, c, cols], c == 0, c == EC - 1)
                last.then_inc(logit_done, 1)
            pe.wait_ge(logit_copied, NB)
            for t in range(NT):
                last = nc.tensor.transpose(flip_bank[:, t * W:(t + 1) * W], logitsT[:, t * P:(t + 1) * P],
                                           ident[0:W, 0:W])
            last.then_inc(flipped, 1)
            pe.wait_ge(member_ready, 1)
            pe.wait_ge(tables_ready, 6)
            m = member[:, :, :].rearrange("p t e -> p (t e)")
            nc.tensor.matmul(rank_bank[:, 0:NT * XP], before[:, :], m, start=True, stop=True)
            nc.tensor.matmul(count_bank[:, 0:NT * XP], ones[:, :], m, start=True, stop=True).then_inc(ranked, 1)

        @block.scalar
        def _(act):
            nc.scalar.preload_act_table(ACT.Exp)
            for n in range(NB):
                act.wait_ge(logit_done, n + 1)
                nc.scalar.activation(logitsT[:, n * 512:(n + 1) * 512], bank[n][0:W, :],
                                     ACT.Copy).then_inc(logit_copied, 1)
            act.wait_ge(step, SHIFTED)
            nc.scalar.activation(expd[:, :, :], shifted[:, :, :], ACT.Exp).then_inc(exp_ready, 1)
            nc.scalar.activation(gate_exp[:, :], logits[:, :, XP], ACT.Exp, scale=-1.0).then_inc(exp_ready, 1)

        @block.vector
        def _(dve):
            steps = [0]

            def chain(instruction):
                steps[0] += 1
                instruction.then_inc(step, 1)
                dve.wait_ge(step, steps[0])

            v = nc.vector
            dve.wait_ge(loaded, 16)
            v.tensor_copy(rw[:, HI, :, :], rw_raw[:, :, :]).then_inc(rw_hi, 1)
            dve.wait_ge(rw_hi, 1)
            v.tensor_tensor(rw[:, LO, :, :], rw_raw[:, :, :], rw[:, HI, :, :], ALU.subtract).then_inc(rw_ready, 1)
            dve.wait_ge(flipped, 1)
            chain(v.tensor_copy(logits[:, :, :], flip_bank[:, :].rearrange("p (t w) -> p t w", w=W)))
            chain(v.tensor_reduce(top[:, :], logits[:, :, 0:XP], AX_X, ALU.max))
            chain(v.tensor_tensor(shifted[:, :, :], logits[:, :, 0:XP],
                                  top[:, :].unsqueeze(2).to_broadcast([P, NT, XP]), ALU.subtract))
            assert steps[0] == SHIFTED
            dve.wait_ge(exp_ready, 1)
            chain(v.reduce_sum(total[:, :], expd[:, :, :], AX_X))
            chain(v.reciprocal(total[:, :], total[:, :]))
            chain(v.tensor_tensor(probs[:, :, :], expd[:, :, :], total[:, :].unsqueeze(2).to_broadcast([P, NT, XP]),
                                  ALU.mult))
            for t in range(NT):
                ins = v.max(best[:, t, :], probs[:, t, :])
            chain(ins)
            for t in range(NT):
                ins = v.max_index(best_at[:, t, :], best[:, t, :], probs[:, t, :])
            chain(ins)
            chain(v.tensor_copy(chosen[:, :, :], best_at[:, :, 0:TOPK]))
            chain(v.reduce_sum(top_sum[:, :], best[:, :, 0:TOPK], AX_X))
            chain(v.tensor_scalar(top_sum[:, :], top_sum[:, :], 1e-9, None, ALU.max))
            chain(v.reciprocal(top_sum[:, :], top_sum[:, :]))
            v.tensor_tensor(top_w[:, :, :], best[:, :, 0:TOPK],
                            top_sum[:, :].unsqueeze(2).to_broadcast([P, NT, TOPK]), ALU.mult)
            dve.wait_ge(tables_ready, 6)
            chain(v.tensor_tensor(onehot[:, :, :, :],
                                  chosen[:, :, :].unsqueeze(3).to_broadcast([P, NT, TOPK, XP]),
                                  expert_ids[:, :].unsqueeze(1).unsqueeze(1).to_broadcast([P, NT, TOPK, XP]),
                                  ALU.is_equal))
            with nc.allow_low_precision(reason="zeros and ones"):
                v.reduce_sum(member[:, :, :], onehot[:, :, :, :].rearrange("p t k e -> p t e k"),
                             AX_X).then_inc(member_ready, 1)
            dve.wait_ge(exp_ready, 2)
            chain(v.tensor_scalar(shared_gate[:, :], gate_exp[:, :], 1.0, None, ALU.add))
            v.reciprocal(shared_gate[:, :], shared_gate[:, :])
            dve.wait_ge(ranked, 1)
            chain(v.tensor_copy(in_tile[:, :, :], count_bank[:, 0:NT * XP].rearrange("p (t e) -> p t e", e=XP)))
            chain(v.memset(prior[:, 0, :], 0.0))
            for t in range(1, NT):
                chain(v.tensor_tensor(prior[:, t, :], prior[:, t - 1, :], in_tile[:, t - 1, :], ALU.add))
            chain(v.tensor_tensor(count[:, :], prior[:, NT - 1, :], in_tile[:, NT - 1, :], ALU.add))
            chain(v.tensor_tensor(used[:, :, :], count[:, :].unsqueeze(2).to_broadcast([P, XP, N // TS]),
                                  tile_starts[:, :].unsqueeze(1).to_broadcast([P, XP, N // TS]), ALU.is_gt))
            chain(v.reduce_sum(tiles[:, :], used[:, :, :], AX_X))
            chain(v.tensor_tensor_scan(tiles_to[:, :], one_row[:, :], tiles[:, :], 0.0, ALU.mult, ALU.add))
            chain(v.tensor_tensor(base[:, :], tiles_to[:, :], tiles[:, :], ALU.subtract))
            chain(v.tensor_scalar(base[:, :], base[:, :], float(TS), None, ALU.mult))
            chain(v.tensor_tensor(place[:, :, :], rank_bank[:, 0:NT * XP].rearrange("p (t e) -> p t e", e=XP),
                                  prior[:, :, :], ALU.add))
            chain(v.tensor_tensor(place[:, :, :], place[:, :, :], base[:, :].unsqueeze(1).to_broadcast([P, NT, XP]),
                                  ALU.add))
            chain(v.tensor_tensor(picked[:, :, :, :], onehot[:, :, :, :],
                                  place[:, :, :].unsqueeze(2).to_broadcast([P, NT, TOPK, XP]), ALU.mult))
            chain(v.reduce_sum(place_k[:, :, :], picked[:, :, :, :], AX_X))
            chain(v.tensor_copy(slot[:, :, :], place_k[:, :, :]))
            chain(v.tensor_tensor(past[:, :, :], tiles_to[:, :].unsqueeze(1).to_broadcast([P, ROUTED, XP]),
                                  tile_ids[:, :].unsqueeze(2).to_broadcast([P, ROUTED, XP]), ALU.is_le))
            chain(v.reduce_sum(owner[:, :], past[:, :, :], AX_X))
            chain(v.tensor_scalar(owner[:, :], owner[:, :], float(XP - 1), None, ALU.min))
            chain(v.tensor_copy(expert_of[:, :], owner[:, :]))


def experts(nc, x, rows, slot, shared_gate, expert_of, ident, row_dram, slot_rows, slot_out, w_gate, w_up, w_down):
    IT = 3
    WR = WI - 2 * P
    NS = SHARED_STEPS
    LAST = STEPS - 1
    with Space(nc, "moe") as s:
        x_rows = s.sb("x_rows", [P, 2, E])
        g_raw = s.sb("g_raw", [P, EC, WI])
        u_raw = s.sb("u_raw", [P, EC, WI])
        d_raw = s.sb("d_raw", [P, IT, E])
        g_w = s.sb("g_w", [P, 2, EC, WI], F32R)
        u_w = s.sb("u_w", [P, 2, EC, WI], F32R)
        d_w = s.sb("d_w", [P, 2, IT, E], F32R)
        hT = s.sb("hT", [P, 2, EC, TS], F32R)
        silu = s.sb("silu", [P, IT, TS])
        act_full = s.sb("act_full", [P, IT, TS])
        act_w = s.sb("act_w", [P, 2, IT, TS], F32R)
        y = s.sb("y", [P, 2, E])
        flip_bank = [s.bank(f"flip{k}") for k in range(2)]
        gate_bank = [s.bank(f"gate{k}") for k in range(2)]
        up_bank = [s.bank(f"up{k}") for k in range(2)]
        down_bank = [s.bank(f"down{k}") for k in range(2)]
        x_loaded = s.sem("x_loaded")
        g_loaded = s.sem("g_loaded")
        u_loaded = s.sem("u_loaded")
        d_loaded = s.sem("d_loaded")
        g_hi = s.sem("g_hi")
        u_hi = s.sem("u_hi")
        d_hi = s.sem("d_hi")
        g_ready = s.sem("g_ready")
        u_ready = s.sem("u_ready")
        d_ready = s.sem("d_ready")
        flipped = s.sem("flipped")
        hT_hi = s.sem("hT_hi")
        hT_ready = s.sem("hT_ready")
        gate_done = s.sem("gate_done")
        up_done = s.sem("up_done")
        silu_ready = s.sem("silu_ready")
        act_ready = s.sem("act_ready")
        act_hi = s.sem("act_hi")
        act_split = s.sem("act_split")
        down_done = s.sem("down_done")
        down_read = s.sem("down_read")
        y_stored = s.sem("y_stored")
        dispatched = s.sem("dispatched")
        block = s.block()

        def inner(bank_pair, n):
            return bank_pair[n // 2][0:(P if n < 2 else WR), (n % 2) * TS:(n % 2 + 1) * TS]

        def both(bank_pair, buf):
            return [(bank_pair[0][:, :], buf[:, 0:2, :].rearrange("p i n -> p (i n)")),
                    (bank_pair[1][0:WR, 0:TS], buf[0:WR, 2, :])]

        @block.sync
        def _(sp):
            def load_x(n, shared):
                if not isinstance(n, int) or n > 0:
                    sp.wait_ge(flipped, n)
                if shared:
                    src = row_dram.rearrange("(s t p) e -> s p t e", t=2, p=P)[bass.ds(n % (N // TS), 1), :, :, :]
                else:
                    src = slot_rows.rearrange("(s t p) e -> s p t e", t=2, p=P)[bass.ds(n - NS, 1), :, :, :]
                sp.dma_start(x_rows[:, :, :], src.rearrange("s p t e -> (s p) t e")).then_inc(x_loaded, 16)

            def expert(n, shared):
                if shared:
                    return n // (N // TS) + XP
                return sp.value_load(expert_of[0:1, bass.ds(n - NS, 1)], min_val=0, max_val=XP - 1)

            def load_w(n, e, w, raw, loaded, ready):
                if not isinstance(n, int) or n > 0:
                    sp.wait_ge(ready, n)
                sp.dma_start(raw[:, :, :], w[bass.ds(e, 1), :, :, :].rearrange("x p c n -> (x p) c n")).then_inc(
                    loaded, 16)

            def store_y(n):
                dst = slot_out.rearrange("(s t p) e -> s p t e", t=2, p=P)[bass.ds(n - NS, 1), :, :, :]
                sp.wait_ge(down_read, n + 1)
                sp.dma_start(dst.rearrange("s p t e -> (s p) t e"), y[:, :, :]).then_inc(y_stored, 16)

            def step(n, next_shared, this_shared, store):
                if next_shared is not None:
                    e = expert(n + 1, next_shared)
                    load_x(n + 1, next_shared)
                    load_w(n + 1, e, w_gate, g_raw, g_loaded, g_ready)
                    load_w(n + 1, e, w_up, u_raw, u_loaded, u_ready)
                e = expert(n, this_shared)
                load_w(n, e, w_down, d_raw, d_loaded, d_ready)
                if store:
                    store_y(n - 2)

            load_x(0, True)
            load_w(0, XP, w_gate, g_raw, g_loaded, g_ready)
            load_w(0, XP, w_up, u_raw, u_loaded, u_ready)
            step(0, True, True, False)
            with sp.Fori(1, NS - 1) as n:
                step(n, True, True, False)
            sp.wait_ge(dispatched, 16 * NT * TOPK)
            step(NS - 1, False, True, False)
            step(NS, False, False, False)
            step(NS + 1, False, False, False)
            with sp.Fori(NS + 2, LAST) as n:
                step(n, False, False, True)
            step(LAST, None, False, True)
            store_y(LAST - 1)
            store_y(LAST)
            sp.wait_ge(y_stored, 16 * ROUTED)

        @block.gpsimd
        def _(pool):
            for t in range(NT):
                for k in range(TOPK):
                    nc.gpsimd.indirect_dma_start(
                        out=slot_rows, out_offset=bass.IndirectOffsetOnAxis(ap=slot[:, t, k:k + 1], axis=0),
                        in_=rows[:, t, :], in_offset=None).then_inc(dispatched, 16)
            pool.wait_ge(dispatched, 16 * NT * TOPK)

        @block.tensor
        def _(pe):
            def flip(n):
                pe.wait_ge(x_loaded, 16 * n + 16)
                if not isinstance(n, int) or n > 0:
                    pe.wait_ge(hT_ready, n)
                for tile in range(2):
                    for c in range(EC):
                        bank, col = flip_bank[c // 2], (c % 2) * TS + tile * P
                        last = nc.tensor.transpose(bank[:, col:col + P], x_rows[:, tile, c * P:(c + 1) * P],
                                                   ident[:, :])
                last.then_inc(flipped, 1)

            def widen(n, w, w_ready, banks, banks_read, done):
                pe.wait_ge(hT_ready, n + 1)
                pe.wait_ge(w_ready, n + 1)
                if not isinstance(n, int) or n > 0:
                    pe.wait_ge(banks_read, n)
                for it in range(IT):
                    cols = slice(it * P, min((it + 1) * P, WI))
                    for c in range(EC):
                        last = matmul3(nc, inner(banks, it), w[:, HI, c, cols], w[:, LO, c, cols],
                                       hT[:, HI, c, :], hT[:, LO, c, :], c == 0, c == EC - 1)
                last.then_inc(done, 1)

            def narrow(n):
                pe.wait_ge(act_split, n + 1)
                pe.wait_ge(d_ready, n + 1)
                if not isinstance(n, int) or n > 0:
                    pe.wait_ge(down_read, n)
                for tile in range(2):
                    toks = slice(tile * P, (tile + 1) * P)
                    for it in range(IT):
                        k = P if it < 2 else WR
                        last = matmul3(nc, down_bank[tile][:, :], act_w[0:k, HI, it, toks], act_w[0:k, LO, it, toks],
                                       d_w[0:k, HI, it, :], d_w[0:k, LO, it, :], it == 0, it == IT - 1)
                last.then_inc(down_done, 1)

            def step(n, first, last):
                widen(n, g_w, g_ready, gate_bank, silu_ready, gate_done)
                widen(n, u_w, u_ready, up_bank, act_ready, up_done)
                if not last:
                    flip(n + 1)
                if not first:
                    narrow(n - 1)

            flip(0)
            step(0, True, False)
            with pe.Fori(1, LAST) as n:
                step(n, False, False)
            step(LAST, False, True)
            narrow(LAST)

        @block.scalar
        def _(act):
            nc.scalar.preload_act_table(ACT.Silu)

            def weights_high(n, loaded, raw, w, users, hi):
                act.wait_ge(loaded, 16 * n + 16)
                if not isinstance(n, int) or n > 0:
                    act.wait_ge(users, n)
                nc.scalar.activation(w[:, HI, :, :], raw[:, :, :], ACT.Copy).then_inc(hi, 1)

            def hT_high(n):
                act.wait_ge(flipped, n + 1)
                for k in range(2):
                    last = nc.scalar.activation(hT[:, HI, 2 * k:2 * k + 2, :].rearrange("p c n -> p (c n)"),
                                                flip_bank[k][:, :], ACT.Copy)
                last.then_inc(hT_hi, 1)

            def act_high(n):
                act.wait_ge(act_ready, n + 1)
                if not isinstance(n, int) or n > 0:
                    act.wait_ge(down_done, n)
                nc.scalar.activation(act_w[:, HI, 0:2, :], act_full[:, 0:2, :], ACT.Copy)
                nc.scalar.activation(act_w[0:WR, HI, 2, :], act_full[0:WR, 2, :], ACT.Copy).then_inc(act_hi, 1)

            def silus(n):
                act.wait_ge(gate_done, n + 1)
                if not isinstance(n, int) or n > 0:
                    act.wait_ge(act_ready, n)
                for src, dst in both(gate_bank, silu):
                    last = nc.scalar.activation(dst, src, ACT.Silu)
                last.then_inc(silu_ready, 1)

            def results(n):
                act.wait_ge(down_done, n + 1)
                if not isinstance(n, int) or n > NS:
                    act.wait_ge(y_stored, 16 * (n - NS))
                nc.scalar.activation(y[:, 0, :], down_bank[0][:, :], ACT.Copy)
                nc.scalar.activation(y[:, 1, :], down_bank[1][:, :], ACT.Copy).then_inc(down_read, 1)

            def step(n, first, last, keep):
                if not first:
                    act_high(n - 1)
                    weights_high(n - 1, d_loaded, d_raw, d_w, down_done, d_hi)
                silus(n)
                if not last:
                    weights_high(n + 1, g_loaded, g_raw, g_w, gate_done, g_hi)
                    hT_high(n + 1)
                    weights_high(n + 1, u_loaded, u_raw, u_w, up_done, u_hi)
                if keep:
                    results(n - 1)

            weights_high(0, g_loaded, g_raw, g_w, gate_done, g_hi)
            hT_high(0)
            weights_high(0, u_loaded, u_raw, u_w, up_done, u_hi)
            step(0, True, False, False)
            with act.Fori(1, NS + 1) as n:
                step(n, False, False, False)
            step(NS + 1, False, False, True)
            with act.Fori(NS + 2, LAST) as n:
                step(n, False, False, True)
            step(LAST, False, True, True)
            act_high(LAST)
            weights_high(LAST, d_loaded, d_raw, d_w, down_done, d_hi)
            results(LAST)

        @block.vector
        def _(dve):
            def weights_low(n, raw, w, hi, ready):
                dve.wait_ge(hi, n + 1)
                nc.vector.tensor_tensor(w[:, LO, :, :], raw[:, :, :], w[:, HI, :, :], ALU.subtract).then_inc(ready, 1)

            def hT_low(n):
                dve.wait_ge(hT_hi, n + 1)
                for k in range(2):
                    last = nc.vector.tensor_tensor(hT[:, LO, 2 * k:2 * k + 2, :].rearrange("p c n -> p (c n)"),
                                                   flip_bank[k][:, :],
                                                   hT[:, HI, 2 * k:2 * k + 2, :].rearrange("p c n -> p (c n)"),
                                                   ALU.subtract)
                last.then_inc(hT_ready, 1)

            def products(n):
                dve.wait_ge(silu_ready, n + 1)
                dve.wait_ge(up_done, n + 1)
                if not isinstance(n, int) or n > 0:
                    dve.wait_ge(act_split, n)
                for (src, full), (_, other) in zip(both(up_bank, act_full), both(up_bank, silu)):
                    last = nc.vector.tensor_tensor(full, src, other, ALU.mult)
                last.then_inc(act_ready, 1)

            def act_low(n):
                dve.wait_ge(act_hi, n + 1)
                nc.vector.tensor_tensor(act_w[:, LO, 0:2, :], act_full[:, 0:2, :], act_w[:, HI, 0:2, :], ALU.subtract)
                nc.vector.tensor_tensor(act_w[0:WR, LO, 2, :], act_full[0:WR, 2, :], act_w[0:WR, HI, 2, :],
                                        ALU.subtract).then_inc(act_split, 1)

            def add_shared(n):
                dve.wait_ge(down_done, n + 1)
                for tile in range(2):
                    t = (n % (N // TS)) * 2 + tile
                    rows_of = x[:, bass.ds(t, 1), :].rearrange("p a e -> p (a e)")
                    last = nc.vector.scalar_tensor_tensor(rows_of, down_bank[tile][:, :],
                                                          shared_gate[:, bass.ds(t, 1)], rows_of, ALU.mult, ALU.add)
                last.then_inc(down_read, 1)

            def step(n, first, last, add):
                if not first:
                    act_low(n - 1)
                    weights_low(n - 1, d_raw, d_w, d_hi, d_ready)
                if not last:
                    weights_low(n + 1, g_raw, g_w, g_hi, g_ready)
                products(n)
                if not last:
                    hT_low(n + 1)
                    weights_low(n + 1, u_raw, u_w, u_hi, u_ready)
                if add:
                    add_shared(n - 1)

            weights_low(0, g_raw, g_w, g_hi, g_ready)
            hT_low(0)
            weights_low(0, u_raw, u_w, u_hi, u_ready)
            step(0, True, False, False)
            with dve.Fori(1, NS + 1) as n:
                step(n, False, False, True)
            with dve.Fori(NS + 1, LAST) as n:
                step(n, False, False, False)
            step(LAST, False, True, False)
            act_low(LAST)
            weights_low(LAST, d_raw, d_w, d_hi, d_ready)


def combine(nc, x, slot, top_w, slot_out, out):
    DEPTH = 4
    with Space(nc, "combine") as s:
        got = s.sb("got", [P, DEPTH, TOPK, E])
        fetched = [s.sem(f"fetched{k}") for k in range(DEPTH)]
        step = s.sem("step")
        ready = s.sem("ready")
        stored = s.sem("stored")
        block = s.block()
        outv = out.rearrange("b (t p) e -> p (b t) e", p=P)

        @block.gpsimd
        def _(pool):
            for t in range(NT):
                if t >= DEPTH:
                    pool.wait_ge(ready, t - DEPTH + 1)
                for k in range(TOPK):
                    nc.gpsimd.indirect_dma_start(
                        out=got[:, t % DEPTH, k, :], out_offset=None, in_=slot_out,
                        in_offset=bass.IndirectOffsetOnAxis(ap=slot[:, t, k:k + 1], axis=0)).then_inc(
                        fetched[t % DEPTH], 16)

        @block.vector
        def _(dve):
            n = 0
            for t in range(NT):
                dve.wait_ge(fetched[t % DEPTH], 16 * TOPK * (t // DEPTH + 1))
                for k in range(TOPK):
                    ins = nc.vector.scalar_tensor_tensor(x[:, t, :], got[:, t % DEPTH, k, :], top_w[:, t, k:k + 1],
                                                         x[:, t, :], ALU.mult, ALU.add)
                    if k < TOPK - 1:
                        n += 1
                        ins.then_inc(step, 1)
                        dve.wait_ge(step, n)
                ins.then_inc(ready, 1)

        @block.sync
        def _(sp):
            for t in range(NT):
                sp.wait_ge(ready, t + 1)
                sp.dma_start(outv[:, t, :], x[:, t, :]).then_inc(stored, 16)
            sp.wait_ge(stored, 16 * NT)


def program(nc, ins, out, stop=9):
    xt_dram = nc.dram_tensor("xt_scratch", [B, P, 2, EC, S], F32, kind="Internal").ap()
    row_dram = nc.dram_tensor("row_scratch", [N, E], F32, kind="Internal").ap()
    slot_rows = nc.dram_tensor("slot_rows", [SLOTS, E], F32, kind="Internal").ap()
    slot_out = nc.dram_tensor("slot_out", [SLOTS, E], F32, kind="Internal").ap()
    with Space(nc, "all") as top:
        ident = top.sb("ident", [P, P])
        neg_half = top.sb("neg_half", [P, NT])
        x = top.sb("x", [P, NT, E])
        make_constants(nc, top, ident, neg_half)
        with Space(nc, "ln1buf") as s:
            xT = s.sb("xT", [P, 2, EC, N], F32R)
            layernorm_transpose(nc, "ln1", x, xT, ident, neg_half, x_dram=ins["x"], xt_dram=xt_dram)
        attention(nc, x, ident, neg_half, xt_dram, ins["wqkv"], ins["wo"], ins["q_scale"], ins["k_scale"],
                  slot_rows)
        if stop >= 2:
            with Space(nc, "ln2buf") as s:
                xT = s.sb("xT", [P, 2, EC, N], F32R)
                layernorm_transpose(nc, "ln2", x, xT, ident, neg_half)
                retention(nc, x, xT, ident, neg_half, ins["ctxT"], ins["head_w"], ins["decayT"], ins["gate_w"],
                          ins["out_w"], ins["gamma"], ins["beta"])
        if stop >= 3:
            top_w = top.sb("top_w", [P, NT, TOPK])
            slot = top.sb("slot", [P, NT, TOPK], U32)
            shared_gate = top.sb("shared_gate", [P, NT])
            expert_of = top.sb("expert_of", [P, ROUTED], I32)
            with Space(nc, "rows") as keep:
                rows = keep.sb("rows", [P, NT, E])
                with Space(nc, "ln3buf") as s:
                    xT = s.sb("xT", [P, 2, EC, N], F32R)
                    layernorm_transpose(nc, "ln3", x, xT, ident, neg_half, rows=rows, rows_dram=row_dram)
                    route(nc, xT, ident, ins["router"], top_w, slot, shared_gate, expert_of)
                experts(nc, x, rows, slot, shared_gate, expert_of, ident, row_dram, slot_rows, slot_out,
                        ins["w_gate"], ins["w_up"], ins["w_down"])
            combine(nc, x, slot, top_w, slot_out, out)
        if stop <= 2:
            with Space(nc, "store") as s:
                stored = s.sem("stored")
                block = s.block()

                @block.sync
                def _(sp):
                    sp.dma_start(out.rearrange("b (t p) e -> p (b t) e", p=P), x[:, :, :]).then_inc(stored, 16)
                    sp.wait_ge(stored, 16)


def decay_masks():
    heads = E // P
    gam = 1.0 - 2.0 ** (-5.0 - np.arange(heads))
    d = np.arange(S)[:, None] - np.arange(S)[None, :]
    m = np.where(d >= 0, gam[:, None, None] ** (-d[None].astype(float)), 0.0)
    m = m / np.sqrt(m.sum(axis=-1, keepdims=True)).transpose(0, 2, 1) / np.sqrt(P)
    return np.ascontiguousarray(m.transpose(0, 2, 1).reshape(heads, 2, P, S).transpose(0, 2, 1, 3)).astype(np.float32)


def kernel(stop=9, **inputs):
    from concourse import bacc
    from concourse.bass_utils import run_bass_kernel_spmd

    a = {k: np.ascontiguousarray(v) for k, v in inputs.items()}
    qkv = np.stack([a[f"L0_attn_w{c}"].reshape(EC, P, G, HG * P) for c in "qkv"])
    def with_shared(routed, shared):
        w = np.concatenate([a[routed], a[shared].reshape(E, SHARED, WI).transpose(1, 0, 2)])
        return np.ascontiguousarray(w.reshape(XP + SHARED, EC, P, WI).transpose(0, 2, 1, 3))

    down = np.zeros((XP + SHARED, 3 * P, E), np.float32)
    down[:XP, :WI] = a["L0_ffn_w_down"]
    down[XP:, :WI] = a["L0_ffn_sh_down"].reshape(SHARED, WI, E)
    router = np.zeros((P, EC, P), np.float32)
    router[:, :, :XP] = a["L0_ffn_router_w"].reshape(XP, EC, P).transpose(2, 1, 0)
    router[:, :, XP] = a["L0_ffn_sh_gate_w"].reshape(EC, P).T
    arrays = {
        "x": a["x"],
        "wqkv": np.ascontiguousarray(qkv.transpose(3, 0, 2, 1, 4)).reshape(G, 3, P, EC * HG * P),
        "wo": a["L0_attn_wo"].reshape(G, HG, P, E),
        "q_scale": a["L0_attn_q_scale"],
        "k_scale": a["L0_attn_k_scale"],
        "ctxT": np.ascontiguousarray(a["ctx_2048"].reshape(N, EC, P).transpose(1, 2, 0)),
        "head_w": a["L0_xattn_Wh"],
        "decayT": decay_masks(),
        "gate_w": a["L0_xattn_wg_w"],
        "out_w": a["L0_xattn_wo_w"],
        "gamma": a["L0_xattn_gn_gamma"],
        "beta": a["L0_xattn_gn_beta"],
        "router": router,
        "w_gate": with_shared("L0_ffn_w_gate", "L0_ffn_sh_gate"),
        "w_up": with_shared("L0_ffn_w_up", "L0_ffn_sh_up"),
        "w_down": np.ascontiguousarray(down.reshape(XP + SHARED, 3, P, E).transpose(0, 2, 1, 3)),
    }
    nc = bacc.Bacc("TRN2", target_bir_lowering=False, num_devices=1)
    ins = {k: nc.dram_tensor(f"in_{k}", v.shape, mybir.dt.from_np(v.dtype), kind="ExternalInput").ap()
           for k, v in arrays.items()}
    out = nc.dram_tensor("out", [B, S, E], F32, kind="ExternalOutput").ap()
    program(nc, ins, out, stop)
    r = run_bass_kernel_spmd(nc, [{f"in_{k}": v for k, v in arrays.items()}], core_ids=[0])
    return r.results[0]["out"]
```

```python
from contextlib import ExitStack

import concourse.bass as bass
from concourse import mybir
import numpy as np

F32 = mybir.dt.float32
F32R = mybir.dt.float32r
BF16 = mybir.dt.bfloat16
I32 = mybir.dt.int32
U32 = mybir.dt.uint32
ALU = mybir.AluOpType
ACT = mybir.ActivationFunctionType
AX_X = mybir.AxisListType.X

P = 128
B, S, E = 8, 256, 512
N = B * S
NT = N // P
EC = E // P
H = 16
HG = 4
G = H // HG
ROUNDS = G * B
LN_EPS = 1e-5
RMS_EPS = 1e-6
XP = 16
TOPK = 4
W = 32
WI = 352
SHARED = 4
WS = 1408
WP = 3 * P
TS = 256
ROUTED = N * TOPK // TS + XP - 1
SLOTS = N * TOPK + XP * TS
SHARED_STEPS = SHARED * (N // TS)
STEPS = SHARED_STEPS + ROUTED
ZERO_ROWS = 4
CLEARS = SLOTS // (P * ZERO_ROWS)
HI, LO = 0, 1


class Space:

    def __init__(self, nc, prefix):
        self.nc, self.prefix, self.ctx = nc, prefix, ExitStack()

    def __enter__(self):
        return self

    def __exit__(self, *a):
        return self.ctx.__exit__(*a)

    def sb(self, name, shape, dt=F32):
        return self.ctx.enter_context(self.nc.sbuf_tensor(f"{self.prefix}_{name}", shape, dt))

    def bank(self, name, shape=(P, 512), dt=F32):
        return self.ctx.enter_context(self.nc.psum_tensor(f"{self.prefix}_{name}", list(shape), dt))

    def sem(self, name):
        return self.ctx.enter_context(self.nc.semaphore(f"{self.prefix}_{name}"))

    def block(self):
        return self.ctx.enter_context(self.nc.Block())


def matmul3(nc, out, a_hi, a_lo, b_hi, b_lo, start, stop):
    nc.tensor.matmul(out, a_hi, b_lo, start=start, stop=False)
    nc.tensor.matmul(out, a_lo, b_hi, start=False, stop=False)
    return nc.tensor.matmul(out, a_hi, b_hi, start=False, stop=stop)


def make_constants(nc, sp, ident, neg_half):
    with Space(nc, "const") as s:
        done = s.sem("done")
        block = s.block()

        @block.gpsimd
        def _(pool):
            nc.gpsimd.memset(ident[:, :], 0.0).then_inc(done, 1)
            pool.wait_ge(done, 1)
            nc.gpsimd.affine_select(out=ident[:, :], in_=ident[:, :], compare_op=ALU.not_equal, fill=1.0,
                                    base=0, pattern=[[-1, P]], channel_multiplier=1).then_inc(done, 1)
            nc.gpsimd.memset(neg_half[:, :], -0.5).then_inc(done, 1)
            pool.wait_ge(done, 3)


def moments_from_stats(nc, dve, stats, mean, half, var, eps, step, base, done):
    if not isinstance(base, int) or base > 0:
        dve.wait_ge(step, base)
    nc.vector.tensor_tensor(mean, stats[:, :, 1], stats[:, :, 4], ALU.add).then_inc(step, 1)
    nc.vector.tensor_tensor(half, stats[:, :, 1], stats[:, :, 4], ALU.subtract).then_inc(step, 1)
    nc.vector.tensor_tensor(var, stats[:, :, 2], stats[:, :, 5], ALU.add).then_inc(step, 1)
    dve.wait_ge(step, base + 3)
    nc.vector.tensor_scalar(mean, mean, 0.5, None, ALU.mult).then_inc(step, 1)
    nc.vector.tensor_scalar(var, var, 1.0 / E, eps, ALU.mult, ALU.add).then_inc(step, 1)
    nc.vector.scalar_tensor_tensor(half, half, 0.25, half, ALU.mult, ALU.mult).then_inc(step, 1)
    dve.wait_ge(step, base + 6)
    nc.vector.tensor_tensor(var, var, half, ALU.add).then_inc(done, 1)


def layernorm_transpose(nc, prefix, x, stats, xT, ident, neg_half, x_dram=None, xt_dram=None, first_weights=None):
    PARTS = 4 if x_dram is not None else 1
    PT = NT // PARTS
    with Space(nc, prefix) as s:
        mean = s.sb("mean", [P, NT])
        half = s.sb("half", [P, NT])
        var = s.sb("var", [P, NT])
        rstd = s.sb("rstd", [P, NT])
        xn = s.sb("xn", [P, 2, E])
        flip = [s.bank(f"flip{k}") for k in range(2)]
        loaded = [s.sem(f"loaded{q}") for q in range(PARTS)] if x_dram is not None else None
        step = s.sem("step")
        var_ready = s.sem("var_ready")
        rstd_ready = s.sem("rstd_ready")
        xn_ready = s.sem("xn_ready")
        flipped = s.sem("flipped")
        hi_ready = s.sem("hi_ready")
        lo_ready = s.sem("lo_ready")
        stored = s.sem("stored")
        if first_weights is not None:
            raw_loaded = [s.sem(f"raw_loaded{k}") for k in range(2)]
            w_hi = s.sem("w_hi")
            w_ready = s.sem("w_ready")
        block = s.block()

        @block.sync
        def _(sp):
            if x_dram is not None:
                xv = x_dram.rearrange("b (t p) e -> p (b t) e", p=P)
                for q in range(PARTS):
                    sp.dma_start(x[:, q * PT:(q + 1) * PT, :], xv[:, q * PT:(q + 1) * PT, :]).then_inc(loaded[q], 16)
            if first_weights is not None:
                w, w_raw, wqkv, wo = first_weights

                def load_weights(c):
                    if c >= 2:
                        sp.wait_ge(w_ready, c - 1)
                    if c < 3:
                        sp.dma_start(w_raw[:, c % 2, :], wqkv[0, c, :, :]).then_inc(raw_loaded[c % 2], 16)
                    else:
                        sp.dma_start(w_raw[:, c % 2, :].rearrange("p (h e) -> p h e", h=HG),
                                     wo[0, :, :, :].rearrange("h d e -> d h e")).then_inc(raw_loaded[c % 2], 16)

                load_weights(0)
                load_weights(1)
            if xt_dram is not None:
                def store_batches(first, to):
                    with sp.Fori(first, to) as b:
                        sp.wait_ge(lo_ready, 2 * b + 2)
                        for part in (HI, LO):
                            sp.dma_start(xt_dram[bass.ds(b, 1), :, part, :, :].rearrange("b p c s -> (b p) c s"),
                                         xT[:, part, :, bass.ds(b * S, S)].bitcast(F32)).then_inc(stored, 16)

                store_batches(0, B - 3)
                load_weights(2)
                load_weights(3)
                store_batches(B - 3, B)
                sp.wait_ge(stored, 16 * 2 * B)

        @block.vector
        def _(dve):
            def moments(q):
                tiles = slice(q * PT, (q + 1) * PT)
                made = 0
                if loaded is not None:
                    made = PT
                    dve.wait_ge(loaded[q], 16)
                    with dve.Fori(q * PT, (q + 1) * PT) as t:
                        nc.vector.bn_stats(stats[:, bass.ds(t, 1), :].rearrange("p a s -> p (a s)"),
                                           x[:, bass.ds(t, 1), :].rearrange("p a e -> p (a e)")).then_inc(step, 1)
                moments_from_stats(nc, dve, stats[:, tiles, :], mean[:, tiles], half[:, tiles], var[:, tiles], LN_EPS,
                                   step, (made + 6) * q + made, var_ready)

            def split_lo(c):
                dve.wait_ge(w_hi, c + 1)
                nc.vector.tensor_tensor(first_weights[0][:, c, LO, :], first_weights[1][:, c % 2, :],
                                        first_weights[0][:, c, HI, :], ALU.subtract).then_inc(w_ready, 1)

            def normalise(t, k):
                if not isinstance(t, int) or t > 1:
                    dve.wait_ge(flipped, t - 1)
                nc.vector.tensor_scalar(xn[:, k, :], x[:, bass.ds(t, 1), :].rearrange("p a e -> p (a e)"),
                                        mean[:, bass.ds(t, 1)], rstd[:, bass.ds(t, 1)],
                                        ALU.subtract, ALU.mult).then_inc(xn_ready, 1)

            def low(t, k):
                dve.wait_ge(hi_ready, t + 1)
                nc.vector.tensor_tensor(xT[:, LO, :, bass.ds(t * P, P)],
                                        flip[k][:, :].rearrange("p (c n) -> p c n", c=EC),
                                        xT[:, HI, :, bass.ds(t * P, P)], ALU.subtract).then_inc(lo_ready, 1)

            def pairs(first, to):
                with dve.Fori(first, to) as m:
                    for k in range(2):
                        normalise(2 * m + k, k)
                        low(2 * m + (k - 2), k)

            moments(0)
            dve.wait_ge(rstd_ready, 1)
            normalise(0, 0)
            normalise(1, 1)
            if PARTS == 1:
                pairs(1, NT // 2)
            else:
                pairs(1, PT // 2)
                for q in range(1, PARTS):
                    moments(q)
                    if q == PARTS - 1:
                        split_lo(0)
                        split_lo(1)
                    dve.wait_ge(rstd_ready, q + 1)
                    pairs(q * PT // 2, (q + 1) * PT // 2)
            low(NT - 2, 0)
            low(NT - 1, 1)
            if first_weights is not None:
                split_lo(2)
                split_lo(3)

        @block.gpsimd
        def _(pool):
            for q in range(PARTS):
                tiles = slice(q * PT, (q + 1) * PT)
                pool.wait_ge(var_ready, q + 1)
                nc.gpsimd.tensor_tensor(rstd[:, tiles], var[:, tiles], neg_half[:, 0:PT], ALU.pow).then_inc(
                    rstd_ready, 1)

        @block.tensor
        def _(pe):
            def flips(t, k):
                pe.wait_ge(xn_ready, t + 1)
                if not isinstance(t, int):
                    pe.wait_ge(lo_ready, t - 1)
                for c in range(EC):
                    last = nc.tensor.transpose(flip[k][:, c * P:(c + 1) * P], xn[:, k, c * P:(c + 1) * P],
                                               ident[:, :])
                last.then_inc(flipped, 1)

            flips(0, 0)
            flips(1, 1)
            with pe.Fori(1, NT // 2) as m:
                for k in range(2):
                    flips(2 * m + k, k)

        @block.scalar
        def _(act):
            nc.scalar.preload_act_table(ACT.Exp)

            def split_hi(c):
                act.wait_ge(raw_loaded[c % 2], 16 * (c // 2 + 1))
                nc.scalar.activation(first_weights[0][:, c, HI, :], first_weights[1][:, c % 2, :],
                                     ACT.Copy).then_inc(w_hi, 1)

            def highs(first, to):
                with act.Fori(first, to) as m:
                    for k in range(2):
                        act.wait_ge(flipped, 2 * m + (k + 1))
                        nc.scalar.activation(xT[:, HI, :, bass.ds(m * (2 * P) + k * P, P)],
                                             flip[k][:, :].rearrange("p (c n) -> p c n", c=EC),
                                             ACT.Copy).then_inc(hi_ready, 1)

            if first_weights is None:
                highs(0, NT // 2)
            else:
                highs(0, (NT - PT) // 2)
                split_hi(0)
                split_hi(1)
                highs((NT - PT) // 2, NT // 2)
                split_hi(2)
                split_hi(3)


def attention(nc, x, stats, w, w_raw, ident, neg_half, xt_dram, wqkv, wo, q_scale, k_scale, slot_rows):
    AHEAD = 2
    D = P
    QK = 4
    with Space(nc, "attn") as s:
        xt = s.sb("xt", [P, 2, EC, S], F32R)
        squares = s.sb("squares", [P, 2, HG, D + 1])
        sums = s.sb("sums", [P, QK, HG])
        rms = s.sb("rms", [P, QK, HG])
        qk = s.sb("qk", [P, QK, HG * D])
        v = s.sb("v", [P, 2, 2, HG * D], F32R)
        qT = s.sb("qT", [P, HG, 2, S], F32R)
        kT = s.sb("kT", [P, HG, 2, S], F32R)
        scale_in = s.sb("scale_in", [P, 2])
        scale = s.sb("scale", [P, 1])
        neg_max = s.sb("neg_max", [P, HG, 2])
        row_sum = s.sb("row_sum", [P, HG, 2])
        inv_sum = s.sb("inv_sum", [P, HG, 2])
        probs = s.sb("probs", [P, 2, 2, S])
        pT = s.sb("pT", [P, 2, 2, 2, S], F32R)
        oT = s.sb("oT", [P, HG, 2, S], F32R)
        bank = [s.bank(f"bank{k}") for k in range(8)]
        proj_bank = bank[0:2]
        score_bank = bank[2:4]
        pT_bank = bank[4]
        oT_bank = bank[5]
        flip_bank = [bank[2], bank[3], bank[6], bank[7]]
        out_bank = [bank[4], bank[6]]

        xt_loaded = s.sem("xt_loaded")
        raw_loaded = [s.sem(f"raw_loaded{k}") for k in range(2)]
        w_hi = s.sem("w_hi")
        w_ready = s.sem("w_ready")
        scales_loaded = s.sem("scales_loaded")
        scale_ready = s.sem("scale_ready")
        ones_ready = s.sem("ones_ready")
        projected = s.sem("projected")
        squared = s.sem("squared")
        summed = s.sem("summed")
        rms_ready = s.sem("rms_ready")
        qk_ready = s.sem("qk_ready")
        v_hi = s.sem("v_hi")
        v_ready = s.sem("v_ready")
        flipped = s.sem("flipped")
        qkT_hi = s.sem("qkT_hi")
        qkT_ready = s.sem("qkT_ready")
        scored = s.sem("scored")
        max_ready = s.sem("max_ready")
        exp_ready = s.sem("exp_ready")
        inv_ready = s.sem("inv_ready")
        probs_ready = s.sem("probs_ready")
        p_flipped = s.sem("p_flipped")
        pT_hi = s.sem("pT_hi")
        pT_ready = s.sem("pT_ready")
        o_done = s.sem("o_done")
        oT_hi = s.sem("oT_hi")
        oT_ready = s.sem("oT_ready")
        out_done = s.sem("out_done")
        added = s.sem("added")
        stats_made = s.sem("stats_made")
        zeros = s.sb("zeros", [P, ZERO_ROWS * E])
        zeros_ready = s.sem("zeros_ready")
        slots_cleared = s.sem("slots_cleared")
        block = s.block()

        def rounds(eng, first, body, between=None):
            first()
            body(0, 0, 0)
            with eng.Fori(0, G - 1) as g:
                with eng.Fori(1, B - 2) as b:
                    body(g * B + b, b, g)
                body(g * B + (B - 2), B - 2, g, refill="qk")
                body(g * B + (B - 1), B - 1, g, refill="v")
                body(g * B + B, 0, g + 1, refill="o")
            if between is not None:
                between()
            with eng.Fori(1, B - 1) as b:
                body(b + (G - 1) * B, b, G - 1, last=True)
            body(G * B - 1, B - 1, G - 1, more=False, last=True)

        @block.sync
        def _(sp):
            def load_raw(g, c):
                sp.wait_ge(w_ready, 4 * g + (c - 1 + AHEAD))
                if c < 3:
                    src = wqkv[bass.ds(g + 1, 1), c, :, :].rearrange("g p n -> (g p) n")
                    sp.dma_start(w_raw[:, c % 2, :], src).then_inc(raw_loaded[c % 2], 16)
                else:
                    src = wo[bass.ds(g + 1, 1), :, :, :].rearrange("g h d e -> d (g h) e")
                    sp.dma_start(w_raw[:, c % 2, :].rearrange("p (h e) -> p h e", h=HG),
                                 src).then_inc(raw_loaded[c % 2], 16)

            def load_xt(j, b):
                if not isinstance(j, int) or j > 0:
                    sp.wait_ge(projected, 6 * j)
                sp.dma_start(xt[:, :, :, :].bitcast(F32), xt_dram[bass.ds(b, 1), :, :, :, :].rearrange(
                    "b p l c s -> (b p) l c s")).then_inc(xt_loaded, 16)

            def clear(n):
                sp.dma_start(slot_rows.rearrange("(n p r) e -> n p (r e)", p=P, r=ZERO_ROWS)[bass.ds(n, 1), :, :]
                             .rearrange("n p f -> (n p) f"), zeros[:, :]).then_inc(slots_cleared, 16)

            sp.dma_start(scale_in[:, 0:1], q_scale.rearrange("(p a) -> p a", a=1)).then_inc(scales_loaded, 16)
            sp.dma_start(scale_in[:, 1:2], k_scale.rearrange("(p a) -> p a", a=1)).then_inc(scales_loaded, 16)
            load_xt(0, 0)
            sp.wait_ge(zeros_ready, 1)
            with sp.Fori(0, G - 1) as g:
                load_xt(g * B + 1, 1)
                clear(g * B)
                load_raw(g, 0)
                load_raw(g, 1)
                with sp.Fori(1, B - 1) as b:
                    load_xt(g * B + b + 1, b + 1)
                    clear(g * B + b)
                load_raw(g, 2)
                load_xt(g * B + B, 0)
                clear(g * B + (B - 1))
                load_raw(g, 3)
            with sp.Fori(0, B - 1) as b:
                load_xt(b + ((G - 1) * B + 1), b + 1)
            sp.wait_ge(slots_cleared, 16 * CLEARS)

        @block.tensor
        def _(pe):
            def project(j, n, g=None):
                c, tile = ((n % 2, n // 2) if n < QK else (2, n - QK))
                if n == 0:
                    pe.wait_ge(xt_loaded, 16 * (j + 1))
                if g is not None and n in (0, 1, 4):
                    pe.wait_ge(w_ready, 4 * g + (c + 1 + AHEAD))
                if n >= 2:
                    pe.wait_ge(qk_ready, QK * j + (n - 1))
                elif not isinstance(j, int) or j > 0:
                    pe.wait_ge(v_ready, 2 * j + (n - 1))
                for e in range(EC):
                    cols = slice(e * HG * D, (e + 1) * HG * D)
                    toks = slice(tile * P, tile * P + P)
                    last = matmul3(nc, proj_bank[n % 2][:, :], xt[:, HI, e, toks], xt[:, LO, e, toks],
                                   w[:, c, HI, cols], w[:, c, LO, cols], e == 0, e == EC - 1)
                last.then_inc(projected, 1)

            def flip(j):
                pe.wait_ge(qk_ready, QK * j + QK)
                if not isinstance(j, int) or j > 0:
                    pe.wait_ge(exp_ready, HG * j)
                    pe.wait_ge(added, 2 * j - 2 + AHEAD)
                for u in range(HG):
                    for c in range(2):
                        for tile in range(2):
                            last = nc.tensor.transpose(flip_bank[u][:, (2 * c + tile) * P:(2 * c + tile + 1) * P],
                                                       qk[:, 2 * tile + c, u * D:(u + 1) * D], ident[:, :])
                    last.then_inc(flipped, 1)

            def score(i, u):
                pe.wait_ge(qkT_ready, HG * i + (u + 1))
                if u >= 2:
                    pe.wait_ge(exp_ready, HG * i + (u - 1))
                for tile in range(2):
                    toks = slice(tile * P, tile * P + P)
                    last = matmul3(nc, score_bank[u % 2][:, tile * S:(tile + 1) * S], qT[:, u, HI, toks],
                                   qT[:, u, LO, toks], kT[:, u, HI, :], kT[:, u, LO, :], True, True)
                last.then_inc(scored, 1)

            def flip_probs(i, u):
                pe.wait_ge(probs_ready, HG * i + (u + 1))
                if u == 0:
                    pe.wait_ge(added, 2 * i + AHEAD)
                else:
                    pe.wait_ge(pT_ready, HG * i + u)
                for kt in range(2):
                    for tile in range(2):
                        last = nc.tensor.transpose(pT_bank[:, kt * S + tile * P:kt * S + (tile + 1) * P],
                                                   probs[:, u % 2, tile, kt * P:(kt + 1) * P], ident[:, :])
                last.then_inc(p_flipped, 1)

            def weigh(i, u):
                pe.wait_ge(pT_ready, HG * i + (u + 1))
                if u == 0:
                    pe.wait_ge(v_ready, 2 * i + 2)
                else:
                    pe.wait_ge(oT_ready, HG * i + u)
                for kt in range(2):
                    last = matmul3(nc, oT_bank[:, 0:S], v[:, kt, HI, u * D:(u + 1) * D],
                                   v[:, kt, LO, u * D:(u + 1) * D], pT[:, u % 2, HI, kt, :],
                                   pT[:, u % 2, LO, kt, :], kt == 0, kt == 1)
                last.then_inc(o_done, 1)

            def output(i, g, more):
                pe.wait_ge(oT_ready, HG * i + HG)
                pe.wait_ge(w_ready, 4 * g + AHEAD)
                for tile in range(2):
                    if tile == 1 and more:
                        pe.wait_ge(qkT_ready, HG * i + (HG + 3))
                    for u in range(HG):
                        toks = slice(tile * P, tile * P + P)
                        cols = slice(u * E, (u + 1) * E)
                        last = matmul3(nc, out_bank[tile][:, :], oT[:, u, HI, toks], oT[:, u, LO, toks],
                                       w[:, 3, HI, cols], w[:, 3, LO, cols], u == 0, u == HG - 1)
                    last.then_inc(out_done, 1)

            def body(i, b, g, more=True, refill=None, last=False):
                j = i + 1
                new = g if refill == "v" else None
                score(i, 0)
                if more:
                    project(j, 0, new)
                score(i, 1)
                if more:
                    project(j, 1, new)
                flip_probs(i, 0)
                score(i, 2)
                if more:
                    project(j, 2, new)
                weigh(i, 0)
                flip_probs(i, 1)
                score(i, 3)
                if more:
                    project(j, 3, new)
                weigh(i, 1)
                flip_probs(i, 2)
                if more:
                    project(j, 4, new)
                weigh(i, 2)
                flip_probs(i, 3)
                if more:
                    project(j, 5, new)
                weigh(i, 3)
                if more:
                    flip(j)
                output(i, g, more)

            def first():
                for n in range(6):
                    project(0, n)
                flip(0)

            rounds(pe, first, body)

        @block.scalar
        def _(act):
            def split_hi(g, c):
                act.wait_ge(raw_loaded[c % 2], 32 * g + 16 * (c // 2 + 1))
                if c < 3:
                    act.wait_ge(projected, 6 * B * g + (6 * (B - 1) + (3, 4, 6)[c]))
                else:
                    act.wait_ge(out_done, 2 * B * g + 2 * B)
                nc.scalar.activation(w[:, c, HI, :], w_raw[:, c % 2, :], ACT.Copy).then_inc(w_hi, 1)

            def square(j, n):
                act.wait_ge(projected, 6 * j + (n + 1))
                if not (isinstance(j, int) and j == 0 and n < 2):
                    act.wait_ge(summed, QK * j + (n - 1))
                nc.scalar.activation(squares[:, n % 2, :, 0:D],
                                     proj_bank[n % 2][:, :].rearrange("p (h d) -> p h d", h=HG),
                                     ACT.Square).then_inc(squared, 1)

            def v_high(j, tile):
                act.wait_ge(projected, 6 * j + (QK + tile + 1))
                if not isinstance(j, int) or j > 0:
                    act.wait_ge(o_done, HG * j)
                nc.scalar.activation(v[:, tile, HI, :], proj_bank[tile][:, :], ACT.Copy).then_inc(v_hi, 1)

            def qkT_high(j, u):
                act.wait_ge(flipped, HG * j + (u + 1))
                nc.scalar.activation(qT[:, u, HI, :], flip_bank[u][:, 0:S], ACT.Copy, scale=scale[:, 0:1])
                nc.scalar.activation(kT[:, u, HI, :], flip_bank[u][:, S:2 * S], ACT.Copy).then_inc(qkT_hi, 1)

            def exponentials(i, u):
                act.wait_ge(max_ready, HG * i + (u + 1))
                if u >= 2:
                    act.wait_ge(p_flipped, HG * i + (u - 1))
                for tile in range(2):
                    last = nc.scalar.activation(probs[:, u % 2, tile, :], score_bank[u % 2][:, tile * S:(tile + 1) * S],
                                                ACT.Exp, bias=neg_max[:, u, tile:tile + 1],
                                                accum_out=row_sum[:, u, tile:tile + 1])
                last.then_inc(exp_ready, 1)

            def pT_high(i, u):
                act.wait_ge(p_flipped, HG * i + (u + 1))
                nc.scalar.activation(pT[:, u % 2, HI, :, :].rearrange("p k s -> p (k s)"), pT_bank[:, :],
                                     ACT.Copy).then_inc(pT_hi, 1)

            def oT_high(i, u):
                act.wait_ge(o_done, HG * i + (u + 1))
                nc.scalar.activation(oT[:, u, HI, :], oT_bank[:, 0:S], ACT.Copy).then_inc(oT_hi, 1)

            def body(i, b, g, more=True, refill=None, last=False):
                j = i + 1
                exponentials(i, 0)
                if more:
                    square(j, 0)
                exponentials(i, 1)
                if refill == "v":
                    split_hi(g, 2)
                if more:
                    square(j, 1)
                pT_high(i, 0)
                exponentials(i, 2)
                if more:
                    square(j, 2)
                oT_high(i, 0)
                pT_high(i, 1)
                exponentials(i, 3)
                if more:
                    square(j, 3)
                oT_high(i, 1)
                if refill == "qk":
                    split_hi(g, 0)
                if refill == "o":
                    split_hi(g - 1, 3)
                pT_high(i, 2)
                oT_high(i, 2)
                if refill == "qk":
                    split_hi(g, 1)
                pT_high(i, 3)
                oT_high(i, 3)
                if more:
                    for u in range(HG):
                        qkT_high(j, u)
                    v_high(j, 0)
                    v_high(j, 1)

            def first():
                act.wait_ge(ones_ready, 1)
                act.wait_ge(scale_ready, 1)
                for n in range(QK):
                    square(0, n)
                v_high(0, 0)
                v_high(0, 1)
                for u in range(HG):
                    qkT_high(0, u)

            rounds(act, first, body)

        @block.vector
        def _(dve):
            def split_lo(g, c):
                dve.wait_ge(w_hi, 4 * g + (c + 1))
                nc.vector.tensor_tensor(w[:, c, LO, :], w_raw[:, c % 2, :], w[:, c, HI, :],
                                        ALU.subtract).then_inc(w_ready, 1)

            def sum_squares(j, n):
                dve.wait_ge(squared, QK * j + (n + 1))
                nc.vector.reduce_sum(sums[:, n, :], squares[:, n % 2, :, :], AX_X).then_inc(summed, 1)

            def scale_rows(j, n):
                dve.wait_ge(rms_ready, QK * j + (n + 1))
                nc.vector.tensor_tensor(qk[:, n, :].rearrange("p (h d) -> p h d", h=HG),
                                        proj_bank[n % 2][:, :].rearrange("p (h d) -> p h d", h=HG),
                                        rms[:, n, :].unsqueeze(2).to_broadcast([P, HG, D]),
                                        ALU.mult).then_inc(qk_ready, 1)

            def v_low(j, tile):
                dve.wait_ge(v_hi, 2 * j + (tile + 1))
                nc.vector.tensor_tensor(v[:, tile, LO, :], proj_bank[tile][:, :], v[:, tile, HI, :],
                                        ALU.subtract).then_inc(v_ready, 1)

            def qkT_low(j, u):
                dve.wait_ge(qkT_hi, HG * j + (u + 1))
                nc.vector.scalar_tensor_tensor(qT[:, u, LO, :], flip_bank[u][:, 0:S], scale[:, 0:1],
                                               qT[:, u, HI, :], ALU.mult, ALU.subtract)
                nc.vector.tensor_tensor(kT[:, u, LO, :], flip_bank[u][:, S:2 * S], kT[:, u, HI, :],
                                        ALU.subtract).then_inc(qkT_ready, 1)

            def maxima(i, u):
                dve.wait_ge(scored, HG * i + (u + 1))
                nc.vector.tensor_reduce(neg_max[:, u, :], score_bank[u % 2][:, :].rearrange("p (t k) -> p t k", t=2),
                                        AX_X, ALU.max, negate=True).then_inc(max_ready, 1)

            def invert_sums(i, u):
                dve.wait_ge(exp_ready, HG * i + (u + 1))
                nc.vector.reciprocal(inv_sum[:, u, :], row_sum[:, u, :]).then_inc(inv_ready, 1)

            def pT_low(i, u):
                dve.wait_ge(pT_hi, HG * i + (u + 1))
                nc.vector.tensor_tensor(pT[:, u % 2, LO, :, :].rearrange("p k s -> p (k s)"), pT_bank[:, :],
                                        pT[:, u % 2, HI, :, :].rearrange("p k s -> p (k s)"),
                                        ALU.subtract).then_inc(pT_ready, 1)

            def oT_low(i, u):
                dve.wait_ge(oT_hi, HG * i + (u + 1))
                nc.vector.tensor_tensor(oT[:, u, LO, :], oT_bank[:, 0:S], oT[:, u, HI, :],
                                        ALU.subtract).then_inc(oT_ready, 1)

            def add_output(i, b, tile):
                dve.wait_ge(out_done, 2 * i + (tile + 1))
                rows = x[:, bass.ds(b * 2 + tile, 1), :].rearrange("p a e -> p (a e)")
                nc.vector.tensor_tensor(rows, out_bank[tile][:, :], rows, ALU.add).then_inc(added, 1)

            def body(i, b, g, more=True, refill=None, last=False):
                j = i + 1
                maxima(i, 0)
                if more:
                    sum_squares(j, 0)
                invert_sums(i, 0)
                maxima(i, 1)
                if refill == "v":
                    split_lo(g, 2)
                if more:
                    scale_rows(j, 0)
                    sum_squares(j, 1)
                invert_sums(i, 1)
                pT_low(i, 0)
                maxima(i, 2)
                if more:
                    scale_rows(j, 1)
                    sum_squares(j, 2)
                invert_sums(i, 2)
                oT_low(i, 0)
                pT_low(i, 1)
                maxima(i, 3)
                if more:
                    scale_rows(j, 2)
                    sum_squares(j, 3)
                invert_sums(i, 3)
                oT_low(i, 1)
                if more:
                    scale_rows(j, 3)
                if refill == "qk":
                    split_lo(g, 0)
                if refill == "o":
                    split_lo(g - 1, 3)
                pT_low(i, 2)
                oT_low(i, 2)
                if refill == "qk":
                    split_lo(g, 1)
                pT_low(i, 3)
                oT_low(i, 3)
                if more:
                    for u in range(HG):
                        qkT_low(j, u)
                    v_low(j, 0)
                    v_low(j, 1)
                add_output(i, b, 0)
                add_output(i, b, 1)
                if last:
                    final_stats(i, b)

            def final_stats(i, b):
                for tile in range(2):
                    dve.wait_ge(added, i * 2 + (tile + 1 + AHEAD))
                    nc.vector.bn_stats(stats[:, bass.ds(b * 2 + tile, 1), :].rearrange("p a s -> p (a s)"),
                                       x[:, bass.ds(b * 2 + tile, 1), :].rearrange("p a e -> p (a e)")).then_inc(
                        stats_made, 1)

            def first():
                nc.vector.memset(squares[:, :, :, D:D + 1], RMS_EPS * D).then_inc(ones_ready, 1)
                dve.wait_ge(scales_loaded, 32)
                nc.vector.tensor_scalar(scale[:, :], scale_in[:, 0:1], scale_in[:, 1:2], float(D), ALU.mult,
                                        ALU.mult).then_inc(scale_ready, 1)
                dve.sem_inc(w_ready, AHEAD)
                dve.sem_inc(added, AHEAD)
                dve.wait_ge(ones_ready, 1)
                for n in range(QK):
                    sum_squares(0, n)
                    scale_rows(0, n)
                v_low(0, 0)
                v_low(0, 1)
                for u in range(HG):
                    qkT_low(0, u)

            rounds(dve, first, body, lambda: final_stats((G - 1) * B, 0))
            dve.wait_ge(stats_made, NT)

        @block.gpsimd
        def _(pool):
            def inverse_rms(j, n):
                pool.wait_ge(summed, QK * j + (n + 1))
                nc.gpsimd.tensor_tensor(rms[:, n, :], sums[:, n, :], neg_half[:, 0:HG], ALU.pow).then_inc(rms_ready, 1)

            def normalise(i, u):
                pool.wait_ge(inv_ready, HG * i + (u + 1))
                nc.gpsimd.tensor_tensor(probs[:, u % 2, :, :], probs[:, u % 2, :, :],
                                        inv_sum[:, u, :].unsqueeze(2).to_broadcast([P, 2, S]),
                                        ALU.mult).then_inc(probs_ready, 1)

            def body(i, b, g, more=True, refill=None, last=False):
                for u in range(HG):
                    if more:
                        inverse_rms(i + 1, u)
                    normalise(i, u)

            def first():
                nc.gpsimd.memset(zeros[:, :], 0.0).then_inc(zeros_ready, 1)
                for n in range(QK):
                    inverse_rms(0, n)

            rounds(pool, first, body)


def retention(nc, x, xT, o, ident, neg_half, ctxT, head_w, decayT, gate_w, out_w, gamma, beta, router, row_dram,
              exp_logits, exp_gate):
    RH = E // P
    NB = N // 512
    GN_EPS = 1e-3
    rows = o
    with Space(nc, "ret") as keep:
        w_raw = keep.sb("w_raw", [P, EC, E])
        o_stats = keep.sb("o_stats", [P, NT, 2 * RH, 3])
        with Space(nc, "heads") as s:
            ctx_raw = w_raw[:, 0:2, :]
            ctx = s.sb("ctx", [P, 2, 2, 512], F32R)
            hw_raw = s.sb("hw_raw", [P, P])
            hw = s.sb("hw", [P, 2, P], F32R)
            decay = s.sb("decay", [P, 2, S])
            k_full = w_raw[:, 2:4, :]
            kT = s.sb("kT", [P, 2, N], F32R)
            qT = s.sb("qT", [P, 2, N], F32R)
            v = s.sb("v", [P, 2, 2, B, P], F32R)
            masked = k_full[:, 0, :].rearrange("p (t s) -> p t s", t=2)
            a32 = k_full[:, 1, :].rearrange("p (t s) -> p t s", t=2)
            a = s.sb("a", [P, 2, 2, S], F32R)
            bank = [s.bank(f"bank{k}") for k in range(8)]
            k_bank = bank[0:2]
            v_bank = bank[2:4]
            q_bank = [bank[4], bank[5], bank[4], bank[5]]
            score_bank = bank[6:8]
            o_bank = [bank[0], bank[1], bank[2], bank[3]]
            ctx_loaded = [s.sem(f"ctx_loaded{k}") for k in range(2)]
            head_loaded = s.sem("head_loaded")
            ctx_hi = s.sem("ctx_hi")
            ctx_ready = s.sem("ctx_ready")
            hw_hi = s.sem("hw_hi")
            hw_ready = s.sem("hw_ready")
            k_done = s.sem("k_done")
            k_full_ready = s.sem("k_full_ready")
            k_hi = s.sem("k_hi")
            k_ready = s.sem("k_ready")
            q_done = s.sem("q_done")
            q_hi = s.sem("q_hi")
            q_ready = s.sem("q_ready")
            v_flipped = s.sem("v_flipped")
            v_hi = s.sem("v_hi")
            v_ready = s.sem("v_ready")
            scored = s.sem("scored")
            decayed = s.sem("decayed")
            negated = s.sem("negated")
            a_full = s.sem("a_full")
            a_hi = s.sem("a_hi")
            a_ready = s.sem("a_ready")
            o_done = s.sem("o_done")
            o_read = s.sem("o_read")
            stats_made = s.sem("stats_made")
            gate_w_loaded = s.sem("gate_w_loaded")
            block = s.block()

            @block.sync
            def _(sp):
                def load_head(h, first):
                    if not first:
                        sp.wait_ge(decayed, 2 * h)
                    sp.dma_start(hw_raw[:, :], head_w[bass.ds(h, 1), :, :].rearrange("h d e -> (h d) e")).then_inc(
                        head_loaded, 16)
                    sp.dma_start(decay[:, :, :], decayT[bass.ds(h, 1), :, :, :].rearrange(
                        "h p t s -> (h p) t s")).then_inc(head_loaded, 16)
                    for n in range(NB):
                        if n >= 2:
                            sp.wait_ge(ctx_ready, NB * h + (n - 1))
                        sp.dma_start(ctx_raw[:, n % 2, :], ctxT[bass.ds(h, 1), :, n * 512:(n + 1) * 512].rearrange(
                            "h d n -> (h d) n")).then_inc(ctx_loaded[n % 2], 16)

                load_head(0, True)
                with sp.Fori(1, RH) as h:
                    load_head(h, False)
                sp.wait_ge(ctx_ready, NB * RH)
                sp.wait_ge(a_ready, 2 * RH)
                sp.dma_start(w_raw[:, :, :], gate_w.rearrange("(c p) n -> p c n", p=P)).then_inc(gate_w_loaded, 16)
                sp.wait_ge(gate_w_loaded, 16)

            @block.tensor
            def _(pe):
                def head(h, first):
                    def keys(n):
                        if n == 0:
                            pe.wait_ge(hw_ready, h + 1)
                            if not first:
                                pe.wait_ge(o_read, 4 * h)
                        if n >= 2:
                            pe.wait_ge(k_ready, NB * h + (n - 1))
                        pe.wait_ge(ctx_ready, NB * h + (n + 1))
                        matmul3(nc, k_bank[n % 2][:, :], hw[:, HI, :], hw[:, LO, :], ctx[:, n % 2, HI, :],
                                ctx[:, n % 2, LO, :], True, True).then_inc(k_done, 1)

                    def values(n):
                        pe.wait_ge(k_full_ready, NB * h + (n + 1))
                        if n >= 2:
                            pe.wait_ge(v_ready, NB * h + (n - 1))
                        for q in range(4):
                            last = nc.tensor.transpose(v_bank[n % 2][:, q * P:(q + 1) * P],
                                                       k_full[:, n % 2, q * P:(q + 1) * P], ident[:, :])
                        last.then_inc(v_flipped, 1)

                    def queries(n):
                        if n >= 2:
                            pe.wait_ge(q_ready, NB * h + (n - 1))
                        cols = slice(n * 512, (n + 1) * 512)
                        matmul3(nc, q_bank[n][:, :], hw[:, HI, :], hw[:, LO, :],
                                xT[:, HI, bass.ds(h, 1), cols].rearrange("p a n -> p (a n)"),
                                xT[:, LO, bass.ds(h, 1), cols].rearrange("p a n -> p (a n)"),
                                True, True).then_inc(q_done, 1)

                    keys(0)
                    keys(1)
                    queries(0)
                    values(0)
                    keys(2)
                    queries(1)
                    values(1)
                    keys(3)
                    queries(2)
                    values(2)
                    queries(3)
                    values(3)
                    pe.wait_ge(k_ready, NB * h + NB)
                    pe.wait_ge(q_ready, NB * h + NB)
                    for kt in range(2):
                        for b in range(B):
                            keys_of = slice(b * S + kt * P, b * S + (kt + 1) * P)
                            queries_of = slice(b * S, (b + 1) * S)
                            last = matmul3(nc, score_bank[kt][:, 0:S], kT[:, HI, keys_of], kT[:, LO, keys_of],
                                           qT[:, HI, queries_of], qT[:, LO, queries_of], b == 0, b == B - 1)
                        last.then_inc(scored, 1)
                    pe.wait_ge(a_ready, 2 * h + 2)
                    pe.wait_ge(v_ready, NB * h + NB)
                    for st in range(2):
                        for half in range(2):
                            for kt in range(2):
                                batches = slice(4 * half, 4 * half + 4)
                                last = matmul3(nc, o_bank[2 * st + half][:, :], a[:, HI, kt, st * P:(st + 1) * P],
                                               a[:, LO, kt, st * P:(st + 1) * P], v[:, HI, kt, batches, :],
                                               v[:, LO, kt, batches, :], kt == 0, kt == 1)
                            last.then_inc(o_done, 1)

                head(0, True)
                with pe.Fori(1, RH) as h:
                    head(h, False)

            def v_view(part, n):
                return v[:, part, :, 2 * n:2 * n + 2, :]

            def v_psum(n):
                return v_bank[n % 2][:, :].rearrange("p (b t e) -> p t b e", b=2, t=2)

            @block.scalar
            def _(act):
                nc.scalar.preload_act_table(ACT.Exp)
                with act.Fori(0, RH) as h:
                    def keys(n):
                        act.wait_ge(k_done, NB * h + (n + 1))
                        if n >= 2:
                            act.wait_ge(v_flipped, NB * h + (n - 1))
                        nc.scalar.activation(k_full[:, n % 2, :], k_bank[n % 2][:, :], ACT.Copy).then_inc(
                            k_full_ready, 1)
                        nc.scalar.activation(kT[:, HI, n * 512:(n + 1) * 512], k_bank[n % 2][:, :],
                                             ACT.Copy).then_inc(k_hi, 1)

                    def queries(n):
                        act.wait_ge(q_done, NB * h + (n + 1))
                        nc.scalar.activation(qT[:, HI, n * 512:(n + 1) * 512], q_bank[n][:, :],
                                             ACT.Copy).then_inc(q_hi, 1)

                    def values(n):
                        act.wait_ge(v_flipped, NB * h + (n + 1))
                        nc.scalar.activation(v_view(HI, n), v_psum(n), ACT.Copy).then_inc(v_hi, 1)

                    keys(0)
                    keys(1)
                    queries(0)
                    values(0)
                    keys(2)
                    queries(1)
                    values(1)
                    keys(3)
                    queries(2)
                    values(2)
                    queries(3)
                    values(3)
                    for kt in range(2):
                        act.wait_ge(a_full, 2 * h + (kt + 1))
                        nc.scalar.activation(a[:, HI, kt, :], a32[:, kt, :], ACT.Copy).then_inc(a_hi, 1)
                    for st in range(2):
                        for half in range(2):
                            act.wait_ge(o_done, 4 * h + (2 * st + half + 1))
                            tiles = o[:, 8 * half:8 * half + 8, bass.ds(h * P, P)].rearrange(
                                "p (b s) e -> p b s e", s=2)[:, :, st, :]
                            nc.scalar.activation(tiles, o_bank[2 * st + half][:, :].rearrange(
                                "p (b e) -> p b e", b=4), ACT.Copy).then_inc(o_read, 1)

            @block.vector
            def _(dve):
                def head_stats(h):
                    for t in range(NT):
                        dve.wait_ge(o_read, 4 * h + (4 if t == NT - 1 else 2 * (t % 2) + t // 8 + 1))
                        nc.vector.bn_stats(o_stats[:, t, bass.ds(2 * h, 2), :].rearrange("p a s -> p (a s)"),
                                           o[:, t, bass.ds(h * P, P)]).then_inc(stats_made, 1)

                def head(h, first):
                    def context(n):
                        dve.wait_ge(ctx_loaded[n % 2], 8 * NB * h + 16 * (n // 2 + 1))
                        if n >= 2:
                            dve.wait_ge(k_done, NB * h + (n - 1))
                        nc.vector.tensor_copy(ctx[:, n % 2, HI, :], ctx_raw[:, n % 2, :]).then_inc(ctx_hi, 1)
                        dve.wait_ge(ctx_hi, NB * h + (n + 1))
                        nc.vector.tensor_tensor(ctx[:, n % 2, LO, :], ctx_raw[:, n % 2, :], ctx[:, n % 2, HI, :],
                                                ALU.subtract).then_inc(ctx_ready, 1)

                    def keys(n):
                        dve.wait_ge(k_hi, NB * h + (n + 1))
                        nc.vector.tensor_tensor(kT[:, LO, n * 512:(n + 1) * 512], k_bank[n % 2][:, :],
                                                kT[:, HI, n * 512:(n + 1) * 512], ALU.subtract).then_inc(k_ready, 1)

                    def queries(n):
                        dve.wait_ge(q_hi, NB * h + (n + 1))
                        nc.vector.tensor_tensor(qT[:, LO, n * 512:(n + 1) * 512], q_bank[n][:, :],
                                                qT[:, HI, n * 512:(n + 1) * 512], ALU.subtract).then_inc(q_ready, 1)

                    def values(n):
                        dve.wait_ge(v_hi, NB * h + (n + 1))
                        nc.vector.tensor_tensor(v_view(LO, n), v_psum(n), v_view(HI, n),
                                                ALU.subtract).then_inc(v_ready, 1)

                    dve.wait_ge(head_loaded, 32 * h + 32)
                    if not first:
                        dve.wait_ge(q_done, NB * h)
                    nc.vector.tensor_copy(hw[:, HI, :], hw_raw[:, :]).then_inc(hw_hi, 1)
                    dve.wait_ge(hw_hi, h + 1)
                    nc.vector.tensor_tensor(hw[:, LO, :], hw_raw[:, :], hw[:, HI, :], ALU.subtract).then_inc(hw_ready, 1)
                    context(0)
                    context(1)
                    keys(0)
                    context(2)
                    keys(1)
                    queries(0)
                    context(3)
                    values(0)
                    keys(2)
                    queries(1)
                    values(1)
                    keys(3)
                    queries(2)
                    values(2)
                    queries(3)
                    values(3)
                    if not first:
                        head_stats(h - 1)
                    for kt in range(2):
                        dve.wait_ge(scored, 2 * h + (kt + 1))
                        nc.vector.tensor_tensor(masked[:, kt, :], score_bank[kt][:, 0:S], decay[:, kt, :],
                                                ALU.mult).then_inc(decayed, 1)
                        dve.wait_ge(decayed, 2 * h + (kt + 1))
                        nc.vector.tensor_scalar(a32[:, kt, :], masked[:, kt, :], -1.0, 1.0, ALU.mult,
                                                ALU.max).then_inc(negated, 1)
                        dve.wait_ge(negated, 2 * h + (kt + 1))
                        nc.vector.tensor_tensor(a32[:, kt, :], masked[:, kt, :], a32[:, kt, :],
                                                ALU.max).then_inc(a_full, 1)
                    for kt in range(2):
                        dve.wait_ge(a_hi, 2 * h + (kt + 1))
                        nc.vector.tensor_tensor(a[:, LO, kt, :], a32[:, kt, :], a[:, HI, kt, :],
                                                ALU.subtract).then_inc(a_ready, 1)

                head(0, True)
                with dve.Fori(1, RH) as h:
                    head(h, False)
                head_stats(RH - 1)
                dve.wait_ge(stats_made, NT * RH)

        with Space(nc, "mix") as s:
            gw = s.sb("gw", [P, 2, EC, E], F32R)
            ow = s.sb("ow", [P, 2, EC, E], F32R)
            gamma_b = s.sb("gamma_b", [P, E])
            beta_b = s.sb("beta_b", [P, E])
            mean = s.sb("mean", [P, NT])
            half = s.sb("half", [P, NT])
            var = s.sb("var", [P, NT])
            apart = s.sb("apart", [P, NT, 2 * RH])
            rstd = s.sb("rstd", [P, NT])
            xs = s.sb("xs", [P, 2, 2, EC, P], F32R)
            y = s.sb("y", [P, 2, E])
            wy = s.sb("wy", [P, 2, E])
            wyT = s.sb("wyT", [P, 2, 2, EC, P], F32R)
            ln_stats = s.sb("ln_stats", [P, 2, 6])
            ln_mean = s.sb("ln_mean", [P, 2])
            ln_half = s.sb("ln_half", [P, 2])
            ln_var = s.sb("ln_var", [P, 2])
            ln_rstd = s.sb("ln_rstd", [P, 2])
            xn = s.sb("xn", [P, 2, E])
            rw_raw = s.sb("rw_raw", [P, EC, W])
            rw = s.sb("rw", [P, 2, EC, W], F32R)
            logits = s.sb("logits", [P, NT, XP + 1])
            top = s.sb("top", [P, NT])
            logitsT = w_raw[:, :, :].rearrange("p c n -> p (c n)")[0:W, :]
            gate_bank = [s.bank(f"gate{k}") for k in range(2)]
            flip_bank = [s.bank(f"flip{k}") for k in range(2)]
            out_bank = [s.bank(f"out{k}") for k in range(2)]
            ln_bank = [s.bank(f"ln{k}") for k in range(2)]
            logit_bank = gate_bank + flip_bank
            w_loaded = s.sem("w_loaded")
            affine_loaded = s.sem("affine_loaded")
            w_hi = s.sem("w_hi")
            w_ready = s.sem("w_ready")
            step = s.sem("step")
            var_ready = s.sem("var_ready")
            rstd_ready = s.sem("rstd_ready")
            xs_loaded = [s.sem(f"xs_loaded{k}") for k in range(2)]
            y_normal = s.sem("y_normal")
            y_scaled = s.sem("y_scaled")
            y_ready = s.sem("y_ready")
            gated = s.sem("gated")
            wy_ready = s.sem("wy_ready")
            flipped = s.sem("flipped")
            wyT_hi = s.sem("wyT_hi")
            wyT_ready = s.sem("wyT_ready")
            out_done = s.sem("out_done")
            added = s.sem("added")
            ln_step = s.sem("ln_step")
            ln_var_ready = s.sem("ln_var_ready")
            ln_rstd_ready = s.sem("ln_rstd_ready")
            xn_ready = s.sem("xn_ready")
            ln_flipped = s.sem("ln_flipped")
            ln_hi = s.sem("ln_hi")
            ln_ready = s.sem("ln_ready")
            row_kept = s.sem("row_kept")
            rows_stored = s.sem("rows_stored")
            rw_loaded = s.sem("rw_loaded")
            rw_hi = s.sem("rw_hi")
            rw_ready = s.sem("rw_ready")
            logit_done = s.sem("logit_done")
            logit_copied = s.sem("logit_copied")
            logit_flipped = s.sem("logit_flipped")
            logits_step = s.sem("logits_step")
            exp_done = s.sem("exp_done")
            block = s.block()

            @block.sync
            def _(sp):
                sp.dma_start(gamma_b[:, :], gamma.rearrange("(a e) -> a e", a=1).to_broadcast([P, E])).then_inc(
                    affine_loaded, 16)
                sp.dma_start(beta_b[:, :], beta.rearrange("(a e) -> a e", a=1).to_broadcast([P, E])).then_inc(
                    affine_loaded, 16)

                def tile_in(t, k):
                    first = t * P
                    if not isinstance(t, int) or t > 1:
                        first = sp.snap(first)
                        sp.wait_ge(gated, t - 1)
                    sp.dma_start(xs[:, k, :, :, :].bitcast(F32), xT[:, :, :, bass.ds(first, P)].bitcast(F32)).then_inc(
                        xs_loaded[k], 16)

                tile_in(0, 0)
                tile_in(1, 1)
                sp.wait_ge(w_ready, 1)
                sp.dma_start(w_raw[:, :, :], out_w.rearrange("(c p) n -> p c n", p=P)).then_inc(w_loaded, 16)
                sp.dma_start(rw_raw[:, :, :], router).then_inc(rw_loaded, 16)

                def store_rows(pair):
                    dst = row_dram.rearrange("(s t p) e -> s p t e", t=2, p=P)[bass.ds(pair, 1), :, :, :]
                    src = rows[:, bass.ds(2 * pair, 2), :]
                    sp.wait_ge(row_kept, 2 * pair + 2)
                    sp.dma_start(dst.rearrange("s p t e -> (s p) t e"), src).then_inc(rows_stored, 16)

                with sp.Fori(1, 3) as m:
                    for k in range(2):
                        tile_in(2 * m + k, k)
                with sp.Fori(3, NT // 2) as m:
                    for k in range(2):
                        tile_in(2 * m + k, k)
                    store_rows(m - 3)
                for pair in range(NT // 2 - 3, NT // 2):
                    store_rows(pair)
                sp.wait_ge(rows_stored, 16 * NT // 2)

            @block.tensor
            def _(pe):
                def gate(m, k):
                    t = 2 * m + k
                    pe.wait_ge(xs_loaded[k], 16 * m + 16)
                    if not isinstance(t, int) or t > 1:
                        pe.wait_ge(wy_ready, t - 1)
                    for c in range(EC):
                        last = matmul3(nc, gate_bank[k][:, :], xs[:, k, HI, c, :], xs[:, k, LO, c, :],
                                       gw[:, HI, c, :], gw[:, LO, c, :], c == 0, c == EC - 1)
                    last.then_inc(gated, 1)

                def flip(t, k):
                    pe.wait_ge(wy_ready, t + 1)
                    if not isinstance(t, int) or t > 1:
                        pe.wait_ge(wyT_ready, t - 1)
                    for c in range(EC):
                        last = nc.tensor.transpose(flip_bank[k][:, c * P:(c + 1) * P], wy[:, k, c * P:(c + 1) * P],
                                                   ident[:, :])
                    last.then_inc(flipped, 1)

                def out(t, k):
                    pe.wait_ge(wyT_ready, t + 1)
                    if not isinstance(t, int) or t > 1:
                        pe.wait_ge(added, t - k)
                    for c in range(EC):
                        last = matmul3(nc, out_bank[k][:, :], wyT[:, k, HI, c, :], wyT[:, k, LO, c, :],
                                       ow[:, HI, c, :], ow[:, LO, c, :], c == 0, c == EC - 1)
                    last.then_inc(out_done, 1)

                def ln_flip(t, k):
                    pe.wait_ge(xn_ready, t + 1)
                    if not isinstance(t, int) or t > 1:
                        pe.wait_ge(ln_ready, t - 1)
                    for c in range(EC):
                        last = nc.tensor.transpose(ln_bank[k][:, c * P:(c + 1) * P], xn[:, k, c * P:(c + 1) * P],
                                                   ident[:, :])
                    last.then_inc(ln_flipped, 1)

                def route_logits(n):
                    pe.wait_ge(ln_ready, 4 * n + 4)
                    cols = slice(n * 512, (n + 1) * 512)
                    for c in range(EC):
                        last = matmul3(nc, logit_bank[n][0:W, :], rw[:, HI, c, :], rw[:, LO, c, :], xT[:, HI, c, cols],
                                       xT[:, LO, c, cols], c == 0, c == EC - 1)
                    last.then_inc(logit_done, 1)

                def round_(m, ln):
                    gate(m, 0)
                    flip(2 * m - 1, 1)
                    out(2 * m - 2, 0)
                    if ln:
                        ln_flip(2 * m - 4, 0)
                    gate(m, 1)
                    flip(2 * m, 0)
                    out(2 * m - 1, 1)
                    if ln:
                        ln_flip(2 * m - 3, 1)

                pe.wait_ge(w_ready, 1)
                gate(0, 0)
                gate(0, 1)
                flip(0, 0)
                pe.wait_ge(w_ready, 2)
                round_(1, False)
                round_(2, True)
                with pe.Fori(3, NT // 2) as m:
                    round_(m, True)
                ln_flip(NT - 4, 0)
                flip(NT - 1, 1)
                out(NT - 2, 0)
                ln_flip(NT - 3, 1)
                out(NT - 1, 1)
                pe.wait_ge(rw_ready, 1)
                for n in range(NB - 1):
                    route_logits(n)
                ln_flip(NT - 2, 0)
                ln_flip(NT - 1, 1)
                route_logits(NB - 1)
                pe.wait_ge(logit_copied, NB)
                pe.wait_ge(added, NT)
                for t in range(NT):
                    last = nc.tensor.transpose(out_bank[0][:, t * W:(t + 1) * W], logitsT[:, t * P:(t + 1) * P],
                                               ident[0:W, 0:W])
                last.then_inc(logit_flipped, 1)

            @block.scalar
            def _(act):
                nc.scalar.preload_act_table(ACT.Exp)
                for n, w in enumerate((gw, ow)):
                    if n == 1:
                        act.wait_ge(w_loaded, 16)
                    nc.scalar.activation(w[:, HI, :, :], w_raw[:, :, :], ACT.Copy).then_inc(w_hi, 1)

                def high(t, k):
                    act.wait_ge(flipped, t + 1)
                    nc.scalar.activation(wyT[:, k, HI, :, :], flip_bank[k][:, :].rearrange(
                        "p (c n) -> p c n", c=EC), ACT.Copy).then_inc(wyT_hi, 1)

                def ln_high(t, k):
                    act.wait_ge(ln_flipped, t + 1)
                    nc.scalar.activation(xT[:, HI, :, bass.ds(t * P, P)], ln_bank[k][:, :].rearrange(
                        "p (c n) -> p c n", c=EC), ACT.Copy).then_inc(ln_hi, 1)

                def keep_row(t, k):
                    act.wait_ge(xn_ready, t + 1)
                    nc.scalar.activation(rows[:, bass.ds(t, 1), :].rearrange("p a e -> p (a e)"),
                                         xn[:, k, :], ACT.Copy).then_inc(row_kept, 1)

                high(0, 0)
                high(1, 1)
                high(2, 0)
                with act.Fori(2, NT // 2) as m:
                    high(2 * m - 1, 1)
                    ln_high(2 * m - 4, 0)
                    keep_row(2 * m - 4, 0)
                    high(2 * m, 0)
                    keep_row(2 * m - 3, 1)
                    ln_high(2 * m - 3, 1)
                ln_high(NT - 4, 0)
                high(NT - 1, 1)
                keep_row(NT - 4, 0)
                ln_high(NT - 3, 1)
                keep_row(NT - 3, 1)

                def copy_logits(n):
                    act.wait_ge(logit_done, n + 1)
                    nc.scalar.activation(logitsT[:, n * 512:(n + 1) * 512], logit_bank[n][0:W, :],
                                         ACT.Copy).then_inc(logit_copied, 1)

                for n in range(NB - 1):
                    copy_logits(n)
                for k in range(2):
                    ln_high(NT - 2 + k, k)
                    keep_row(NT - 2 + k, k)
                copy_logits(NB - 1)
                act.wait_ge(logits_step, 3)
                nc.scalar.activation(exp_logits[:, :, :], exp_logits[:, :, :], ACT.Exp).then_inc(exp_done, 1)
                nc.scalar.activation(exp_gate[:, :], logits[:, :, XP], ACT.Exp, scale=-1.0).then_inc(exp_done, 1)
                act.wait_ge(exp_done, 2)

            @block.vector
            def _(dve):
                dve.wait_ge(w_hi, 1)
                nc.vector.tensor_tensor(gw[:, LO, :, :], w_raw[:, :, :], gw[:, HI, :, :], ALU.subtract).then_inc(
                    w_ready, 1)
                PARTS = 2 * RH
                nc.vector.reduce_sum(mean[:, :], o_stats[:, :, :, 1], AX_X).then_inc(step, 1)
                nc.vector.reduce_sum(var[:, :], o_stats[:, :, :, 2], AX_X).then_inc(step, 1)
                dve.wait_ge(step, 2)
                nc.vector.tensor_scalar(mean[:, :], mean[:, :], 1.0 / PARTS, None, ALU.mult).then_inc(step, 1)
                nc.vector.tensor_scalar(var[:, :], var[:, :], 1.0 / E, GN_EPS, ALU.mult, ALU.add).then_inc(step, 1)
                dve.wait_ge(step, 4)
                nc.vector.tensor_tensor(apart[:, :, :], o_stats[:, :, :, 1],
                                        mean[:, :].unsqueeze(2).to_broadcast([P, NT, PARTS]),
                                        ALU.subtract).then_inc(step, 1)
                dve.wait_ge(step, 5)
                nc.vector.tensor_tensor(apart[:, :, :], apart[:, :, :], apart[:, :, :], ALU.mult).then_inc(step, 1)
                dve.wait_ge(step, 6)
                nc.vector.reduce_sum(half[:, :], apart[:, :, :], AX_X).then_inc(step, 1)
                dve.wait_ge(step, 7)
                nc.vector.scalar_tensor_tensor(var[:, :], half[:, :], 1.0 / PARTS, var[:, :], ALU.mult,
                                               ALU.add).then_inc(var_ready, 1)
                dve.wait_ge(rstd_ready, 1)

                def normal(t, k):
                    if not isinstance(t, int) or t > 1:
                        dve.wait_ge(wy_ready, t - 1)
                    nc.vector.tensor_scalar(y[:, k, :], o[:, bass.ds(t, 1), :].rearrange("p a e -> p (a e)"),
                                            mean[:, bass.ds(t, 1)], rstd[:, bass.ds(t, 1)],
                                            ALU.subtract, ALU.mult).then_inc(y_normal, 1)

                def gate_y(t, k):
                    dve.wait_ge(gated, t + 1)
                    dve.wait_ge(y_ready, t + 1)
                    if not isinstance(t, int) or t > 1:
                        dve.wait_ge(flipped, t - 1)
                    nc.vector.scalar_tensor_tensor(wy[:, k, :], gate_bank[k][:, :], 0.0, y[:, k, :], ALU.max,
                                                   ALU.mult).then_inc(wy_ready, 1)

                def low(t, k):
                    dve.wait_ge(wyT_hi, t + 1)
                    nc.vector.tensor_tensor(wyT[:, k, LO, :, :], flip_bank[k][:, :].rearrange(
                        "p (c n) -> p c n", c=EC), wyT[:, k, HI, :, :], ALU.subtract).then_inc(wyT_ready, 1)

                def add(t, k):
                    dve.wait_ge(out_done, t + 1)
                    rows = x[:, bass.ds(t, 1), :].rearrange("p a e -> p (a e)")
                    nc.vector.tensor_tensor(rows, out_bank[k][:, :], rows, ALU.add).then_inc(added, 1)

                def ln_moments(pair):
                    for k in range(2):
                        if not isinstance(pair, int) or pair > 0:
                            dve.wait_ge(xn_ready, 2 * pair)
                        dve.wait_ge(added, 2 * pair + (k + 1))
                        nc.vector.bn_stats(ln_stats[:, k, :], x[:, bass.ds(2 * pair + k, 1), :].rearrange(
                            "p a e -> p (a e)")).then_inc(ln_step, 1)
                    moments_from_stats(nc, dve, ln_stats[:, :, :], ln_mean[:, :], ln_half[:, :], ln_var[:, :], LN_EPS,
                                       ln_step, 8 * pair + 2, ln_var_ready)

                def ln_normal(t, k):
                    if not isinstance(t, int) or t > 1:
                        dve.wait_ge(ln_flipped, t - 1)
                        dve.wait_ge(row_kept, t - 1)
                    nc.vector.tensor_scalar(xn[:, k, :], x[:, bass.ds(t, 1), :].rearrange("p a e -> p (a e)"),
                                            ln_mean[:, k:k + 1], ln_rstd[:, k:k + 1],
                                            ALU.subtract, ALU.mult).then_inc(xn_ready, 1)

                def ln_low(t, k):
                    dve.wait_ge(ln_hi, t + 1)
                    nc.vector.tensor_tensor(xT[:, LO, :, bass.ds(t * P, P)],
                                            ln_bank[k][:, :].rearrange("p (c n) -> p c n", c=EC),
                                            xT[:, HI, :, bass.ds(t * P, P)], ALU.subtract).then_inc(ln_ready, 1)

                def round_(m, ln, more=True):
                    gate_y(2 * m, 0)
                    if more:
                        normal(2 * m + 2, 0)
                    low(2 * m - 1, 1)
                    if ln:
                        dve.wait_ge(ln_rstd_ready, m - 1)
                        ln_normal(2 * m - 4, 0)
                    add(2 * m - 2, 0)
                    if ln:
                        ln_normal(2 * m - 3, 1)
                    gate_y(2 * m + 1, 1)
                    if more:
                        normal(2 * m + 3, 1)
                    if ln:
                        ln_low(2 * m - 4, 0)
                    low(2 * m, 0)
                    add(2 * m - 1, 1)
                    ln_moments(m - 1)
                    if ln:
                        ln_low(2 * m - 3, 1)

                normal(0, 0)
                normal(1, 1)
                dve.wait_ge(w_hi, 2)
                nc.vector.tensor_tensor(ow[:, LO, :, :], w_raw[:, :, :], ow[:, HI, :, :], ALU.subtract).then_inc(
                    w_ready, 1)
                dve.wait_ge(rw_loaded, 16)
                nc.vector.tensor_copy(rw[:, HI, :, :], rw_raw[:, :, :]).then_inc(rw_hi, 1)
                dve.wait_ge(rw_hi, 1)
                nc.vector.tensor_tensor(rw[:, LO, :, :], rw_raw[:, :, :], rw[:, HI, :, :], ALU.subtract).then_inc(
                    rw_ready, 1)
                gate_y(0, 0)
                normal(2, 0)
                gate_y(1, 1)
                normal(3, 1)
                low(0, 0)
                round_(1, False)
                round_(2, True)
                with dve.Fori(3, NT // 2 - 1) as m:
                    round_(m, True)
                round_(NT // 2 - 1, True, more=False)
                dve.wait_ge(ln_rstd_ready, NT // 2 - 1)
                ln_normal(NT - 4, 0)
                ln_normal(NT - 3, 1)
                low(NT - 1, 1)
                add(NT - 2, 0)
                add(NT - 1, 1)
                ln_moments(NT // 2 - 1)
                ln_low(NT - 4, 0)
                ln_low(NT - 3, 1)
                dve.wait_ge(ln_rstd_ready, NT // 2)
                ln_normal(NT - 2, 0)
                ln_normal(NT - 1, 1)
                ln_low(NT - 2, 0)
                ln_low(NT - 1, 1)
                dve.wait_ge(logit_flipped, 1)
                nc.vector.tensor_copy(logits[:, :, :], out_bank[0][:, :].rearrange(
                    "p (t w) -> p t w", w=W)[:, :, 0:XP + 1]).then_inc(logits_step, 1)
                dve.wait_ge(logits_step, 1)
                nc.vector.tensor_reduce(top[:, :], logits[:, :, 0:XP], AX_X, ALU.max).then_inc(logits_step, 1)
                dve.wait_ge(logits_step, 2)
                nc.vector.tensor_tensor(exp_logits[:, :, :], logits[:, :, 0:XP],
                                        top[:, :].unsqueeze(2).to_broadcast([P, NT, XP]),
                                        ALU.subtract).then_inc(logits_step, 1)

            @block.gpsimd
            def _(pool):
                pool.wait_ge(var_ready, 1)
                nc.gpsimd.tensor_tensor(rstd[:, :], var[:, :], neg_half[:, 0:NT], ALU.pow).then_inc(rstd_ready, 1)
                pool.wait_ge(affine_loaded, 32)

                def affine(t, k):
                    pool.wait_ge(y_normal, t + 1)
                    nc.gpsimd.tensor_tensor(y[:, k, :], y[:, k, :], gamma_b[:, :], ALU.mult).then_inc(y_scaled, 1)
                    pool.wait_ge(y_scaled, t + 1)
                    nc.gpsimd.tensor_tensor(y[:, k, :], y[:, k, :], beta_b[:, :], ALU.add).then_inc(y_ready, 1)

                def inverse_deviation(pair):
                    pool.wait_ge(ln_var_ready, pair + 1)
                    nc.gpsimd.tensor_tensor(ln_rstd[:, :], ln_var[:, :], neg_half[:, 0:2], ALU.pow).then_inc(
                        ln_rstd_ready, 1)

                affine(0, 0)
                affine(1, 1)
                affine(2, 0)
                affine(3, 1)
                with pool.Fori(2, NT // 2) as m:
                    affine(2 * m, 0)
                    affine(2 * m + 1, 1)
                    inverse_deviation(m - 2)
                inverse_deviation(NT // 2 - 2)
                inverse_deviation(NT // 2 - 1)


def experts(nc, x, rows, exp_logits, exp_gate, ident, row_dram, slot_rows, slot_out, w_gate, w_up, w_down, out):
    RANK_STEP = 2
    BATCHES = N // TS
    ROUTE = "routed"
    IT = 3
    R0 = SHARED_STEPS // 2
    R1 = R0 + ROUTED
    C0 = R1 + 2
    O0 = STEPS - BATCHES + 1
    SEED = 1
    LAST = STEPS - 1
    with Space(nc, "moe") as s:
        x_rows = s.sb("x_rows", [P, 2, E])
        g_raw = s.sb("g_raw", [P, EC, WP])
        u_raw = s.sb("u_raw", [P, EC, WP])
        d_raw = s.sb("d_raw", [P, IT, E])
        g_w = s.sb("g_w", [P, 2, EC, WP], F32R)
        u_w = s.sb("u_w", [P, 2, EC, WP], F32R)
        d_w = s.sb("d_w", [P, 2, IT, E], F32R)
        hT = s.sb("hT", [P, 2, EC, TS], F32R)
        silu = s.sb("silu", [P, IT, TS])
        act_full = s.sb("act_full", [P, IT, TS])
        act_w = s.sb("act_w", [P, 2, IT, TS], F32R)
        y = s.sb("y", [P, 2, E])
        got = s.sb("got", [P, 2, TOPK, E])
        top_w = s.sb("top_w", [P, NT, TOPK])
        slot = s.sb("slot", [P, NT, TOPK], U32)
        shared_gate = s.sb("shared_gate", [P, NT])
        expert_of = s.sb("expert_of", [P, ROUTED], I32)
        total = s.sb("total", [P, NT])
        probs = s.sb("probs", [P, NT, XP])
        best = s.sb("best", [P, NT, 8])
        best_at = s.sb("best_at", [P, NT, 8], U32)
        chosen = s.sb("chosen", [P, NT, TOPK])
        top_sum = s.sb("top_sum", [P, NT])
        expert_ids = s.sb("expert_ids", [P, XP])
        onehot = s.sb("onehot", [P, NT, TOPK, XP])
        member = s.sb("member", [P, NT, XP], BF16)
        before = s.sb("before", [P, P], BF16)
        ones = s.sb("ones", [P, P], BF16)
        in_tile = s.sb("in_tile", [P, NT, XP])
        rank = s.sb("rank", [P, NT, XP])
        prior = s.sb("prior", [P, NT, XP])
        count = s.sb("count", [P, XP])
        tile_starts = s.sb("tile_starts", [P, N // TS])
        used = s.sb("used", [P, XP, N // TS])
        tiles = s.sb("tiles", [P, XP])
        one_row = s.sb("one_row", [P, XP])
        tiles_to = s.sb("tiles_to", [P, XP])
        base = s.sb("base", [P, XP])
        place = s.sb("place", [P, NT, XP])
        picked = s.sb("picked", [P, NT, TOPK, XP])
        place_k = s.sb("place_k", [P, NT, TOPK])
        tile_ids = s.sb("tile_ids", [P, ROUTED])
        past = s.sb("past", [P, ROUTED, XP])
        owner = s.sb("owner", [P, ROUTED])
        flip_bank = [s.bank(f"flip{k}") for k in range(2)]
        gate_bank = [s.bank(f"gate{k}") for k in range(2)]
        up_bank = [s.bank(f"up{k}") for k in range(2)]
        down_bank = [s.bank(f"down{k}") for k in range(2)]
        x_loaded = s.sem("x_loaded")
        g_loaded = s.sem("g_loaded")
        u_loaded = s.sem("u_loaded")
        d_loaded = s.sem("d_loaded")
        g_hi = s.sem("g_hi")
        u_hi = s.sem("u_hi")
        d_hi = s.sem("d_hi")
        g_ready = s.sem("g_ready")
        u_ready = s.sem("u_ready")
        d_ready = s.sem("d_ready")
        flipped = s.sem("flipped")
        hT_hi = s.sem("hT_hi")
        hT_ready = s.sem("hT_ready")
        gate_done = s.sem("gate_done")
        up_done = s.sem("up_done")
        silu_ready = s.sem("silu_ready")
        act_ready = s.sem("act_ready")
        act_hi = s.sem("act_hi")
        act_split = s.sem("act_split")
        down_done = s.sem("down_done")
        down_read = s.sem("down_read")
        y_stored = s.sem("y_stored")
        dispatched = s.sem("dispatched")
        fetched = s.sem("fetched")
        gathered = s.sem("gathered")
        out_stored = s.sem("out_stored")
        table_made = s.sem("table_made")
        tables_ready = s.sem("tables_ready")
        member_ready = s.sem("member_ready")
        ranked = s.sem("ranked")
        rank_read = s.sem("rank_read")
        route_step = s.sem("route_step")
        slots_ready = s.sem("slots_ready")
        owners_ready = s.sem("owners_ready")
        block = s.block()

        def phase(n):
            if n < 0 or n >= STEPS:
                return None
            if R0 <= n < R1:
                return ROUTE
            return n // BATCHES if n < R0 else SHARED // 2 + (n - R1) // BATCHES

        def start(part):
            return part * BATCHES if part < SHARED // 2 else R1 + (part - SHARED // 2) * BATCHES

        def fresh(before, this):
            return this is not None and (this == ROUTE or this != before)

        def load_index(n, this):
            if this == ROUTE:
                return n - (R0 - SHARED // 2)
            return this if this < SHARED // 2 else this + ROUTED

        def width(this):
            return WI if this == ROUTE else min(WP, WS - this * WP)

        def inner_tiles(this):
            return [(it, min(P, width(this) - it * P)) for it in range(-(-width(this) // P))]

        def runs(eng, body, own=lambda n: None):
            traits = [(tuple(phase(n + d) for d in (-2, -1, 0, 1)), own(n)) for n in range(STEPS)]
            first = 0
            while first < STEPS:
                to = first + 1
                while to < STEPS and traits[to] == traits[first]:
                    to += 1
                if to == first + 1:
                    body(first, *traits[first])
                else:
                    with eng.Fori(first, to) as n:
                        body(n, *traits[first])
                first = to

        def inner(bank_pair, it, rows_of):
            return bank_pair[it // 2][0:rows_of, (it % 2) * TS:(it % 2 + 1) * TS]

        def both(bank_pair, buf, this):
            views = [(bank_pair[0][:, :], buf[:, 0:2, :].rearrange("p i n -> p (i n)"))]
            for it, k in inner_tiles(this)[2:]:
                views.append((bank_pair[1][0:k, 0:TS], buf[0:k, it, :]))
            return views

        def halves(this):
            return [(slice(0, P), slice(0, 2))] + [(slice(0, k), it) for it, k in inner_tiles(this)[2:]]

        @block.sync
        def _(sp):
            def load_x(n, this):
                if not isinstance(n, int) or n > 0:
                    sp.wait_ge(flipped, n)
                if this == ROUTE:
                    src = slot_rows.rearrange("(s t p) e -> s p t e", t=2, p=P)[bass.ds(n - R0, 1), :, :, :]
                else:
                    src = row_dram.rearrange("(s t p) e -> s p t e", t=2, p=P)[bass.ds(n - start(this), 1), :, :, :]
                sp.dma_start(x_rows[:, :, :], src.rearrange("s p t e -> (s p) t e")).then_inc(x_loaded, 16)

            def expert(n, this):
                return sp.value_load(expert_of[0:1, bass.ds(n - R0, 1)], min_val=0, max_val=XP - 1)

            def load_w(n, this, e, w, raw, loaded, ready):
                i = load_index(n, this)
                if not isinstance(i, int) or i > 0:
                    sp.wait_ge(ready, i)
                routed, shared = w
                if raw is d_raw:
                    part = slice(0, len(inner_tiles(this))), slice(0, E)
                else:
                    part = slice(0, EC), slice(0, width(this))
                src = routed[bass.ds(e, 1), :, part[0], part[1]].rearrange("x p c n -> (x p) c n") \
                    if this == ROUTE else shared[this, :, part[0], part[1]]
                sp.dma_start(raw[:, part[0], part[1]], src).then_inc(loaded, 16)

            def store_y(n):
                dst = slot_out.rearrange("(s t p) e -> s p t e", t=2, p=P)[bass.ds(n - R0, 1), :, :, :]
                sp.wait_ge(down_read, n + 1)
                sp.dma_start(dst.rearrange("s p t e -> (s p) t e"), y[:, :, :]).then_inc(y_stored, 16)

            def store_out(pair):
                dst = out.rearrange("b (t p) e -> b p t e", p=P)[bass.ds(pair, 1), :, :, :]
                src = x[:, bass.ds(2 * pair, 2), :]
                sp.wait_ge(down_read, pair + O0)
                sp.wait_ge(gathered, SEED + TOPK * 2 * (pair + 1))
                sp.dma_start(dst.rearrange("b p t e -> (b p) t e"), src).then_inc(out_stored, 16)

            def step(n, phases, own):
                _, before, this, after = phases
                if isinstance(n, int) and n == R0 - 1:
                    sp.wait_ge(owners_ready, 1)
                    sp.wait_ge(dispatched, 16 * NT * TOPK)
                e = expert(n + 1, after) if after == ROUTE else None
                if after is not None:
                    load_x(n + 1, after)
                if fresh(this, after):
                    load_w(n + 1, after, e, w_gate, g_raw, g_loaded, g_ready)
                    load_w(n + 1, after, e, w_up, u_raw, u_loaded, u_ready)
                if fresh(before, this):
                    e = expert(n, this) if this == ROUTE else None
                    load_w(n, this, e, w_down, d_raw, d_loaded, d_ready)
                if own == "results":
                    store_y(n - 2)
                if own == "output":
                    store_out(n - (O0 + 2))

            load_x(0, 0)
            load_w(0, 0, None, w_gate, g_raw, g_loaded, g_ready)
            load_w(0, 0, None, w_up, u_raw, u_loaded, u_ready)
            runs(sp, step, lambda n: "results" if R0 <= n - 2 < R1 else "output" if n >= O0 + 2 else None)
            for pair in range(STEPS - (O0 + 2), BATCHES):
                store_out(pair)
            sp.wait_ge(out_stored, 16 * BATCHES)

        @block.gpsimd
        def _(pool):
            nc.gpsimd.memset(before[:, :], 1.0).then_inc(table_made, 1)
            nc.gpsimd.memset(ones[:, :], 1.0).then_inc(tables_ready, 1)
            nc.gpsimd.memset(one_row[:, :], 1.0).then_inc(tables_ready, 1)
            pool.wait_ge(table_made, 1)
            nc.gpsimd.affine_select(out=before[:, :], in_=before[:, :], compare_op=ALU.is_gt, fill=0.0, base=0,
                                    pattern=[[1, P]], channel_multiplier=-1).then_inc(tables_ready, 1)
            for table, step_by in ((expert_ids, 1), (tile_starts, TS), (tile_ids, 1)):
                nc.gpsimd.iota(table[:, :], pattern=[[step_by, table.shape[1]]], base=0, channel_multiplier=0,
                               allow_small_or_imprecise_dtypes=True).then_inc(tables_ready, 1)
            pool.wait_ge(slots_ready, 1)
            for t in range(NT):
                for k in range(TOPK):
                    nc.gpsimd.indirect_dma_start(
                        out=slot_rows, out_offset=bass.IndirectOffsetOnAxis(ap=slot[:, t, k:k + 1], axis=0),
                        in_=rows[:, t, :], in_offset=None).then_inc(dispatched, 16)
            pool.wait_ge(dispatched, 16 * NT * TOPK)
            pool.wait_ge(y_stored, 16 * ROUTED)
            for t in range(NT):
                if t > 0:
                    pool.wait_ge(fetched, 16 * TOPK * t)
                if t > 1:
                    pool.wait_ge(gathered, SEED + TOPK * (t - 1))
                for k in range(TOPK):
                    nc.gpsimd.indirect_dma_start(
                        out=got[:, t % 2, k, :], out_offset=None, in_=slot_out,
                        in_offset=bass.IndirectOffsetOnAxis(ap=slot[:, t, k:k + 1], axis=0)).then_inc(fetched, 16)

        @block.tensor
        def _(pe):
            def flip(n):
                pe.wait_ge(x_loaded, 16 * n + 16)
                if not isinstance(n, int) or n > 0:
                    pe.wait_ge(hT_ready, n)
                for tile in range(2):
                    for c in range(EC):
                        bank, col = flip_bank[c // 2], (c % 2) * TS + tile * P
                        last = nc.tensor.transpose(bank[:, col:col + P], x_rows[:, tile, c * P:(c + 1) * P],
                                                   ident[:, :])
                last.then_inc(flipped, 1)

            def widen(n, this, w, w_ready, banks, banks_read, done):
                pe.wait_ge(hT_ready, n + 1)
                pe.wait_ge(w_ready, load_index(n, this) + 1)
                if not isinstance(n, int) or n > 0:
                    pe.wait_ge(banks_read, n)
                for it, k in inner_tiles(this):
                    cols = slice(it * P, it * P + k)
                    for c in range(EC):
                        last = matmul3(nc, inner(banks, it, k), w[:, HI, c, cols], w[:, LO, c, cols],
                                       hT[:, HI, c, :], hT[:, LO, c, :], c == 0, c == EC - 1)
                last.then_inc(done, 1)

            def narrow(n, this):
                pe.wait_ge(act_split, n + 1)
                pe.wait_ge(d_ready, load_index(n, this) + 1)
                if not isinstance(n, int) or n > 0:
                    pe.wait_ge(down_read, n)
                its = inner_tiles(this)
                for tile in range(2):
                    toks = slice(tile * P, (tile + 1) * P)
                    for it, k in its:
                        last = matmul3(nc, down_bank[tile][:, :], act_w[0:k, HI, it, toks], act_w[0:k, LO, it, toks],
                                       d_w[0:k, HI, it, :], d_w[0:k, LO, it, :], it == 0, it == len(its) - 1)
                last.then_inc(down_done, 1)

            def count_tokens():
                m = member[:, :, :].rearrange("p t e -> p (t e)")
                pe.wait_ge(member_ready, 1)
                pe.wait_ge(tables_ready, 6)
                pe.wait_ge(hT_ready, RANK_STEP + 1)
                nc.tensor.matmul(flip_bank[0][:, 0:NT * XP], before[:, :], m, start=True, stop=True)
                nc.tensor.matmul(flip_bank[0][:, NT * XP:2 * NT * XP], ones[:, :], m, start=True,
                                 stop=True).then_inc(ranked, 1)
                pe.wait_ge(rank_read, 1)

            def step(n, phases, counting):
                _, before, this, after = phases
                widen(n, this, g_w, g_ready, gate_bank, silu_ready, gate_done)
                widen(n, this, u_w, u_ready, up_bank, act_ready, up_done)
                if counting:
                    count_tokens()
                if after is not None:
                    flip(n + 1)
                if before is not None:
                    narrow(n - 1, before)

            flip(0)
            runs(pe, step, lambda n: n == RANK_STEP)
            narrow(LAST, phase(LAST))

        @block.scalar
        def _(act):
            nc.scalar.preload_act_table(ACT.Silu)

            def weights_high(n, this, loaded, raw, w, users, hi):
                act.wait_ge(loaded, load_index(n, this) * 16 + 16)
                if not isinstance(n, int) or n > 0:
                    act.wait_ge(users, n)
                if raw is d_raw:
                    its = len(inner_tiles(this))
                    nc.scalar.activation(w[:, HI, 0:its, :], raw[:, 0:its, :], ACT.Copy).then_inc(hi, 1)
                else:
                    cols = width(this)
                    nc.scalar.activation(w[:, HI, :, 0:cols], raw[:, :, 0:cols], ACT.Copy).then_inc(hi, 1)

            def hT_high(n):
                act.wait_ge(flipped, n + 1)
                for k in range(2):
                    last = nc.scalar.activation(hT[:, HI, 2 * k:2 * k + 2, :].rearrange("p c n -> p (c n)"),
                                                flip_bank[k][:, :], ACT.Copy)
                last.then_inc(hT_hi, 1)

            def act_high(n, this):
                act.wait_ge(act_ready, n + 1)
                if not isinstance(n, int) or n > 0:
                    act.wait_ge(down_done, n)
                for k, it in halves(this):
                    last = nc.scalar.activation(act_w[k, HI, it, :], act_full[k, it, :], ACT.Copy)
                last.then_inc(act_hi, 1)

            def silus(n, this):
                act.wait_ge(gate_done, n + 1)
                if not isinstance(n, int) or n > 0:
                    act.wait_ge(act_ready, n)
                for src, dst in both(gate_bank, silu, this):
                    last = nc.scalar.activation(dst, src, ACT.Silu)
                last.then_inc(silu_ready, 1)

            def results(n):
                act.wait_ge(down_done, n + 1)
                if not isinstance(n, int) or n > R0:
                    act.wait_ge(y_stored, 16 * (n - R0))
                nc.scalar.activation(y[:, 0, :], down_bank[0][:, :], ACT.Copy)
                nc.scalar.activation(y[:, 1, :], down_bank[1][:, :], ACT.Copy).then_inc(down_read, 1)

            def step(n, phases, own):
                before2, before, this, after = phases
                if before is not None:
                    act_high(n - 1, before)
                if fresh(before2, before):
                    weights_high(n - 1, before, d_loaded, d_raw, d_w, down_done, d_hi)
                silus(n, this)
                if fresh(this, after):
                    weights_high(n + 1, after, g_loaded, g_raw, g_w, gate_done, g_hi)
                if after is not None:
                    hT_high(n + 1)
                if fresh(this, after):
                    weights_high(n + 1, after, u_loaded, u_raw, u_w, up_done, u_hi)
                if before == ROUTE:
                    results(n - 1)

            weights_high(0, 0, g_loaded, g_raw, g_w, gate_done, g_hi)
            hT_high(0)
            weights_high(0, 0, u_loaded, u_raw, u_w, up_done, u_hi)
            runs(act, step)
            act_high(LAST, phase(LAST))

        @block.vector
        def _(dve):
            def weights_low(n, this, raw, w, hi, ready):
                dve.wait_ge(hi, load_index(n, this) + 1)
                if raw is d_raw:
                    part = slice(0, len(inner_tiles(this))), slice(0, E)
                else:
                    part = slice(0, EC), slice(0, width(this))
                nc.vector.tensor_tensor(w[:, LO, part[0], part[1]], raw[:, part[0], part[1]],
                                        w[:, HI, part[0], part[1]], ALU.subtract).then_inc(ready, 1)

            def hT_low(n):
                dve.wait_ge(hT_hi, n + 1)
                for k in range(2):
                    last = nc.vector.tensor_tensor(hT[:, LO, 2 * k:2 * k + 2, :].rearrange("p c n -> p (c n)"),
                                                   flip_bank[k][:, :],
                                                   hT[:, HI, 2 * k:2 * k + 2, :].rearrange("p c n -> p (c n)"),
                                                   ALU.subtract)
                last.then_inc(hT_ready, 1)

            def products(n, this):
                dve.wait_ge(silu_ready, n + 1)
                dve.wait_ge(up_done, n + 1)
                if not isinstance(n, int) or n > 0:
                    dve.wait_ge(act_split, n)
                for (src, full), (_, other) in zip(both(up_bank, act_full, this), both(up_bank, silu, this)):
                    last = nc.vector.tensor_tensor(full, src, other, ALU.mult)
                last.then_inc(act_ready, 1)

            def act_low(n, this):
                dve.wait_ge(act_hi, n + 1)
                for k, it in halves(this):
                    last = nc.vector.tensor_tensor(act_w[k, LO, it, :], act_full[k, it, :], act_w[k, HI, it, :],
                                                   ALU.subtract)
                last.then_inc(act_split, 1)

            def add_shared(n, this):
                dve.wait_ge(down_done, n + 1)
                for tile in range(2):
                    t = (n - start(this)) * 2 + tile
                    rows_of = x[:, bass.ds(t, 1), :].rearrange("p a e -> p (a e)")
                    last = nc.vector.scalar_tensor_tensor(rows_of, down_bank[tile][:, :],
                                                          shared_gate[:, bass.ds(t, 1)], rows_of, ALU.mult, ALU.add)
                last.then_inc(down_read, 1)

            def add_routed(t):
                dve.wait_ge(fetched, t * (16 * TOPK) + 16 * TOPK)
                rows_of = x[:, bass.ds(t, 1), :].rearrange("p a e -> p (a e)")
                for j in range(TOPK):
                    dve.wait_ge(gathered, TOPK * t + (j + SEED))
                    nc.vector.scalar_tensor_tensor(
                        rows_of, got[:, bass.ds(t % 2, 1), j, :].rearrange("p a e -> p (a e)"),
                        top_w[:, bass.ds(t, 1), j:j + 1].rearrange("p a j -> p (a j)"),
                        rows_of, ALU.mult, ALU.add).then_inc(gathered, 1)

            steps = [0]

            def chain(instruction):
                steps[0] += 1
                instruction.then_inc(route_step, 1)
                dve.wait_ge(route_step, steps[0])

            v = nc.vector

            def choose():
                chain(v.reduce_sum(total[:, :], exp_logits[:, :, :], AX_X))
                chain(v.reciprocal(total[:, :], total[:, :]))
                chain(v.tensor_tensor(probs[:, :, :], exp_logits[:, :, :],
                                      total[:, :].unsqueeze(2).to_broadcast([P, NT, XP]), ALU.mult))
                for t in range(NT):
                    ins = v.max(best[:, t, :], probs[:, t, :])
                chain(ins)
                chain(v.tensor_scalar(shared_gate[:, :], exp_gate[:, :], 1.0, None, ALU.add))
                chain(v.reciprocal(shared_gate[:, :], shared_gate[:, :]))

            def name_chosen():
                for t in range(NT):
                    ins = v.max_index(best_at[:, t, :], best[:, t, :], probs[:, t, :])
                chain(ins)
                chain(v.tensor_copy(chosen[:, :, :], best_at[:, :, 0:TOPK]))
                dve.wait_ge(tables_ready, 6)
                chain(v.tensor_tensor(onehot[:, :, :, :],
                                      chosen[:, :, :].unsqueeze(3).to_broadcast([P, NT, TOPK, XP]),
                                      expert_ids[:, :].unsqueeze(1).unsqueeze(1).to_broadcast([P, NT, TOPK, XP]),
                                      ALU.is_equal))
                with nc.allow_low_precision(reason="zeros and ones"):
                    v.reduce_sum(member[:, :, :], onehot[:, :, :, :].rearrange("p t k e -> p t e k"),
                                 AX_X).then_inc(member_ready, 1)

            def read_counts():
                dve.wait_ge(ranked, 1)
                v.tensor_copy(rank[:, :, :], flip_bank[0][:, 0:NT * XP].rearrange("p (t e) -> p t e", e=XP))
                v.tensor_copy(in_tile[:, :, :], flip_bank[0][:, NT * XP:2 * NT * XP].rearrange(
                    "p (t e) -> p t e", e=XP)).then_inc(rank_read, 1)
                dve.wait_ge(rank_read, 1)

            def count_prior():
                chain(v.memset(prior[:, 0, :], 0.0))
                for t in range(1, NT):
                    chain(v.tensor_tensor(prior[:, t, :], prior[:, t - 1, :], in_tile[:, t - 1, :], ALU.add))
                chain(v.tensor_tensor(count[:, :], prior[:, NT - 1, :], in_tile[:, NT - 1, :], ALU.add))

            def lay_out():
                chain(v.tensor_tensor(used[:, :, :], count[:, :].unsqueeze(2).to_broadcast([P, XP, N // TS]),
                                      tile_starts[:, :].unsqueeze(1).to_broadcast([P, XP, N // TS]), ALU.is_gt))
                chain(v.reduce_sum(tiles[:, :], used[:, :, :], AX_X))
                chain(v.tensor_tensor_scan(tiles_to[:, :], one_row[:, :], tiles[:, :], 0.0, ALU.mult, ALU.add))
                chain(v.tensor_tensor(base[:, :], tiles_to[:, :], tiles[:, :], ALU.subtract))
                chain(v.tensor_scalar(base[:, :], base[:, :], float(TS), None, ALU.mult))
                chain(v.tensor_tensor(place[:, :, :], rank[:, :, :], prior[:, :, :], ALU.add))
                chain(v.tensor_tensor(place[:, :, :], place[:, :, :],
                                      base[:, :].unsqueeze(1).to_broadcast([P, NT, XP]), ALU.add))

            def place_tokens():
                chain(v.tensor_tensor(picked[:, :, :, :], onehot[:, :, :, :],
                                      place[:, :, :].unsqueeze(2).to_broadcast([P, NT, TOPK, XP]), ALU.mult))
                chain(v.reduce_sum(place_k[:, :, :], picked[:, :, :, :], AX_X))
                v.tensor_copy(slot[:, :, :], place_k[:, :, :]).then_inc(slots_ready, 1)

            def name_owners():
                chain(v.tensor_tensor(past[:, :, :], tiles_to[:, :].unsqueeze(1).to_broadcast([P, ROUTED, XP]),
                                      tile_ids[:, :].unsqueeze(2).to_broadcast([P, ROUTED, XP]), ALU.is_le))
                chain(v.reduce_sum(owner[:, :], past[:, :, :], AX_X))
                chain(v.tensor_scalar(owner[:, :], owner[:, :], float(XP - 1), None, ALU.min))
                v.tensor_copy(expert_of[:, :], owner[:, :]).then_inc(owners_ready, 1)
                chain(v.reduce_sum(top_sum[:, :], best[:, :, 0:TOPK], AX_X))
                chain(v.tensor_scalar(top_sum[:, :], top_sum[:, :], 1e-9, None, ALU.max))
                chain(v.reciprocal(top_sum[:, :], top_sum[:, :]))
                chain(v.tensor_tensor(top_w[:, :, :], best[:, :, 0:TOPK],
                                      top_sum[:, :].unsqueeze(2).to_broadcast([P, NT, TOPK]), ALU.mult))

            routing = {0: choose, 1: name_chosen, 2: count_prior, 3: lay_out, 4: place_tokens, 5: name_owners}

            def step(n, phases, own):
                before2, before, this, after = phases
                if before is not None:
                    act_low(n - 1, before)
                if fresh(before2, before):
                    weights_low(n - 1, before, d_raw, d_w, d_hi, d_ready)
                if fresh(this, after):
                    weights_low(n + 1, after, g_raw, g_w, g_hi, g_ready)
                if own == RANK_STEP:
                    read_counts()
                products(n, this)
                if after is not None:
                    hT_low(n + 1)
                if fresh(this, after):
                    weights_low(n + 1, after, u_raw, u_w, u_hi, u_ready)
                if own == "gathered":
                    t = n - C0
                    dve.wait_ge(down_read, n - 1)
                    add_routed(t)
                    dve.wait_ge(gathered, TOPK * t + (TOPK + SEED))
                if before not in (None, ROUTE):
                    add_shared(n - 1, before)
                if own in routing:
                    routing[own]()

            dve.sem_inc(gathered, SEED)
            weights_low(0, 0, g_raw, g_w, g_hi, g_ready)
            hT_low(0)
            weights_low(0, 0, u_raw, u_w, u_hi, u_ready)
            runs(dve, step, lambda n: n if n in routing else "gathered" if n >= C0 else None)
            act_low(LAST, phase(LAST))
            dve.wait_ge(down_read, LAST)
            for t in range(STEPS - C0, NT):
                add_routed(t)
            dve.wait_ge(gathered, SEED + TOPK * NT)
            add_shared(LAST, phase(LAST))


def program(nc, ins, out, stop=9):
    xt_dram = nc.dram_tensor("xt_scratch", [B, P, 2, EC, S], F32, kind="Internal").ap()
    row_dram = nc.dram_tensor("row_scratch", [N, E], F32, kind="Internal").ap()
    slot_rows = nc.dram_tensor("slot_rows", [SLOTS, E], F32, kind="Internal").ap()
    slot_out = nc.dram_tensor("slot_out", [ROUTED * TS, E], F32, kind="Internal").ap()
    with Space(nc, "all") as top:
        ident = top.sb("ident", [P, P])
        neg_half = top.sb("neg_half", [P, NT])
        x = top.sb("x", [P, NT, E])
        stats = top.sb("stats", [P, NT, 6])
        make_constants(nc, top, ident, neg_half)
        with Space(nc, "weights") as keep:
            w_raw = keep.sb("w_raw", [P, 2, EC * HG * P])
            w = keep.sb("w", [P, 4, 2, EC * HG * P], F32R)
            with Space(nc, "ln1buf") as s:
                xT = s.sb("xT", [P, 2, EC, N], F32R)
                layernorm_transpose(nc, "ln1", x, stats, xT, ident, neg_half, x_dram=ins["x"], xt_dram=xt_dram,
                                    first_weights=(w, w_raw, ins["wqkv"], ins["wo"]))
            attention(nc, x, stats, w, w_raw, ident, neg_half, xt_dram, ins["wqkv"], ins["wo"], ins["q_scale"],
                      ins["k_scale"], slot_rows)
        if stop >= 2:
            rows = top.sb("rows", [P, NT, E])
            exp_logits = top.sb("exp_logits", [P, NT, XP])
            exp_gate = top.sb("exp_gate", [P, NT])
            with Space(nc, "ln2buf") as s:
                xT = s.sb("xT", [P, 2, EC, N], F32R)
                layernorm_transpose(nc, "ln2", x, stats, xT, ident, neg_half)
                retention(nc, x, xT, rows, ident, neg_half, ins["ctxT"], ins["head_w"], ins["decayT"],
                          ins["gate_w"], ins["out_w"], ins["gamma"], ins["beta"], ins["router"], row_dram,
                          exp_logits, exp_gate)
        if stop >= 3:
            experts(nc, x, rows, exp_logits, exp_gate, ident, row_dram, slot_rows, slot_out,
                    (ins["w_gate"], ins["sh_gate"]), (ins["w_up"], ins["sh_up"]), (ins["w_down"], ins["sh_down"]),
                    out)
        if stop <= 2:
            with Space(nc, "store") as s:
                stored = s.sem("stored")
                block = s.block()

                @block.sync
                def _(sp):
                    sp.dma_start(out.rearrange("b (t p) e -> p (b t) e", p=P), x[:, :, :]).then_inc(stored, 16)
                    sp.wait_ge(stored, 16)


def decay_masks():
    heads = E // P
    gam = 1.0 - 2.0 ** (-5.0 - np.arange(heads))
    d = np.arange(S)[:, None] - np.arange(S)[None, :]
    m = np.where(d >= 0, gam[:, None, None] ** (-d[None].astype(float)), 0.0)
    m = m / np.sqrt(m.sum(axis=-1, keepdims=True)).transpose(0, 2, 1) / np.sqrt(P)
    return np.ascontiguousarray(m.transpose(0, 2, 1).reshape(heads, 2, P, S).transpose(0, 2, 1, 3)).astype(np.float32)


def kernel(stop=9, **inputs):
    from concourse import bacc
    from concourse.bass_utils import run_bass_kernel_spmd

    a = {k: np.ascontiguousarray(v) for k, v in inputs.items()}
    qkv = np.stack([a[f"L0_attn_w{c}"].reshape(EC, P, G, HG * P) for c in "qkv"])
    def wide(w):
        return np.ascontiguousarray(w.reshape(-1, EC, P, w.shape[-1]).transpose(0, 2, 1, 3))

    def deep(w):
        padded = np.zeros((w.shape[0], WP, E), np.float32)
        padded[:, :w.shape[1]] = w
        return np.ascontiguousarray(padded.reshape(-1, 3, P, E).transpose(0, 2, 1, 3))

    def parts(w):
        padded = np.zeros((E, SHARED * WP), np.float32)
        padded[:, :WS] = w
        return np.ascontiguousarray(padded.reshape(E, SHARED, WP).transpose(1, 0, 2))

    down = np.zeros((SHARED * WP, E), np.float32)
    down[:WS] = a["L0_ffn_sh_down"]
    router = np.zeros((P, EC, W), np.float32)
    router[:, :, :XP] = a["L0_ffn_router_w"].reshape(XP, EC, P).transpose(2, 1, 0)
    router[:, :, XP] = a["L0_ffn_sh_gate_w"].reshape(EC, P).T
    arrays = {
        "x": a["x"],
        "wqkv": np.ascontiguousarray(qkv.transpose(3, 0, 2, 1, 4)).reshape(G, 3, P, EC * HG * P),
        "wo": a["L0_attn_wo"].reshape(G, HG, P, E),
        "q_scale": a["L0_attn_q_scale"],
        "k_scale": a["L0_attn_k_scale"],
        "ctxT": np.ascontiguousarray(a["ctx_2048"].reshape(N, EC, P).transpose(1, 2, 0)),
        "head_w": a["L0_xattn_Wh"],
        "decayT": decay_masks(),
        "gate_w": a["L0_xattn_wg_w"],
        "out_w": a["L0_xattn_wo_w"],
        "gamma": a["L0_xattn_gn_gamma"],
        "beta": a["L0_xattn_gn_beta"],
        "router": router,
        "w_gate": wide(a["L0_ffn_w_gate"]),
        "w_up": wide(a["L0_ffn_w_up"]),
        "w_down": deep(a["L0_ffn_w_down"]),
        "sh_gate": wide(parts(a["L0_ffn_sh_gate"])),
        "sh_up": wide(parts(a["L0_ffn_sh_up"])),
        "sh_down": deep(down.reshape(SHARED, WP, E)),
    }
    nc = bacc.Bacc("TRN2", target_bir_lowering=False, num_devices=1)
    ins = {k: nc.dram_tensor(f"in_{k}", v.shape, mybir.dt.from_np(v.dtype), kind="ExternalInput").ap()
           for k, v in arrays.items()}
    out = nc.dram_tensor("out", [B, S, E], F32, kind="ExternalOutput").ap()
    program(nc, ins, out, stop)
    r = run_bass_kernel_spmd(nc, [{f"in_{k}": v for k, v in arrays.items()}], core_ids=[0])
    return r.results[0]["out"]
```

```python
from contextlib import ExitStack

import concourse.bass as bass
from concourse import mybir
import numpy as np

F32 = mybir.dt.float32
F32R = mybir.dt.float32r
BF16 = mybir.dt.bfloat16
I32 = mybir.dt.int32
U32 = mybir.dt.uint32
ALU = mybir.AluOpType
ACT = mybir.ActivationFunctionType
AX_X = mybir.AxisListType.X

P = 128
B, S, E = 8, 256, 512
N = B * S
NT = N // P
EC = E // P
H = 16
HG = 4
G = H // HG
LN_EPS = 1e-5
RMS_EPS = 1e-6
XP = 16
TOPK = 4
W = 32
WI = 352
SHARED = 4
WS = 1408
WP = 3 * P
TS = 256
ROUTED = N * TOPK // TS + XP - 1
SLOTS = N * TOPK + XP * TS
SHARED_STEPS = SHARED * (N // TS)
STEPS = SHARED_STEPS + ROUTED
ZERO_ROWS = 4
CLEARS = SLOTS // (P * ZERO_ROWS)
HI, LO = 0, 1


class Space:

    def __init__(self, nc, prefix):
        self.nc, self.prefix, self.ctx = nc, prefix, ExitStack()

    def __enter__(self):
        return self

    def __exit__(self, *a):
        return self.ctx.__exit__(*a)

    def sb(self, name, shape, dt=F32):
        return self.ctx.enter_context(self.nc.sbuf_tensor(f"{self.prefix}_{name}", shape, dt))

    def bank(self, name, shape=(P, 512), dt=F32):
        return self.ctx.enter_context(self.nc.psum_tensor(f"{self.prefix}_{name}", list(shape), dt))

    def sem(self, name):
        return self.ctx.enter_context(self.nc.semaphore(f"{self.prefix}_{name}"))

    def block(self):
        return self.ctx.enter_context(self.nc.Block())


def matmul3(nc, out, a_hi, a_lo, b_hi, b_lo, start, stop):
    nc.tensor.matmul(out, a_hi, b_lo, start=start, stop=False)
    nc.tensor.matmul(out, a_lo, b_hi, start=False, stop=False)
    return nc.tensor.matmul(out, a_hi, b_hi, start=False, stop=stop)


def make_constants(nc, ident, neg_half):
    with Space(nc, "const") as s:
        done = s.sem("done")
        block = s.block()

        @block.gpsimd
        def _(pool):
            nc.gpsimd.memset(ident[:, :], 0.0).then_inc(done, 1)
            pool.wait_ge(done, 1)
            nc.gpsimd.affine_select(out=ident[:, :], in_=ident[:, :], compare_op=ALU.not_equal, fill=1.0,
                                    base=0, pattern=[[-1, P]], channel_multiplier=1).then_inc(done, 1)
            nc.gpsimd.memset(neg_half[:, :], -0.5).then_inc(done, 1)
            pool.wait_ge(done, 3)


def moments_from_stats(nc, dve, stats, mean, half, var, eps, step, base, done):
    if not isinstance(base, int) or base > 0:
        dve.wait_ge(step, base)
    nc.vector.tensor_tensor(mean, stats[:, :, 1], stats[:, :, 4], ALU.add).then_inc(step, 1)
    nc.vector.tensor_tensor(half, stats[:, :, 1], stats[:, :, 4], ALU.subtract).then_inc(step, 1)
    nc.vector.tensor_tensor(var, stats[:, :, 2], stats[:, :, 5], ALU.add).then_inc(step, 1)
    dve.wait_ge(step, base + 3)
    nc.vector.tensor_scalar(mean, mean, 0.5, None, ALU.mult).then_inc(step, 1)
    nc.vector.tensor_scalar(var, var, 1.0 / E, eps, ALU.mult, ALU.add).then_inc(step, 1)
    nc.vector.scalar_tensor_tensor(half, half, 0.25, half, ALU.mult, ALU.mult).then_inc(step, 1)
    dve.wait_ge(step, base + 6)
    nc.vector.tensor_tensor(var, var, half, ALU.add).then_inc(done, 1)


def first_layernorm(nc, x, stats, xT, xt, w, w_raw, ident, neg_half, x_dram, xt_dram, wqkv):
    PARTS = 4
    PT = NT // PARTS
    with Space(nc, "ln1") as s:
        mean = s.sb("mean", [P, NT])
        half = s.sb("half", [P, NT])
        var = s.sb("var", [P, NT])
        rstd = s.sb("rstd", [P, NT])
        xn = s.sb("xn", [P, 2, E])
        flip = [s.bank(f"flip{k}") for k in range(2)]
        loaded = [s.sem(f"loaded{q}") for q in range(PARTS)]
        step = s.sem("step")
        var_ready = s.sem("var_ready")
        rstd_ready = s.sem("rstd_ready")
        xn_ready = s.sem("xn_ready")
        flipped = s.sem("flipped")
        hi_ready = s.sem("hi_ready")
        lo_ready = s.sem("lo_ready")
        stored = s.sem("stored")
        first_kept = s.sem("first_kept")
        raw_loaded = [s.sem(f"raw_loaded{k}") for k in range(2)]
        w_hi = s.sem("w_hi")
        w_ready = s.sem("w_ready")
        block = s.block()

        @block.sync
        def _(sp):
            xv = x_dram.rearrange("b (t p) e -> p (b t) e", p=P)
            for q in range(PARTS):
                sp.dma_start(x[:, q * PT:(q + 1) * PT, :], xv[:, q * PT:(q + 1) * PT, :]).then_inc(loaded[q], 16)
            for c in range(2):
                sp.dma_start(w_raw[:, c, :], wqkv[0, c, :, :]).then_inc(raw_loaded[c], 16)
            sp.wait_ge(lo_ready, 2)
            sp.dma_start(xt[:, :, :, :].bitcast(F32), xT[:, :, :, 0:S].bitcast(F32)).then_inc(first_kept, 16)
            with sp.Fori(0, B) as b:
                sp.wait_ge(lo_ready, 2 * b + 2)
                for part in (HI, LO):
                    sp.dma_start(xt_dram[bass.ds(b, 1), :, part, :, :].rearrange("b p c s -> (b p) c s"),
                                 xT[:, part, :, bass.ds(b * S, S)].bitcast(F32)).then_inc(stored, 16)
            sp.wait_ge(first_kept, 16)
            sp.wait_ge(stored, 16 * 2 * B)

        @block.vector
        def _(dve):
            def moments(q):
                tiles = slice(q * PT, (q + 1) * PT)
                dve.wait_ge(loaded[q], 16)
                with dve.Fori(q * PT, (q + 1) * PT) as t:
                    nc.vector.bn_stats(stats[:, bass.ds(t, 1), :].rearrange("p a s -> p (a s)"),
                                       x[:, bass.ds(t, 1), :].rearrange("p a e -> p (a e)")).then_inc(step, 1)
                moments_from_stats(nc, dve, stats[:, tiles, :], mean[:, tiles], half[:, tiles], var[:, tiles], LN_EPS,
                                   step, (PT + 6) * q + PT, var_ready)

            def split_lo(c):
                dve.wait_ge(w_hi, c + 1)
                nc.vector.tensor_tensor(w[:, c, LO, :], w_raw[:, c, :], w[:, c, HI, :],
                                        ALU.subtract).then_inc(w_ready, 1)

            def normalise(t, k):
                if not isinstance(t, int) or t > 1:
                    dve.wait_ge(flipped, t - 1)
                nc.vector.tensor_scalar(xn[:, k, :], x[:, bass.ds(t, 1), :].rearrange("p a e -> p (a e)"),
                                        mean[:, bass.ds(t, 1)], rstd[:, bass.ds(t, 1)],
                                        ALU.subtract, ALU.mult).then_inc(xn_ready, 1)

            def low(t, k):
                dve.wait_ge(hi_ready, t + 1)
                nc.vector.tensor_tensor(xT[:, LO, :, bass.ds(t * P, P)],
                                        flip[k][:, :].rearrange("p (c n) -> p c n", c=EC),
                                        xT[:, HI, :, bass.ds(t * P, P)], ALU.subtract).then_inc(lo_ready, 1)

            def pairs(first, to):
                with dve.Fori(first, to) as m:
                    for k in range(2):
                        normalise(2 * m + k, k)
                        low(2 * m + (k - 2), k)

            moments(0)
            dve.wait_ge(rstd_ready, 1)
            normalise(0, 0)
            normalise(1, 1)
            pairs(1, PT // 2)
            for q in range(1, PARTS):
                moments(q)
                dve.wait_ge(rstd_ready, q + 1)
                pairs(q * PT // 2, (q + 1) * PT // 2)
            low(NT - 2, 0)
            low(NT - 1, 1)
            split_lo(0)
            split_lo(1)

        @block.gpsimd
        def _(pool):
            for q in range(PARTS):
                tiles = slice(q * PT, (q + 1) * PT)
                pool.wait_ge(var_ready, q + 1)
                nc.gpsimd.tensor_tensor(rstd[:, tiles], var[:, tiles], neg_half[:, 0:PT], ALU.pow).then_inc(
                    rstd_ready, 1)

        @block.tensor
        def _(pe):
            def flips(t, k):
                pe.wait_ge(xn_ready, t + 1)
                if not isinstance(t, int):
                    pe.wait_ge(lo_ready, t - 1)
                for c in range(EC):
                    last = nc.tensor.transpose(flip[k][:, c * P:(c + 1) * P], xn[:, k, c * P:(c + 1) * P],
                                               ident[:, :])
                last.then_inc(flipped, 1)

            flips(0, 0)
            flips(1, 1)
            with pe.Fori(1, NT // 2) as m:
                for k in range(2):
                    flips(2 * m + k, k)

        @block.scalar
        def _(act):
            nc.scalar.preload_act_table(ACT.Exp)
            with act.Fori(0, NT // 2) as m:
                for k in range(2):
                    act.wait_ge(flipped, 2 * m + (k + 1))
                    nc.scalar.activation(xT[:, HI, :, bass.ds(m * (2 * P) + k * P, P)],
                                         flip[k][:, :].rearrange("p (c n) -> p c n", c=EC),
                                         ACT.Copy).then_inc(hi_ready, 1)
            for c in range(2):
                act.wait_ge(raw_loaded[c], 16)
                nc.scalar.activation(w[:, c, HI, :], w_raw[:, c, :], ACT.Copy).then_inc(w_hi, 1)


def attention(nc, x, stats, xt, w, w_raw, ident, neg_half, xt_dram, wqkv, wo, q_scale, k_scale, slot_rows):
    AHEAD = 2
    QUARTERS = 4
    D = P
    QK = 4
    with Space(nc, "attn") as s:
        squares = s.sb("squares", [P, 2, HG, D + 1])
        sums = s.sb("sums", [P, QK, HG])
        rms = s.sb("rms", [P, QK, HG])
        qk = s.sb("qk", [P, QK, HG * D])
        v = s.sb("v", [P, 2, 2, HG * D], F32R)
        qT = s.sb("qT", [P, HG, 2, S], F32R)
        kT = s.sb("kT", [P, HG, 2, S], F32R)
        scale_in = s.sb("scale_in", [P, 2])
        scale = s.sb("scale", [P, 1])
        neg_max = s.sb("neg_max", [P, HG, 2])
        row_sum = s.sb("row_sum", [P, HG, 2])
        inv_sum = s.sb("inv_sum", [P, HG, 2])
        probs = s.sb("probs", [P, 2, 2, S])
        pT = s.sb("pT", [P, 2, 2, 2, S], F32R)
        oT = s.sb("oT", [P, HG, 2, S], F32R)
        bank = [s.bank(f"bank{k}") for k in range(8)]
        proj_bank = bank[0:2]
        score_bank = bank[2:4]
        pT_bank = bank[4]
        oT_bank = bank[5]
        flip_bank = [bank[2], bank[3], bank[6], bank[7]]
        out_bank = [bank[4], bank[6]]

        xt_loaded = s.sem("xt_loaded")
        raw_loaded = [s.sem(f"raw_loaded{k}") for k in range(2)]
        w_hi = s.sem("w_hi")
        w_ready = s.sem("w_ready")
        scales_loaded = s.sem("scales_loaded")
        scale_ready = s.sem("scale_ready")
        ones_ready = s.sem("ones_ready")
        projected = s.sem("projected")
        squared = s.sem("squared")
        summed = s.sem("summed")
        rms_ready = s.sem("rms_ready")
        qk_ready = s.sem("qk_ready")
        v_hi = s.sem("v_hi")
        v_ready = s.sem("v_ready")
        flipped = s.sem("flipped")
        qkT_hi = s.sem("qkT_hi")
        qkT_ready = s.sem("qkT_ready")
        scored = s.sem("scored")
        max_ready = s.sem("max_ready")
        exp_ready = s.sem("exp_ready")
        inv_ready = s.sem("inv_ready")
        probs_ready = s.sem("probs_ready")
        p_flipped = s.sem("p_flipped")
        pT_hi = s.sem("pT_hi")
        pT_ready = s.sem("pT_ready")
        o_done = s.sem("o_done")
        oT_hi = s.sem("oT_hi")
        oT_ready = s.sem("oT_ready")
        out_done = s.sem("out_done")
        added = s.sem("added")
        stats_made = s.sem("stats_made")
        zeros = s.sb("zeros", [P, ZERO_ROWS * E])
        zeros_ready = s.sem("zeros_ready")
        slots_cleared = s.sem("slots_cleared")
        block = s.block()

        def rounds(eng, first, body, between=None):
            first()
            body(0, 0, 0)
            with eng.Fori(0, G - 1) as g:
                with eng.Fori(1, B - 2) as b:
                    body(g * B + b, b, g)
                body(g * B + (B - 2), B - 2, g, refill="qk")
                body(g * B + (B - 1), B - 1, g, refill="v")
                body(g * B + B, 0, g + 1, refill="o")
            if between is not None:
                between()
            with eng.Fori(1, B - 1) as b:
                body(b + (G - 1) * B, b, G - 1, last=True)
            body(G * B - 1, B - 1, G - 1, more=False, last=True)

        def quarters(g, c):
            return (4 * g + (c + AHEAD)) * QUARTERS

        def refills(refill, place):
            if refill in ("v", "o"):
                return [({"v": 2, "o": 3}[refill], place)] if place < QUARTERS else []
            if refill == "qk":
                return {4: [(0, 0)], 5: [(0, 1), (0, 2)], 6: [(0, 3), (1, 0)], 7: [(1, 1), (1, 2)],
                        8: [(1, 3)]}.get(place, [])
            return []

        @block.sync
        def _(sp):
            def load_raw(g, c):
                if not isinstance(g, int):
                    sp.wait_ge(w_ready, quarters(g, c - 1))
                if c < 3:
                    src = wqkv[bass.ds(g + 1, 1), c, :, :].rearrange("g p n -> (g p) n")
                    sp.dma_start(w_raw[:, c, :], src).then_inc(raw_loaded[c % 2], 16)
                else:
                    src = wo[bass.ds(g + 1, 1), :, :, :].rearrange("g h d e -> d (g h) e")
                    sp.dma_start(w_raw[:, c, :].rearrange("p (h e) -> p h e", h=HG),
                                 src).then_inc(raw_loaded[c % 2], 16)

            def load_xt(j, b):
                sp.wait_ge(projected, 6 * j)
                sp.dma_start(xt[:, :, :, :].bitcast(F32), xt_dram[bass.ds(b, 1), :, :, :, :].rearrange(
                    "b p l c s -> (b p) l c s")).then_inc(xt_loaded, 16)

            def clear(n):
                sp.dma_start(slot_rows.rearrange("(n p r) e -> n p (r e)", p=P, r=ZERO_ROWS)[bass.ds(n, 1), :, :]
                             .rearrange("n p f -> (n p) f"), zeros[:, :]).then_inc(slots_cleared, 16)

            sp.dma_start(scale_in[:, 0:1], q_scale.rearrange("(p a) -> p a", a=1)).then_inc(scales_loaded, 16)
            sp.dma_start(scale_in[:, 1:2], k_scale.rearrange("(p a) -> p a", a=1)).then_inc(scales_loaded, 16)
            load_raw(-1, 2)
            load_raw(-1, 3)
            sp.wait_ge(zeros_ready, 1)
            with sp.Fori(0, G - 1) as g:
                load_xt(g * B + 1, 1)
                clear(g * B)
                load_raw(g, 0)
                load_raw(g, 1)
                with sp.Fori(1, B - 1) as b:
                    load_xt(g * B + b + 1, b + 1)
                    clear(g * B + b)
                load_raw(g, 2)
                load_xt(g * B + B, 0)
                clear(g * B + (B - 1))
                load_raw(g, 3)
            with sp.Fori(0, B - 1) as b:
                load_xt(b + ((G - 1) * B + 1), b + 1)
            sp.wait_ge(slots_cleared, 16 * CLEARS)

        @block.tensor
        def _(pe):
            def project(j, n, g=None):
                c, tile = ((n % 2, n // 2) if n < QK else (2, n - QK))
                if n == 0 and (not isinstance(j, int) or j > 0):
                    pe.wait_ge(xt_loaded, 16 * j)
                if isinstance(j, int) and j == 0 and n == QK:
                    pe.wait_ge(w_ready, QUARTERS)
                if g is not None and n in (0, 1, 4):
                    pe.wait_ge(w_ready, quarters(g, c + 1))
                if n >= 2:
                    pe.wait_ge(qk_ready, QK * j + (n - 1))
                elif not isinstance(j, int) or j > 0:
                    pe.wait_ge(v_ready, 2 * j + (n - 1))
                for e in range(EC):
                    cols = slice(e * HG * D, (e + 1) * HG * D)
                    toks = slice(tile * P, tile * P + P)
                    last = matmul3(nc, proj_bank[n % 2][:, :], xt[:, HI, e, toks], xt[:, LO, e, toks],
                                   w[:, c, HI, cols], w[:, c, LO, cols], e == 0, e == EC - 1)
                last.then_inc(projected, 1)

            def flip(j):
                pe.wait_ge(qk_ready, QK * j + QK)
                if not isinstance(j, int) or j > 0:
                    pe.wait_ge(exp_ready, HG * j)
                    pe.wait_ge(added, 2 * j - 2 + AHEAD)
                for u in range(HG):
                    for c in range(2):
                        for tile in range(2):
                            last = nc.tensor.transpose(flip_bank[u][:, (2 * c + tile) * P:(2 * c + tile + 1) * P],
                                                       qk[:, 2 * tile + c, u * D:(u + 1) * D], ident[:, :])
                    last.then_inc(flipped, 1)

            def score(i, u):
                pe.wait_ge(qkT_ready, HG * i + (u + 1))
                if u >= 2:
                    pe.wait_ge(exp_ready, HG * i + (u - 1))
                for tile in range(2):
                    toks = slice(tile * P, tile * P + P)
                    last = matmul3(nc, score_bank[u % 2][:, tile * S:(tile + 1) * S], qT[:, u, HI, toks],
                                   qT[:, u, LO, toks], kT[:, u, HI, :], kT[:, u, LO, :], True, True)
                last.then_inc(scored, 1)

            def flip_probs(i, u):
                pe.wait_ge(probs_ready, HG * i + (u + 1))
                if u == 0:
                    pe.wait_ge(added, 2 * i + AHEAD)
                else:
                    pe.wait_ge(pT_ready, HG * i + u)
                for kt in range(2):
                    for tile in range(2):
                        last = nc.tensor.transpose(pT_bank[:, kt * S + tile * P:kt * S + (tile + 1) * P],
                                                   probs[:, u % 2, tile, kt * P:(kt + 1) * P], ident[:, :])
                last.then_inc(p_flipped, 1)

            def weigh(i, u):
                pe.wait_ge(pT_ready, HG * i + (u + 1))
                if u == 0:
                    pe.wait_ge(v_ready, 2 * i + 2)
                else:
                    pe.wait_ge(oT_ready, HG * i + u)
                for kt in range(2):
                    last = matmul3(nc, oT_bank[:, 0:S], v[:, kt, HI, u * D:(u + 1) * D],
                                   v[:, kt, LO, u * D:(u + 1) * D], pT[:, u % 2, HI, kt, :],
                                   pT[:, u % 2, LO, kt, :], kt == 0, kt == 1)
                last.then_inc(o_done, 1)

            def output(i, g, more):
                pe.wait_ge(oT_ready, HG * i + HG)
                pe.wait_ge(w_ready, quarters(g, 0))
                for tile in range(2):
                    if tile == 1 and more:
                        pe.wait_ge(qkT_ready, HG * i + (HG + 3))
                    for u in range(HG):
                        toks = slice(tile * P, tile * P + P)
                        cols = slice(u * E, (u + 1) * E)
                        last = matmul3(nc, out_bank[tile][:, :], oT[:, u, HI, toks], oT[:, u, LO, toks],
                                       w[:, 3, HI, cols], w[:, 3, LO, cols], u == 0, u == HG - 1)
                    last.then_inc(out_done, 1)

            def body(i, b, g, more=True, refill=None, last=False):
                j = i + 1
                new = g if refill == "v" else None
                score(i, 0)
                if more:
                    project(j, 0, new)
                score(i, 1)
                if more:
                    project(j, 1, new)
                flip_probs(i, 0)
                score(i, 2)
                if more:
                    project(j, 2, new)
                weigh(i, 0)
                flip_probs(i, 1)
                score(i, 3)
                if more:
                    project(j, 3, new)
                weigh(i, 1)
                flip_probs(i, 2)
                if more:
                    project(j, 4, new)
                weigh(i, 2)
                flip_probs(i, 3)
                if more:
                    project(j, 5, new)
                weigh(i, 3)
                if more:
                    flip(j)
                output(i, g, more)

            def first():
                for n in range(6):
                    project(0, n)
                flip(0)

            rounds(pe, first, body)

        @block.scalar
        def _(act):
            def split_hi(g, c, q):
                act.wait_ge(raw_loaded[c % 2], 32 * g + 16 * (c // 2 + 2))
                if isinstance(g, int) and g < 0:
                    pass
                elif c < 3:
                    act.wait_ge(projected, 6 * B * g + (6 * (B - 1) + (3, 4, 6)[c]))
                else:
                    act.wait_ge(out_done, 2 * B * g + 2 * B)
                part = slice(q * HG * D, (q + 1) * HG * D)
                nc.scalar.activation(w[:, c, HI, part], w_raw[:, c, part], ACT.Copy).then_inc(w_hi, 1)

            def split_some(g, refill, place):
                for c, q in refills(refill, place):
                    split_hi(g - 1 if refill == "o" else g, c, q)

            def square(j, n):
                act.wait_ge(projected, 6 * j + (n + 1))
                if not (isinstance(j, int) and j == 0 and n < 2):
                    act.wait_ge(summed, QK * j + (n - 1))
                nc.scalar.activation(squares[:, n % 2, :, 0:D],
                                     proj_bank[n % 2][:, :].rearrange("p (h d) -> p h d", h=HG),
                                     ACT.Square).then_inc(squared, 1)

            def v_high(j, tile):
                act.wait_ge(projected, 6 * j + (QK + tile + 1))
                if not isinstance(j, int) or j > 0:
                    act.wait_ge(o_done, HG * j)
                nc.scalar.activation(v[:, tile, HI, :], proj_bank[tile][:, :], ACT.Copy).then_inc(v_hi, 1)

            def qkT_high(j, u):
                act.wait_ge(flipped, HG * j + (u + 1))
                nc.scalar.activation(qT[:, u, HI, :], flip_bank[u][:, 0:S], ACT.Copy, scale=scale[:, 0:1])
                nc.scalar.activation(kT[:, u, HI, :], flip_bank[u][:, S:2 * S], ACT.Copy).then_inc(qkT_hi, 1)

            def exponentials(i, u):
                act.wait_ge(max_ready, HG * i + (u + 1))
                if u >= 2:
                    act.wait_ge(p_flipped, HG * i + (u - 1))
                for tile in range(2):
                    last = nc.scalar.activation(probs[:, u % 2, tile, :], score_bank[u % 2][:, tile * S:(tile + 1) * S],
                                                ACT.Exp, bias=neg_max[:, u, tile:tile + 1],
                                                accum_out=row_sum[:, u, tile:tile + 1])
                last.then_inc(exp_ready, 1)

            def pT_high(i, u):
                act.wait_ge(p_flipped, HG * i + (u + 1))
                nc.scalar.activation(pT[:, u % 2, HI, :, :].rearrange("p k s -> p (k s)"), pT_bank[:, :],
                                     ACT.Copy).then_inc(pT_hi, 1)

            def oT_high(i, u):
                act.wait_ge(o_done, HG * i + (u + 1))
                nc.scalar.activation(oT[:, u, HI, :], oT_bank[:, 0:S], ACT.Copy).then_inc(oT_hi, 1)

            def body(i, b, g, more=True, refill=None, last=False):
                j = i + 1
                exponentials(i, 0)
                if more:
                    square(j, 0)
                split_some(g, refill, 0)
                exponentials(i, 1)
                if more:
                    square(j, 1)
                split_some(g, refill, 1)
                pT_high(i, 0)
                exponentials(i, 2)
                if more:
                    square(j, 2)
                split_some(g, refill, 2)
                oT_high(i, 0)
                pT_high(i, 1)
                split_some(g, refill, 3)
                exponentials(i, 3)
                if more:
                    square(j, 3)
                split_some(g, refill, 4)
                oT_high(i, 1)
                split_some(g, refill, 5)
                pT_high(i, 2)
                oT_high(i, 2)
                split_some(g, refill, 6)
                pT_high(i, 3)
                oT_high(i, 3)
                split_some(g, refill, 7)
                if more:
                    for u in range(HG):
                        qkT_high(j, u)
                    v_high(j, 0)
                    v_high(j, 1)
                split_some(g, refill, 8)

            def first():
                act.wait_ge(ones_ready, 1)
                act.wait_ge(scale_ready, 1)
                for n in range(QK):
                    square(0, n)
                    if n == 1:
                        for q in range(QUARTERS):
                            split_hi(-1, 2, q)
                v_high(0, 0)
                v_high(0, 1)
                for u in range(HG):
                    qkT_high(0, u)
                for q in range(QUARTERS):
                    split_hi(-1, 3, q)

            rounds(act, first, body)

        @block.vector
        def _(dve):
            def split_lo(g, c, q):
                dve.wait_ge(w_hi, quarters(g, c) + (q + 1))
                part = slice(q * HG * D, (q + 1) * HG * D)
                nc.vector.tensor_tensor(w[:, c, LO, part], w_raw[:, c, part], w[:, c, HI, part],
                                        ALU.subtract).then_inc(w_ready, 1)

            def split_some(g, refill, place):
                for c, q in refills(refill, place):
                    split_lo(g - 1 if refill == "o" else g, c, q)

            def sum_squares(j, n):
                dve.wait_ge(squared, QK * j + (n + 1))
                nc.vector.reduce_sum(sums[:, n, :], squares[:, n % 2, :, :], AX_X).then_inc(summed, 1)

            def scale_rows(j, n):
                dve.wait_ge(rms_ready, QK * j + (n + 1))
                nc.vector.tensor_tensor(qk[:, n, :].rearrange("p (h d) -> p h d", h=HG),
                                        proj_bank[n % 2][:, :].rearrange("p (h d) -> p h d", h=HG),
                                        rms[:, n, :].unsqueeze(2).to_broadcast([P, HG, D]),
                                        ALU.mult).then_inc(qk_ready, 1)

            def v_low(j, tile):
                dve.wait_ge(v_hi, 2 * j + (tile + 1))
                nc.vector.tensor_tensor(v[:, tile, LO, :], proj_bank[tile][:, :], v[:, tile, HI, :],
                                        ALU.subtract).then_inc(v_ready, 1)

            def qkT_low(j, u):
                dve.wait_ge(qkT_hi, HG * j + (u + 1))
                nc.vector.scalar_tensor_tensor(qT[:, u, LO, :], flip_bank[u][:, 0:S], scale[:, 0:1],
                                               qT[:, u, HI, :], ALU.mult, ALU.subtract)
                nc.vector.tensor_tensor(kT[:, u, LO, :], flip_bank[u][:, S:2 * S], kT[:, u, HI, :],
                                        ALU.subtract).then_inc(qkT_ready, 1)

            def maxima(i, u):
                dve.wait_ge(scored, HG * i + (u + 1))
                nc.vector.tensor_reduce(neg_max[:, u, :], score_bank[u % 2][:, :].rearrange("p (t k) -> p t k", t=2),
                                        AX_X, ALU.max, negate=True).then_inc(max_ready, 1)

            def invert_sums(i, u):
                dve.wait_ge(exp_ready, HG * i + (u + 1))
                nc.vector.reciprocal(inv_sum[:, u, :], row_sum[:, u, :]).then_inc(inv_ready, 1)

            def pT_low(i, u):
                dve.wait_ge(pT_hi, HG * i + (u + 1))
                nc.vector.tensor_tensor(pT[:, u % 2, LO, :, :].rearrange("p k s -> p (k s)"), pT_bank[:, :],
                                        pT[:, u % 2, HI, :, :].rearrange("p k s -> p (k s)"),
                                        ALU.subtract).then_inc(pT_ready, 1)

            def oT_low(i, u):
                dve.wait_ge(oT_hi, HG * i + (u + 1))
                nc.vector.tensor_tensor(oT[:, u, LO, :], oT_bank[:, 0:S], oT[:, u, HI, :],
                                        ALU.subtract).then_inc(oT_ready, 1)

            def add_output(i, b, tile):
                dve.wait_ge(out_done, 2 * i + (tile + 1))
                rows = x[:, bass.ds(b * 2 + tile, 1), :].rearrange("p a e -> p (a e)")
                nc.vector.tensor_tensor(rows, out_bank[tile][:, :], rows, ALU.add).then_inc(added, 1)

            def body(i, b, g, more=True, refill=None, last=False):
                j = i + 1
                maxima(i, 0)
                if more:
                    sum_squares(j, 0)
                invert_sums(i, 0)
                maxima(i, 1)
                if more:
                    scale_rows(j, 0)
                split_some(g, refill, 0)
                if more:
                    sum_squares(j, 1)
                invert_sums(i, 1)
                pT_low(i, 0)
                split_some(g, refill, 1)
                maxima(i, 2)
                if more:
                    scale_rows(j, 1)
                    sum_squares(j, 2)
                split_some(g, refill, 2)
                invert_sums(i, 2)
                oT_low(i, 0)
                pT_low(i, 1)
                split_some(g, refill, 3)
                maxima(i, 3)
                if more:
                    scale_rows(j, 2)
                    sum_squares(j, 3)
                invert_sums(i, 3)
                split_some(g, refill, 4)
                oT_low(i, 1)
                if more:
                    scale_rows(j, 3)
                split_some(g, refill, 5)
                pT_low(i, 2)
                oT_low(i, 2)
                split_some(g, refill, 6)
                pT_low(i, 3)
                oT_low(i, 3)
                split_some(g, refill, 7)
                if more:
                    for u in range(HG):
                        qkT_low(j, u)
                    v_low(j, 0)
                    v_low(j, 1)
                split_some(g, refill, 8)
                add_output(i, b, 0)
                add_output(i, b, 1)
                if last:
                    final_stats(i, b)

            def final_stats(i, b):
                for tile in range(2):
                    dve.wait_ge(added, i * 2 + (tile + 1 + AHEAD))
                    nc.vector.bn_stats(stats[:, bass.ds(b * 2 + tile, 1), :].rearrange("p a s -> p (a s)"),
                                       x[:, bass.ds(b * 2 + tile, 1), :].rearrange("p a e -> p (a e)")).then_inc(
                        stats_made, 1)

            def first():
                nc.vector.memset(squares[:, :, :, D:D + 1], RMS_EPS * D).then_inc(ones_ready, 1)
                dve.wait_ge(scales_loaded, 32)
                nc.vector.tensor_scalar(scale[:, :], scale_in[:, 0:1], scale_in[:, 1:2], float(D), ALU.mult,
                                        ALU.mult).then_inc(scale_ready, 1)
                dve.sem_inc(added, AHEAD)
                dve.wait_ge(ones_ready, 1)
                for n in range(QK):
                    sum_squares(0, n)
                    scale_rows(0, n)
                    if n == 1:
                        for q in range(QUARTERS):
                            split_lo(-1, 2, q)
                v_low(0, 0)
                v_low(0, 1)
                for u in range(HG):
                    qkT_low(0, u)
                for q in range(QUARTERS):
                    split_lo(-1, 3, q)

            rounds(dve, first, body, lambda: final_stats((G - 1) * B, 0))
            dve.wait_ge(stats_made, NT)

        @block.gpsimd
        def _(pool):
            def inverse_rms(j, n):
                pool.wait_ge(summed, QK * j + (n + 1))
                nc.gpsimd.tensor_tensor(rms[:, n, :], sums[:, n, :], neg_half[:, 0:HG], ALU.pow).then_inc(rms_ready, 1)

            def normalise(i, u):
                pool.wait_ge(inv_ready, HG * i + (u + 1))
                nc.gpsimd.tensor_tensor(probs[:, u % 2, :, :], probs[:, u % 2, :, :],
                                        inv_sum[:, u, :].unsqueeze(2).to_broadcast([P, 2, S]),
                                        ALU.mult).then_inc(probs_ready, 1)

            def body(i, b, g, more=True, refill=None, last=False):
                for u in range(HG):
                    if more:
                        inverse_rms(i + 1, u)
                    normalise(i, u)

            def first():
                nc.gpsimd.memset(zeros[:, :], 0.0).then_inc(zeros_ready, 1)
                for n in range(QK):
                    inverse_rms(0, n)

            rounds(pool, first, body)


def retention(nc, x, stats, xT, o, ident, neg_half, ctxT, head_w, decayT, gate_w, out_w, gamma, beta, router, xt_dram,
              exp_logits, exp_gate):
    RH = E // P
    NB = N // 512
    GN_EPS = 1e-3
    rows = o
    with Space(nc, "ret") as keep:
        w_raw = keep.sb("w_raw", [P, EC, E])
        o_stats = keep.sb("o_stats", [P, NT, 2 * RH, 3])
        with Space(nc, "heads") as s:
            ctx_raw = w_raw[:, 0:2, :]
            ctx = s.sb("ctx", [P, 2, 2, 512], F32R)
            hw_raw = s.sb("hw_raw", [P, P])
            hw = s.sb("hw", [P, 2, P], F32R)
            decay = s.sb("decay", [P, 2, S])
            k_full = w_raw[:, 2:4, :]
            kT = s.sb("kT", [P, 2, N], F32R)
            qT = s.sb("qT", [P, 2, N], F32R)
            v = s.sb("v", [P, 2, 2, B, P], F32R)
            masked = k_full[:, 0, :].rearrange("p (t s) -> p t s", t=2)
            a32 = k_full[:, 1, :].rearrange("p (t s) -> p t s", t=2)
            a = s.sb("a", [P, 2, 2, S], F32R)
            ln_mean = s.sb("ln_mean", [P, NT])
            ln_half = s.sb("ln_half", [P, NT])
            ln_var = s.sb("ln_var", [P, NT])
            ln_rstd = s.sb("ln_rstd", [P, NT])
            xn = s.sb("xn", [P, 2, E])
            bank = [s.bank(f"bank{k}") for k in range(8)]
            ln_bank = bank[4:6]
            k_bank = bank[0:2]
            v_bank = bank[2:4]
            q_bank = [bank[4], bank[5], bank[4], bank[5]]
            score_bank = bank[6:8]
            o_bank = [bank[0], bank[1], bank[2], bank[3]]
            ctx_loaded = [s.sem(f"ctx_loaded{k}") for k in range(2)]
            head_loaded = s.sem("head_loaded")
            ctx_hi = s.sem("ctx_hi")
            ctx_ready = s.sem("ctx_ready")
            hw_hi = s.sem("hw_hi")
            hw_ready = s.sem("hw_ready")
            k_done = s.sem("k_done")
            k_full_ready = s.sem("k_full_ready")
            k_hi = s.sem("k_hi")
            k_ready = s.sem("k_ready")
            q_done = s.sem("q_done")
            q_hi = s.sem("q_hi")
            q_ready = s.sem("q_ready")
            v_flipped = s.sem("v_flipped")
            v_hi = s.sem("v_hi")
            v_ready = s.sem("v_ready")
            scored = s.sem("scored")
            decayed = s.sem("decayed")
            negated = s.sem("negated")
            a_full = s.sem("a_full")
            a_hi = s.sem("a_hi")
            a_ready = s.sem("a_ready")
            o_done = s.sem("o_done")
            o_read = s.sem("o_read")
            stats_made = s.sem("stats_made")
            gate_w_loaded = s.sem("gate_w_loaded")
            ln_step = s.sem("ln_step")
            ln_var_ready = s.sem("ln_var_ready")
            ln_rstd_ready = s.sem("ln_rstd_ready")
            xn_ready = s.sem("xn_ready")
            ln_flipped = s.sem("ln_flipped")
            ln_hi = s.sem("ln_hi")
            ln_ready = s.sem("ln_ready")
            block = s.block()

            @block.sync
            def _(sp):
                def load_head(h, first):
                    if not first:
                        sp.wait_ge(decayed, 2 * h)
                    sp.dma_start(hw_raw[:, :], head_w[bass.ds(h, 1), :, :].rearrange("h d e -> (h d) e")).then_inc(
                        head_loaded, 16)
                    sp.dma_start(decay[:, :, :], decayT[bass.ds(h, 1), :, :, :].rearrange(
                        "h p t s -> (h p) t s")).then_inc(head_loaded, 16)
                    for n in range(NB):
                        if n >= 2:
                            sp.wait_ge(ctx_ready, NB * h + (n - 1))
                        sp.dma_start(ctx_raw[:, n % 2, :], ctxT[bass.ds(h, 1), :, n * 512:(n + 1) * 512].rearrange(
                            "h d n -> (h d) n")).then_inc(ctx_loaded[n % 2], 16)

                load_head(0, True)
                with sp.Fori(1, RH) as h:
                    load_head(h, False)
                sp.wait_ge(ctx_ready, NB * RH)
                sp.wait_ge(a_ready, 2 * RH)
                sp.dma_start(w_raw[:, :, :], gate_w.rearrange("(c p) n -> p c n", p=P)).then_inc(gate_w_loaded, 16)
                sp.wait_ge(gate_w_loaded, 16)

            @block.tensor
            def _(pe):
                def ln_flips():
                    def flip(t, k):
                        pe.wait_ge(xn_ready, t + 1)
                        if not isinstance(t, int):
                            pe.wait_ge(ln_ready, t - 1)
                        for c in range(EC):
                            last = nc.tensor.transpose(ln_bank[k][:, c * P:(c + 1) * P], xn[:, k, c * P:(c + 1) * P],
                                                       ident[:, :])
                        last.then_inc(ln_flipped, 1)

                    flip(0, 0)
                    flip(1, 1)
                    with pe.Fori(1, NT // 2) as m:
                        for k in range(2):
                            flip(2 * m + k, k)
                    pe.wait_ge(ln_ready, NT)

                def head(h, first):
                    def keys(n):
                        if n == 0:
                            pe.wait_ge(hw_ready, h + 1)
                            if not first:
                                pe.wait_ge(o_read, 4 * h)
                        if n >= 2:
                            pe.wait_ge(k_ready, NB * h + (n - 1))
                        pe.wait_ge(ctx_ready, NB * h + (n + 1))
                        matmul3(nc, k_bank[n % 2][:, :], hw[:, HI, :], hw[:, LO, :], ctx[:, n % 2, HI, :],
                                ctx[:, n % 2, LO, :], True, True).then_inc(k_done, 1)

                    def values(n):
                        pe.wait_ge(k_full_ready, NB * h + (n + 1))
                        if n >= 2:
                            pe.wait_ge(v_ready, NB * h + (n - 1))
                        for q in range(4):
                            last = nc.tensor.transpose(v_bank[n % 2][:, q * P:(q + 1) * P],
                                                       k_full[:, n % 2, q * P:(q + 1) * P], ident[:, :])
                        last.then_inc(v_flipped, 1)

                    def queries(n):
                        if n >= 2:
                            pe.wait_ge(q_ready, NB * h + (n - 1))
                        cols = slice(n * 512, (n + 1) * 512)
                        matmul3(nc, q_bank[n][:, :], hw[:, HI, :], hw[:, LO, :],
                                xT[:, HI, bass.ds(h, 1), cols].rearrange("p a n -> p (a n)"),
                                xT[:, LO, bass.ds(h, 1), cols].rearrange("p a n -> p (a n)"),
                                True, True).then_inc(q_done, 1)

                    def scores(n):
                        pe.wait_ge(k_ready, NB * h + (n + 1))
                        pe.wait_ge(q_ready, NB * h + (n + 1))
                        for kt in range(2):
                            for b in (2 * n, 2 * n + 1):
                                keys_of = slice(b * S + kt * P, b * S + (kt + 1) * P)
                                queries_of = slice(b * S, (b + 1) * S)
                                last = matmul3(nc, score_bank[kt][:, 0:S], kT[:, HI, keys_of], kT[:, LO, keys_of],
                                               qT[:, HI, queries_of], qT[:, LO, queries_of], b == 0, b == B - 1)
                            if n == NB - 1:
                                last.then_inc(scored, 1)

                    keys(0)
                    keys(1)
                    if first:
                        ln_flips()
                    queries(0)
                    values(0)
                    keys(2)
                    queries(1)
                    values(1)
                    scores(0)
                    keys(3)
                    queries(2)
                    values(2)
                    scores(1)
                    queries(3)
                    values(3)
                    scores(2)
                    scores(3)
                    pe.wait_ge(a_ready, 2 * h + 2)
                    pe.wait_ge(v_ready, NB * h + NB)
                    for st in range(2):
                        for half in range(2):
                            for kt in range(2):
                                batches = slice(4 * half, 4 * half + 4)
                                last = matmul3(nc, o_bank[2 * st + half][:, :], a[:, HI, kt, st * P:(st + 1) * P],
                                               a[:, LO, kt, st * P:(st + 1) * P], v[:, HI, kt, batches, :],
                                               v[:, LO, kt, batches, :], kt == 0, kt == 1)
                            last.then_inc(o_done, 1)

                head(0, True)
                with pe.Fori(1, RH) as h:
                    head(h, False)

            def v_view(part, n):
                return v[:, part, :, 2 * n:2 * n + 2, :]

            def v_psum(n):
                return v_bank[n % 2][:, :].rearrange("p (b t e) -> p t b e", b=2, t=2)

            @block.scalar
            def _(act):
                def ln_highs():
                    with act.Fori(0, NT // 2) as m:
                        for k in range(2):
                            act.wait_ge(ln_flipped, 2 * m + (k + 1))
                            nc.scalar.activation(xT[:, HI, :, bass.ds(m * (2 * P) + k * P, P)],
                                                 ln_bank[k][:, :].rearrange("p (c n) -> p c n", c=EC),
                                                 ACT.Copy).then_inc(ln_hi, 1)

                def head(h, first):
                    def keys(n):
                        act.wait_ge(k_done, NB * h + (n + 1))
                        if n >= 2:
                            act.wait_ge(v_flipped, NB * h + (n - 1))
                        nc.scalar.activation(k_full[:, n % 2, :], k_bank[n % 2][:, :], ACT.Copy).then_inc(
                            k_full_ready, 1)
                        nc.scalar.activation(kT[:, HI, n * 512:(n + 1) * 512], k_bank[n % 2][:, :],
                                             ACT.Copy).then_inc(k_hi, 1)

                    def queries(n):
                        act.wait_ge(q_done, NB * h + (n + 1))
                        nc.scalar.activation(qT[:, HI, n * 512:(n + 1) * 512], q_bank[n][:, :],
                                             ACT.Copy).then_inc(q_hi, 1)

                    def values(n):
                        act.wait_ge(v_flipped, NB * h + (n + 1))
                        nc.scalar.activation(v_view(HI, n), v_psum(n), ACT.Copy).then_inc(v_hi, 1)

                    keys(0)
                    keys(1)
                    if first:
                        ln_highs()
                    queries(0)
                    values(0)
                    keys(2)
                    queries(1)
                    values(1)
                    keys(3)
                    queries(2)
                    values(2)
                    queries(3)
                    values(3)
                    for kt in range(2):
                        act.wait_ge(a_full, 2 * h + (kt + 1))
                        nc.scalar.activation(a[:, HI, kt, :], a32[:, kt, :], ACT.Copy).then_inc(a_hi, 1)
                    for st in range(2):
                        for half in range(2):
                            act.wait_ge(o_done, 4 * h + (2 * st + half + 1))
                            tiles = o[:, 8 * half:8 * half + 8, bass.ds(h * P, P)].rearrange(
                                "p (b s) e -> p b s e", s=2)[:, :, st, :]
                            nc.scalar.activation(tiles, o_bank[2 * st + half][:, :].rearrange(
                                "p (b e) -> p b e", b=4), ACT.Copy).then_inc(o_read, 1)

                head(0, True)
                with act.Fori(1, RH) as h:
                    head(h, False)

            @block.vector
            def _(dve):
                def ln_normalise():
                    def normalise(t, k):
                        if not isinstance(t, int):
                            dve.wait_ge(ln_flipped, t - 1)
                        nc.vector.tensor_scalar(xn[:, k, :], x[:, bass.ds(t, 1), :].rearrange("p a e -> p (a e)"),
                                                ln_mean[:, bass.ds(t, 1)], ln_rstd[:, bass.ds(t, 1)],
                                                ALU.subtract, ALU.mult).then_inc(xn_ready, 1)

                    def low(t, k):
                        dve.wait_ge(ln_hi, t + 1)
                        nc.vector.tensor_tensor(xT[:, LO, :, bass.ds(t * P, P)],
                                                ln_bank[k][:, :].rearrange("p (c n) -> p c n", c=EC),
                                                xT[:, HI, :, bass.ds(t * P, P)], ALU.subtract).then_inc(ln_ready, 1)

                    dve.wait_ge(ln_rstd_ready, 1)
                    normalise(0, 0)
                    normalise(1, 1)
                    with dve.Fori(1, NT // 2) as m:
                        for k in range(2):
                            normalise(2 * m + k, k)
                            low(2 * m + (k - 2), k)
                    low(NT - 2, 0)
                    low(NT - 1, 1)

                def head_stats(h):
                    for t in range(NT):
                        dve.wait_ge(o_read, 4 * h + (4 if t == NT - 1 else 2 * (t % 2) + t // 8 + 1))
                        nc.vector.bn_stats(o_stats[:, t, bass.ds(2 * h, 2), :].rearrange("p a s -> p (a s)"),
                                           o[:, t, bass.ds(h * P, P)]).then_inc(stats_made, 1)

                def head(h, first):
                    def context(n):
                        dve.wait_ge(ctx_loaded[n % 2], 8 * NB * h + 16 * (n // 2 + 1))
                        if n >= 2:
                            dve.wait_ge(k_done, NB * h + (n - 1))
                        nc.vector.tensor_copy(ctx[:, n % 2, HI, :], ctx_raw[:, n % 2, :]).then_inc(ctx_hi, 1)
                        dve.wait_ge(ctx_hi, NB * h + (n + 1))
                        nc.vector.tensor_tensor(ctx[:, n % 2, LO, :], ctx_raw[:, n % 2, :], ctx[:, n % 2, HI, :],
                                                ALU.subtract).then_inc(ctx_ready, 1)

                    def keys(n):
                        dve.wait_ge(k_hi, NB * h + (n + 1))
                        nc.vector.tensor_tensor(kT[:, LO, n * 512:(n + 1) * 512], k_bank[n % 2][:, :],
                                                kT[:, HI, n * 512:(n + 1) * 512], ALU.subtract).then_inc(k_ready, 1)

                    def queries(n):
                        dve.wait_ge(q_hi, NB * h + (n + 1))
                        nc.vector.tensor_tensor(qT[:, LO, n * 512:(n + 1) * 512], q_bank[n][:, :],
                                                qT[:, HI, n * 512:(n + 1) * 512], ALU.subtract).then_inc(q_ready, 1)

                    def values(n):
                        dve.wait_ge(v_hi, NB * h + (n + 1))
                        nc.vector.tensor_tensor(v_view(LO, n), v_psum(n), v_view(HI, n),
                                                ALU.subtract).then_inc(v_ready, 1)

                    dve.wait_ge(head_loaded, 32 * h + 32)
                    if not first:
                        dve.wait_ge(q_done, NB * h)
                    nc.vector.tensor_copy(hw[:, HI, :], hw_raw[:, :]).then_inc(hw_hi, 1)
                    dve.wait_ge(hw_hi, h + 1)
                    nc.vector.tensor_tensor(hw[:, LO, :], hw_raw[:, :], hw[:, HI, :], ALU.subtract).then_inc(hw_ready, 1)
                    context(0)
                    context(1)
                    if first:
                        ln_normalise()
                    keys(0)
                    context(2)
                    keys(1)
                    queries(0)
                    context(3)
                    values(0)
                    keys(2)
                    queries(1)
                    values(1)
                    keys(3)
                    queries(2)
                    values(2)
                    queries(3)
                    values(3)
                    for kt in range(2):
                        dve.wait_ge(scored, 2 * h + (kt + 1))
                        nc.vector.tensor_tensor(masked[:, kt, :], score_bank[kt][:, 0:S], decay[:, kt, :],
                                                ALU.mult).then_inc(decayed, 1)
                        dve.wait_ge(decayed, 2 * h + (kt + 1))
                        nc.vector.tensor_scalar(a32[:, kt, :], masked[:, kt, :], -1.0, 1.0, ALU.mult,
                                                ALU.max).then_inc(negated, 1)
                        dve.wait_ge(negated, 2 * h + (kt + 1))
                        nc.vector.tensor_tensor(a32[:, kt, :], masked[:, kt, :], a32[:, kt, :],
                                                ALU.max).then_inc(a_full, 1)
                    for kt in range(2):
                        dve.wait_ge(a_hi, 2 * h + (kt + 1))
                        nc.vector.tensor_tensor(a[:, LO, kt, :], a32[:, kt, :], a[:, HI, kt, :],
                                                ALU.subtract).then_inc(a_ready, 1)
                    if not first:
                        head_stats(h - 1)

                moments_from_stats(nc, dve, stats[:, :, :], ln_mean[:, :], ln_half[:, :], ln_var[:, :], LN_EPS, ln_step, 0,
                                   ln_var_ready)
                head(0, True)
                with dve.Fori(1, RH) as h:
                    head(h, False)
                head_stats(RH - 1)
                dve.wait_ge(stats_made, NT * RH)

            @block.gpsimd
            def _(pool):
                pool.wait_ge(ln_var_ready, 1)
                nc.gpsimd.tensor_tensor(ln_rstd[:, :], ln_var[:, :], neg_half[:, 0:NT], ALU.pow).then_inc(
                    ln_rstd_ready, 1)

        with Space(nc, "mix") as s:
            gw = s.sb("gw", [P, 2, EC, E], F32R)
            ow = s.sb("ow", [P, 2, EC, E], F32R)
            gamma_b = s.sb("gamma_b", [P, E])
            beta_b = s.sb("beta_b", [P, E])
            mean = s.sb("mean", [P, NT])
            half = s.sb("half", [P, NT])
            var = s.sb("var", [P, NT])
            apart = s.sb("apart", [P, NT, 2 * RH])
            rstd = s.sb("rstd", [P, NT])
            xs = s.sb("xs", [P, 2, 2, EC, P], F32R)
            y = s.sb("y", [P, 2, E])
            wy = s.sb("wy", [P, 2, E])
            wyT = s.sb("wyT", [P, 2, 2, EC, P], F32R)
            ln_stats = s.sb("ln_stats", [P, 2, 6])
            ln_mean = s.sb("ln_mean", [P, 2])
            ln_half = s.sb("ln_half", [P, 2])
            ln_var = s.sb("ln_var", [P, 2])
            ln_rstd = s.sb("ln_rstd", [P, 2])
            xn = s.sb("xn", [P, 2, E])
            rw_raw = s.sb("rw_raw", [P, EC, W])
            rw = s.sb("rw", [P, 2, EC, W], F32R)
            logits = s.sb("logits", [P, NT, XP + 1])
            top = s.sb("top", [P, NT])
            logitsT = w_raw[:, :, :].rearrange("p c n -> p (c n)")[0:W, :]
            gate_bank = [s.bank(f"gate{k}") for k in range(2)]
            flip_bank = [s.bank(f"flip{k}") for k in range(2)]
            out_bank = [s.bank(f"out{k}") for k in range(2)]
            ln_bank = [s.bank(f"ln{k}") for k in range(2)]
            logit_bank = gate_bank + flip_bank
            w_loaded = s.sem("w_loaded")
            affine_loaded = s.sem("affine_loaded")
            w_hi = s.sem("w_hi")
            w_ready = s.sem("w_ready")
            step = s.sem("step")
            var_ready = s.sem("var_ready")
            rstd_ready = s.sem("rstd_ready")
            xs_loaded = [s.sem(f"xs_loaded{k}") for k in range(2)]
            y_normal = s.sem("y_normal")
            y_scaled = s.sem("y_scaled")
            y_ready = s.sem("y_ready")
            gated = s.sem("gated")
            wy_ready = s.sem("wy_ready")
            flipped = s.sem("flipped")
            wyT_hi = s.sem("wyT_hi")
            wyT_ready = s.sem("wyT_ready")
            out_done = s.sem("out_done")
            added = s.sem("added")
            ln_step = s.sem("ln_step")
            ln_var_ready = s.sem("ln_var_ready")
            ln_rstd_ready = s.sem("ln_rstd_ready")
            xn_ready = s.sem("xn_ready")
            ln_flipped = s.sem("ln_flipped")
            ln_hi = s.sem("ln_hi")
            ln_ready = s.sem("ln_ready")
            row_kept = s.sem("row_kept")
            parts_stored = s.sem("parts_stored")
            rw_loaded = s.sem("rw_loaded")
            rw_hi = s.sem("rw_hi")
            rw_ready = s.sem("rw_ready")
            logit_done = s.sem("logit_done")
            logit_copied = s.sem("logit_copied")
            logit_flipped = s.sem("logit_flipped")
            logits_step = s.sem("logits_step")
            exp_done = s.sem("exp_done")
            block = s.block()

            @block.sync
            def _(sp):
                sp.dma_start(gamma_b[:, :], gamma.rearrange("(a e) -> a e", a=1).to_broadcast([P, E])).then_inc(
                    affine_loaded, 16)
                sp.dma_start(beta_b[:, :], beta.rearrange("(a e) -> a e", a=1).to_broadcast([P, E])).then_inc(
                    affine_loaded, 16)

                def tile_in(t, k):
                    first = t * P
                    if not isinstance(t, int) or t > 1:
                        first = sp.snap(first)
                        sp.wait_ge(gated, t - 1)
                    sp.dma_start(xs[:, k, :, :, :].bitcast(F32), xT[:, :, :, bass.ds(first, P)].bitcast(F32)).then_inc(
                        xs_loaded[k], 16)

                tile_in(0, 0)
                tile_in(1, 1)
                sp.wait_ge(w_ready, EC)
                sp.dma_start(w_raw[:, :, :], out_w.rearrange("(c p) n -> p c n", p=P)).then_inc(w_loaded, 16)
                sp.dma_start(rw_raw[:, :, :], router).then_inc(rw_loaded, 16)

                def store_parts(pair):
                    moves = [(xt_dram[bass.ds(pair, 1), :, part, :, :].rearrange("b p c s -> (b p) c s"),
                              xT[:, part, :, bass.ds(pair * TS, TS)].bitcast(F32)) for part in (HI, LO)]
                    sp.wait_ge(ln_ready, 2 * pair + 2)
                    for dst, src in moves:
                        sp.dma_start(dst, src).then_inc(parts_stored, 16)

                with sp.Fori(1, 3) as m:
                    for k in range(2):
                        tile_in(2 * m + k, k)
                with sp.Fori(3, NT // 2) as m:
                    for k in range(2):
                        tile_in(2 * m + k, k)
                    store_parts(m - 3)
                for pair in range(NT // 2 - 3, NT // 2):
                    store_parts(pair)
                sp.wait_ge(parts_stored, 16 * NT)

            @block.tensor
            def _(pe):
                def gate(m, k):
                    t = 2 * m + k
                    pe.wait_ge(xs_loaded[k], 16 * m + 16)
                    if not isinstance(t, int) or t > 1:
                        pe.wait_ge(wy_ready, t - 1)
                    for c in range(EC):
                        if isinstance(t, int) and t == 0:
                            pe.wait_ge(w_ready, c + 1)
                        last = matmul3(nc, gate_bank[k][:, :], xs[:, k, HI, c, :], xs[:, k, LO, c, :],
                                       gw[:, HI, c, :], gw[:, LO, c, :], c == 0, c == EC - 1)
                    last.then_inc(gated, 1)

                def flip(t, k):
                    pe.wait_ge(wy_ready, t + 1)
                    if not isinstance(t, int) or t > 1:
                        pe.wait_ge(wyT_ready, t - 1)
                    for c in range(EC):
                        last = nc.tensor.transpose(flip_bank[k][:, c * P:(c + 1) * P], wy[:, k, c * P:(c + 1) * P],
                                                   ident[:, :])
                    last.then_inc(flipped, 1)

                def out(t, k):
                    pe.wait_ge(wyT_ready, t + 1)
                    if not isinstance(t, int) or t > 1:
                        pe.wait_ge(added, t - k)
                    for c in range(EC):
                        last = matmul3(nc, out_bank[k][:, :], wyT[:, k, HI, c, :], wyT[:, k, LO, c, :],
                                       ow[:, HI, c, :], ow[:, LO, c, :], c == 0, c == EC - 1)
                    last.then_inc(out_done, 1)

                def ln_flip(t, k):
                    pe.wait_ge(xn_ready, t + 1)
                    if not isinstance(t, int) or t > 1:
                        pe.wait_ge(ln_ready, t - 1)
                    for c in range(EC):
                        last = nc.tensor.transpose(ln_bank[k][:, c * P:(c + 1) * P], xn[:, k, c * P:(c + 1) * P],
                                                   ident[:, :])
                    last.then_inc(ln_flipped, 1)

                def route_logits(n):
                    pe.wait_ge(ln_ready, 4 * n + 4)
                    cols = slice(n * 512, (n + 1) * 512)
                    for c in range(EC):
                        last = matmul3(nc, logit_bank[n][0:W, :], rw[:, HI, c, :], rw[:, LO, c, :], xT[:, HI, c, cols],
                                       xT[:, LO, c, cols], c == 0, c == EC - 1)
                    last.then_inc(logit_done, 1)

                def round_(m, ln):
                    gate(m, 0)
                    flip(2 * m - 1, 1)
                    out(2 * m - 2, 0)
                    if ln:
                        ln_flip(2 * m - 4, 0)
                    gate(m, 1)
                    flip(2 * m, 0)
                    out(2 * m - 1, 1)
                    if ln:
                        ln_flip(2 * m - 3, 1)

                gate(0, 0)
                gate(0, 1)
                flip(0, 0)
                pe.wait_ge(w_ready, 2 * EC)
                round_(1, False)
                round_(2, True)
                with pe.Fori(3, NT // 2) as m:
                    round_(m, True)
                ln_flip(NT - 4, 0)
                flip(NT - 1, 1)
                out(NT - 2, 0)
                ln_flip(NT - 3, 1)
                out(NT - 1, 1)
                pe.wait_ge(rw_ready, 1)
                for n in range(NB - 1):
                    route_logits(n)
                ln_flip(NT - 2, 0)
                ln_flip(NT - 1, 1)
                route_logits(NB - 1)
                pe.wait_ge(logit_copied, NB)
                pe.wait_ge(added, NT)
                for t in range(NT):
                    last = nc.tensor.transpose(out_bank[0][:, t * W:(t + 1) * W], logitsT[:, t * P:(t + 1) * P],
                                               ident[0:W, 0:W])
                last.then_inc(logit_flipped, 1)

            @block.scalar
            def _(act):
                for n, w in enumerate((gw, ow)):
                    if n == 1:
                        act.wait_ge(w_loaded, 16)
                    for c in range(EC):
                        nc.scalar.activation(w[:, HI, c, :], w_raw[:, c, :], ACT.Copy).then_inc(w_hi, 1)

                def high(t, k):
                    act.wait_ge(flipped, t + 1)
                    nc.scalar.activation(wyT[:, k, HI, :, :], flip_bank[k][:, :].rearrange(
                        "p (c n) -> p c n", c=EC), ACT.Copy).then_inc(wyT_hi, 1)

                def ln_high(t, k):
                    act.wait_ge(ln_flipped, t + 1)
                    nc.scalar.activation(xT[:, HI, :, bass.ds(t * P, P)], ln_bank[k][:, :].rearrange(
                        "p (c n) -> p c n", c=EC), ACT.Copy).then_inc(ln_hi, 1)

                def keep_row(t, k):
                    act.wait_ge(xn_ready, t + 1)
                    nc.scalar.activation(rows[:, bass.ds(t, 1), :].rearrange("p a e -> p (a e)"),
                                         xn[:, k, :], ACT.Copy).then_inc(row_kept, 1)

                high(0, 0)
                high(1, 1)
                high(2, 0)
                with act.Fori(2, NT // 2) as m:
                    high(2 * m - 1, 1)
                    ln_high(2 * m - 4, 0)
                    keep_row(2 * m - 4, 0)
                    high(2 * m, 0)
                    keep_row(2 * m - 3, 1)
                    ln_high(2 * m - 3, 1)
                ln_high(NT - 4, 0)
                high(NT - 1, 1)
                keep_row(NT - 4, 0)
                ln_high(NT - 3, 1)
                keep_row(NT - 3, 1)

                def copy_logits(n):
                    act.wait_ge(logit_done, n + 1)
                    nc.scalar.activation(logitsT[:, n * 512:(n + 1) * 512], logit_bank[n][0:W, :],
                                         ACT.Copy).then_inc(logit_copied, 1)

                for n in range(NB - 1):
                    copy_logits(n)
                for k in range(2):
                    ln_high(NT - 2 + k, k)
                    keep_row(NT - 2 + k, k)
                copy_logits(NB - 1)
                act.wait_ge(logits_step, 3)
                nc.scalar.activation(exp_logits[:, :, :], exp_logits[:, :, :], ACT.Exp).then_inc(exp_done, 1)
                nc.scalar.activation(exp_gate[:, :], logits[:, :, XP], ACT.Exp, scale=-1.0).then_inc(exp_done, 1)
                act.wait_ge(exp_done, 2)

            @block.vector
            def _(dve):
                for c in range(EC):
                    dve.wait_ge(w_hi, c + 1)
                    nc.vector.tensor_tensor(gw[:, LO, c, :], w_raw[:, c, :], gw[:, HI, c, :], ALU.subtract).then_inc(
                        w_ready, 1)
                PARTS = 2 * RH
                nc.vector.reduce_sum(mean[:, :], o_stats[:, :, :, 1], AX_X).then_inc(step, 1)
                nc.vector.reduce_sum(var[:, :], o_stats[:, :, :, 2], AX_X).then_inc(step, 1)
                dve.wait_ge(step, 2)
                nc.vector.tensor_scalar(mean[:, :], mean[:, :], 1.0 / PARTS, None, ALU.mult).then_inc(step, 1)
                nc.vector.tensor_scalar(var[:, :], var[:, :], 1.0 / E, GN_EPS, ALU.mult, ALU.add).then_inc(step, 1)
                dve.wait_ge(step, 4)
                nc.vector.tensor_tensor(apart[:, :, :], o_stats[:, :, :, 1],
                                        mean[:, :].unsqueeze(2).to_broadcast([P, NT, PARTS]),
                                        ALU.subtract).then_inc(step, 1)
                dve.wait_ge(step, 5)
                nc.vector.tensor_tensor(apart[:, :, :], apart[:, :, :], apart[:, :, :], ALU.mult).then_inc(step, 1)
                dve.wait_ge(step, 6)
                nc.vector.reduce_sum(half[:, :], apart[:, :, :], AX_X).then_inc(step, 1)
                dve.wait_ge(step, 7)
                nc.vector.scalar_tensor_tensor(var[:, :], half[:, :], 1.0 / PARTS, var[:, :], ALU.mult,
                                               ALU.add).then_inc(var_ready, 1)
                dve.wait_ge(rstd_ready, 1)

                def normal(t, k):
                    if not isinstance(t, int) or t > 1:
                        dve.wait_ge(wy_ready, t - 1)
                    nc.vector.tensor_scalar(y[:, k, :], o[:, bass.ds(t, 1), :].rearrange("p a e -> p (a e)"),
                                            mean[:, bass.ds(t, 1)], rstd[:, bass.ds(t, 1)],
                                            ALU.subtract, ALU.mult).then_inc(y_normal, 1)

                def gate_y(t, k):
                    dve.wait_ge(gated, t + 1)
                    dve.wait_ge(y_ready, t + 1)
                    if not isinstance(t, int) or t > 1:
                        dve.wait_ge(flipped, t - 1)
                    nc.vector.scalar_tensor_tensor(wy[:, k, :], gate_bank[k][:, :], 0.0, y[:, k, :], ALU.max,
                                                   ALU.mult).then_inc(wy_ready, 1)

                def low(t, k):
                    dve.wait_ge(wyT_hi, t + 1)
                    nc.vector.tensor_tensor(wyT[:, k, LO, :, :], flip_bank[k][:, :].rearrange(
                        "p (c n) -> p c n", c=EC), wyT[:, k, HI, :, :], ALU.subtract).then_inc(wyT_ready, 1)

                def add(t, k):
                    dve.wait_ge(out_done, t + 1)
                    rows = x[:, bass.ds(t, 1), :].rearrange("p a e -> p (a e)")
                    nc.vector.tensor_tensor(rows, out_bank[k][:, :], rows, ALU.add).then_inc(added, 1)

                def ln_moments(pair):
                    for k in range(2):
                        if not isinstance(pair, int) or pair > 0:
                            dve.wait_ge(xn_ready, 2 * pair)
                        dve.wait_ge(added, 2 * pair + (k + 1))
                        nc.vector.bn_stats(ln_stats[:, k, :], x[:, bass.ds(2 * pair + k, 1), :].rearrange(
                            "p a e -> p (a e)")).then_inc(ln_step, 1)
                    moments_from_stats(nc, dve, ln_stats[:, :, :], ln_mean[:, :], ln_half[:, :], ln_var[:, :], LN_EPS,
                                       ln_step, 8 * pair + 2, ln_var_ready)

                def ln_normal(t, k):
                    if not isinstance(t, int) or t > 1:
                        dve.wait_ge(ln_flipped, t - 1)
                        dve.wait_ge(row_kept, t - 1)
                    nc.vector.tensor_scalar(xn[:, k, :], x[:, bass.ds(t, 1), :].rearrange("p a e -> p (a e)"),
                                            ln_mean[:, k:k + 1], ln_rstd[:, k:k + 1],
                                            ALU.subtract, ALU.mult).then_inc(xn_ready, 1)

                def ln_low(t, k):
                    dve.wait_ge(ln_hi, t + 1)
                    nc.vector.tensor_tensor(xT[:, LO, :, bass.ds(t * P, P)],
                                            ln_bank[k][:, :].rearrange("p (c n) -> p c n", c=EC),
                                            xT[:, HI, :, bass.ds(t * P, P)], ALU.subtract).then_inc(ln_ready, 1)

                def round_(m, ln, more=True):
                    gate_y(2 * m, 0)
                    if more:
                        normal(2 * m + 2, 0)
                    low(2 * m - 1, 1)
                    if ln:
                        dve.wait_ge(ln_rstd_ready, m - 1)
                        ln_normal(2 * m - 4, 0)
                    add(2 * m - 2, 0)
                    if ln:
                        ln_normal(2 * m - 3, 1)
                    gate_y(2 * m + 1, 1)
                    if more:
                        normal(2 * m + 3, 1)
                    if ln:
                        ln_low(2 * m - 4, 0)
                    low(2 * m, 0)
                    add(2 * m - 1, 1)
                    ln_moments(m - 1)
                    if ln:
                        ln_low(2 * m - 3, 1)

                normal(0, 0)
                normal(1, 1)
                for c in range(EC):
                    dve.wait_ge(w_hi, EC + c + 1)
                    nc.vector.tensor_tensor(ow[:, LO, c, :], w_raw[:, c, :], ow[:, HI, c, :], ALU.subtract).then_inc(
                        w_ready, 1)
                dve.wait_ge(rw_loaded, 16)
                nc.vector.tensor_copy(rw[:, HI, :, :], rw_raw[:, :, :]).then_inc(rw_hi, 1)
                dve.wait_ge(rw_hi, 1)
                nc.vector.tensor_tensor(rw[:, LO, :, :], rw_raw[:, :, :], rw[:, HI, :, :], ALU.subtract).then_inc(
                    rw_ready, 1)
                gate_y(0, 0)
                normal(2, 0)
                gate_y(1, 1)
                normal(3, 1)
                low(0, 0)
                round_(1, False)
                round_(2, True)
                with dve.Fori(3, NT // 2 - 1) as m:
                    round_(m, True)
                round_(NT // 2 - 1, True, more=False)
                dve.wait_ge(ln_rstd_ready, NT // 2 - 1)
                ln_normal(NT - 4, 0)
                ln_normal(NT - 3, 1)
                low(NT - 1, 1)
                add(NT - 2, 0)
                add(NT - 1, 1)
                ln_moments(NT // 2 - 1)
                ln_low(NT - 4, 0)
                ln_low(NT - 3, 1)
                dve.wait_ge(ln_rstd_ready, NT // 2)
                ln_normal(NT - 2, 0)
                ln_normal(NT - 1, 1)
                ln_low(NT - 2, 0)
                ln_low(NT - 1, 1)
                dve.wait_ge(logit_flipped, 1)
                nc.vector.tensor_copy(logits[:, :, :], out_bank[0][:, :].rearrange(
                    "p (t w) -> p t w", w=W)[:, :, 0:XP + 1]).then_inc(logits_step, 1)
                dve.wait_ge(logits_step, 1)
                nc.vector.tensor_reduce(top[:, :], logits[:, :, 0:XP], AX_X, ALU.max).then_inc(logits_step, 1)
                dve.wait_ge(logits_step, 2)
                nc.vector.tensor_tensor(exp_logits[:, :, :], logits[:, :, 0:XP],
                                        top[:, :].unsqueeze(2).to_broadcast([P, NT, XP]),
                                        ALU.subtract).then_inc(logits_step, 1)

            @block.gpsimd
            def _(pool):
                pool.wait_ge(var_ready, 1)
                nc.gpsimd.tensor_tensor(rstd[:, :], var[:, :], neg_half[:, 0:NT], ALU.pow).then_inc(rstd_ready, 1)
                pool.wait_ge(affine_loaded, 32)

                def affine(t, k):
                    pool.wait_ge(y_normal, t + 1)
                    nc.gpsimd.tensor_tensor(y[:, k, :], y[:, k, :], gamma_b[:, :], ALU.mult).then_inc(y_scaled, 1)
                    pool.wait_ge(y_scaled, t + 1)
                    nc.gpsimd.tensor_tensor(y[:, k, :], y[:, k, :], beta_b[:, :], ALU.add).then_inc(y_ready, 1)

                def inverse_deviation(pair):
                    pool.wait_ge(ln_var_ready, pair + 1)
                    nc.gpsimd.tensor_tensor(ln_rstd[:, :], ln_var[:, :], neg_half[:, 0:2], ALU.pow).then_inc(
                        ln_rstd_ready, 1)

                affine(0, 0)
                affine(1, 1)
                affine(2, 0)
                affine(3, 1)
                with pool.Fori(2, NT // 2) as m:
                    affine(2 * m, 0)
                    affine(2 * m + 1, 1)
                    inverse_deviation(m - 2)
                inverse_deviation(NT // 2 - 2)
                inverse_deviation(NT // 2 - 1)


def experts(nc, x, rows, exp_logits, exp_gate, ident, xt_dram, slot_rows, slot_out, w_gate, w_up, w_down, out):
    RANK_STEP = 2
    BATCHES = N // TS
    ROUTE = "routed"
    IT = 3
    R0 = SHARED_STEPS // 2
    R1 = R0 + ROUTED
    C0 = R1 + 2
    O0 = STEPS - BATCHES + 1
    SEED = 1
    LAST = STEPS - 1
    with Space(nc, "moe") as s:
        x_rows = s.sb("x_rows", [P, 2, E])
        g_raw = s.sb("g_raw", [P, EC, WP])
        u_raw = s.sb("u_raw", [P, EC, WP])
        d_raw = s.sb("d_raw", [P, IT, E])
        g_w = s.sb("g_w", [P, 2, EC, WP], F32R)
        u_w = s.sb("u_w", [P, 2, EC, WP], F32R)
        d_w = s.sb("d_w", [P, 2, IT, E], F32R)
        hT = s.sb("hT", [P, 2, 2, EC, TS], F32R)
        silu = s.sb("silu", [P, IT, TS])
        act_full = s.sb("act_full", [P, IT, TS])
        act_w = s.sb("act_w", [P, 2, IT, TS], F32R)
        y = s.sb("y", [P, 2, E])
        got = s.sb("got", [P, 2, TOPK, E])
        top_w = s.sb("top_w", [P, NT, TOPK])
        slot = s.sb("slot", [P, NT, TOPK], U32)
        shared_gate = s.sb("shared_gate", [P, NT])
        expert_of = s.sb("expert_of", [P, ROUTED], I32)
        total = s.sb("total", [P, NT])
        probs = s.sb("probs", [P, NT, XP])
        best = s.sb("best", [P, NT, 8])
        best_at = s.sb("best_at", [P, NT, 8], U32)
        chosen = s.sb("chosen", [P, NT, TOPK])
        top_sum = s.sb("top_sum", [P, NT])
        expert_ids = s.sb("expert_ids", [P, XP])
        onehot = s.sb("onehot", [P, NT, TOPK, XP])
        member = s.sb("member", [P, NT, XP], BF16)
        before = s.sb("before", [P, P], BF16)
        ones = s.sb("ones", [P, P], BF16)
        in_tile = s.sb("in_tile", [P, NT, XP])
        rank = s.sb("rank", [P, NT, XP])
        prior = s.sb("prior", [P, NT, XP])
        count = s.sb("count", [P, XP])
        tile_starts = s.sb("tile_starts", [P, N // TS])
        used = s.sb("used", [P, XP, N // TS])
        tiles = s.sb("tiles", [P, XP])
        one_row = s.sb("one_row", [P, XP])
        tiles_to = s.sb("tiles_to", [P, XP])
        base = s.sb("base", [P, XP])
        place = s.sb("place", [P, NT, XP])
        picked = s.sb("picked", [P, NT, TOPK, XP])
        place_k = s.sb("place_k", [P, NT, TOPK])
        tile_ids = s.sb("tile_ids", [P, ROUTED])
        past = s.sb("past", [P, ROUTED, XP])
        owner = s.sb("owner", [P, ROUTED])
        flip_bank = [s.bank(f"flip{k}") for k in range(2)]
        gate_bank = [s.bank(f"gate{k}") for k in range(2)]
        up_bank = [s.bank(f"up{k}") for k in range(2)]
        down_bank = [s.bank(f"down{k}") for k in range(2)]
        x_loaded = s.sem("x_loaded")
        g_loaded = s.sem("g_loaded")
        u_loaded = s.sem("u_loaded")
        d_loaded = s.sem("d_loaded")
        g_hi = s.sem("g_hi")
        u_hi = s.sem("u_hi")
        d_hi = s.sem("d_hi")
        g_ready = s.sem("g_ready")
        u_ready = s.sem("u_ready")
        d_ready = s.sem("d_ready")
        flipped = s.sem("flipped")
        hT_hi = s.sem("hT_hi")
        hT_ready = s.sem("hT_ready")
        gate_done = s.sem("gate_done")
        up_done = s.sem("up_done")
        silu_ready = s.sem("silu_ready")
        act_ready = s.sem("act_ready")
        act_hi = s.sem("act_hi")
        act_split = s.sem("act_split")
        down_done = s.sem("down_done")
        down_read = s.sem("down_read")
        y_stored = s.sem("y_stored")
        dispatched = s.sem("dispatched")
        fetched = s.sem("fetched")
        gathered = s.sem("gathered")
        out_stored = s.sem("out_stored")
        table_made = s.sem("table_made")
        tables_ready = s.sem("tables_ready")
        member_ready = s.sem("member_ready")
        ranked = s.sem("ranked")
        rank_read = s.sem("rank_read")
        route_step = s.sem("route_step")
        slots_ready = s.sem("slots_ready")
        owners_ready = s.sem("owners_ready")
        block = s.block()

        def phase(n):
            if n < 0 or n >= STEPS:
                return None
            if R0 <= n < R1:
                return ROUTE
            return n // BATCHES if n < R0 else SHARED // 2 + (n - R1) // BATCHES

        def start(part):
            return part * BATCHES if part < SHARED // 2 else R1 + (part - SHARED // 2) * BATCHES

        def fresh(before, this):
            return this is not None and (this == ROUTE or this != before)

        def load_index(n, this):
            if this == ROUTE:
                return n - (R0 - SHARED // 2)
            return this if this < SHARED // 2 else this + ROUTED

        def width(this):
            return WI if this == ROUTE else min(WP, WS - this * WP)

        def inner_tiles(this):
            return [(it, min(P, width(this) - it * P)) for it in range(-(-width(this) // P))]

        def runs(eng, body, own=lambda n: None):
            traits = [(tuple(phase(n + d) for d in (-2, -1, 0, 1)), own(n)) for n in range(STEPS)]
            first = 0
            while first < STEPS:
                to = first + 1
                while to < STEPS and traits[to] == traits[first]:
                    to += 1
                if to == first + 1:
                    body(first, *traits[first])
                else:
                    with eng.Fori(first, to) as n:
                        body(n, *traits[first])
                first = to

        def hT_of(n, part, chunks=slice(0, EC)):
            if isinstance(part, slice):
                return hT[:, bass.ds(n % 2, 1), part, chunks, :].rearrange("p s l c n -> p (s l c n)")
            return hT[:, bass.ds(n % 2, 1), part, chunks, :].rearrange("p s c n -> p (s c n)")

        def inner(bank_pair, it, rows_of):
            return bank_pair[it // 2][0:rows_of, (it % 2) * TS:(it % 2 + 1) * TS]

        def both(bank_pair, buf, this):
            views = [(bank_pair[0][:, :], buf[:, 0:2, :].rearrange("p i n -> p (i n)"))]
            for it, k in inner_tiles(this)[2:]:
                views.append((bank_pair[1][0:k, 0:TS], buf[0:k, it, :]))
            return views

        def halves(this):
            return [(slice(0, P), slice(0, 2))] + [(slice(0, k), it) for it, k in inner_tiles(this)[2:]]

        @block.sync
        def _(sp):
            def load_x(n, this):
                if this == ROUTE:
                    dst = x_rows[:, :, :]
                    src = slot_rows.rearrange("(s t p) e -> s p t e", t=2, p=P)[bass.ds(n - R0, 1), :, :, :].rearrange(
                        "s p t e -> (s p) t e")
                    if not isinstance(n, int) or n > R0:
                        sp.wait_ge(flipped, n - R0)
                else:
                    dst = hT_of(n, slice(0, 2)).bitcast(F32)
                    src = xt_dram[bass.ds(n - start(this), 1), :, :, :, :].rearrange("b p l c s -> (b p) (l c s)")
                    if not isinstance(n, int) or n > 1:
                        sp.wait_ge(up_done, n - 1)
                if not isinstance(n, int) or n > 0:
                    sp.wait_ge(x_loaded, 16 * n)
                sp.dma_start(dst, src).then_inc(x_loaded, 16)

            def expert(n, this):
                return sp.value_load(expert_of[0:1, bass.ds(n - R0, 1)], min_val=0, max_val=XP - 1)

            def load_w(n, this, e, w, raw, loaded, ready):
                i = load_index(n, this)
                if not isinstance(i, int) or i > 0:
                    sp.wait_ge(ready, i)
                routed, shared = w
                if raw is d_raw:
                    part = slice(0, len(inner_tiles(this))), slice(0, E)
                else:
                    part = slice(0, EC), slice(0, width(this))
                src = routed[bass.ds(e, 1), :, part[0], part[1]].rearrange("x p c n -> (x p) c n") \
                    if this == ROUTE else shared[this, :, part[0], part[1]]
                sp.dma_start(raw[:, part[0], part[1]], src).then_inc(loaded, 16)

            def store_y(n):
                dst = slot_out.rearrange("(s t p) e -> s p t e", t=2, p=P)[bass.ds(n - R0, 1), :, :, :]
                sp.wait_ge(down_read, n + 1)
                sp.dma_start(dst.rearrange("s p t e -> (s p) t e"), y[:, :, :]).then_inc(y_stored, 16)

            def store_out(pair):
                dst = out.rearrange("b (t p) e -> b p t e", p=P)[bass.ds(pair, 1), :, :, :]
                src = x[:, bass.ds(2 * pair, 2), :]
                sp.wait_ge(down_read, pair + O0)
                sp.wait_ge(gathered, SEED + TOPK * 2 * (pair + 1))
                sp.dma_start(dst.rearrange("b p t e -> (b p) t e"), src).then_inc(out_stored, 16)

            def step(n, phases, own):
                _, before, this, after = phases
                if isinstance(n, int) and n == R0 - 1:
                    sp.wait_ge(owners_ready, 1)
                    sp.wait_ge(dispatched, 16 * NT * TOPK)
                e = expert(n + 1, after) if after == ROUTE else None
                if after is not None:
                    load_x(n + 1, after)
                if fresh(this, after):
                    load_w(n + 1, after, e, w_gate, g_raw, g_loaded, g_ready)
                    load_w(n + 1, after, e, w_up, u_raw, u_loaded, u_ready)
                if fresh(before, this):
                    e = expert(n, this) if this == ROUTE else None
                    load_w(n, this, e, w_down, d_raw, d_loaded, d_ready)
                if own == "results":
                    store_y(n - 2)
                if own == "output":
                    store_out(n - (O0 + 2))

            load_w(0, 0, None, w_gate, g_raw, g_loaded, g_ready)
            load_x(0, 0)
            load_w(0, 0, None, w_up, u_raw, u_loaded, u_ready)
            runs(sp, step, lambda n: "results" if R0 <= n - 2 < R1 else "output" if n >= O0 + 2 else None)
            for pair in range(STEPS - (O0 + 2), BATCHES):
                store_out(pair)
            sp.wait_ge(out_stored, 16 * BATCHES)

        @block.gpsimd
        def _(pool):
            nc.gpsimd.memset(before[:, :], 1.0).then_inc(table_made, 1)
            nc.gpsimd.memset(ones[:, :], 1.0).then_inc(tables_ready, 1)
            nc.gpsimd.memset(one_row[:, :], 1.0).then_inc(tables_ready, 1)
            pool.wait_ge(table_made, 1)
            nc.gpsimd.affine_select(out=before[:, :], in_=before[:, :], compare_op=ALU.is_gt, fill=0.0, base=0,
                                    pattern=[[1, P]], channel_multiplier=-1).then_inc(tables_ready, 1)
            for table, step_by in ((expert_ids, 1), (tile_starts, TS), (tile_ids, 1)):
                nc.gpsimd.iota(table[:, :], pattern=[[step_by, table.shape[1]]], base=0, channel_multiplier=0,
                               allow_small_or_imprecise_dtypes=True).then_inc(tables_ready, 1)
            pool.wait_ge(slots_ready, 1)
            for t in range(NT):
                for k in range(TOPK):
                    nc.gpsimd.indirect_dma_start(
                        out=slot_rows, out_offset=bass.IndirectOffsetOnAxis(ap=slot[:, t, k:k + 1], axis=0),
                        in_=rows[:, t, :], in_offset=None).then_inc(dispatched, 16)
            pool.wait_ge(dispatched, 16 * NT * TOPK)
            pool.wait_ge(y_stored, 16 * ROUTED)
            for t in range(NT):
                if t > 0:
                    pool.wait_ge(fetched, 16 * TOPK * t)
                if t > 1:
                    pool.wait_ge(gathered, SEED + TOPK * (t - 1))
                for k in range(TOPK):
                    nc.gpsimd.indirect_dma_start(
                        out=got[:, t % 2, k, :], out_offset=None, in_=slot_out,
                        in_offset=bass.IndirectOffsetOnAxis(ap=slot[:, t, k:k + 1], axis=0)).then_inc(fetched, 16)

        @block.tensor
        def _(pe):
            def flip(n):
                pe.wait_ge(x_loaded, 16 * n + 16)
                if not isinstance(n, int) or n > R0:
                    pe.wait_ge(hT_ready, n - R0)
                for tile in range(2):
                    for c in range(EC):
                        bank, col = flip_bank[c // 2], (c % 2) * TS + tile * P
                        last = nc.tensor.transpose(bank[:, col:col + P], x_rows[:, tile, c * P:(c + 1) * P],
                                                   ident[:, :])
                last.then_inc(flipped, 1)

            def widen(n, this, w, w_ready, banks, banks_read, done):
                if this == ROUTE:
                    pe.wait_ge(hT_ready, n - R0 + 1)
                else:
                    pe.wait_ge(x_loaded, 16 * n + 16)
                pe.wait_ge(w_ready, load_index(n, this) + 1)
                if not isinstance(n, int) or n > 0:
                    pe.wait_ge(banks_read, n)
                for it, k in inner_tiles(this):
                    cols = slice(it * P, it * P + k)
                    for c in range(EC):
                        last = matmul3(nc, inner(banks, it, k), w[:, HI, c, cols], w[:, LO, c, cols],
                                       hT_of(n, HI, slice(c, c + 1)), hT_of(n, LO, slice(c, c + 1)),
                                       c == 0, c == EC - 1)
                last.then_inc(done, 1)

            def narrow(n, this):
                pe.wait_ge(act_split, n + 1)
                pe.wait_ge(d_ready, load_index(n, this) + 1)
                if not isinstance(n, int) or n > 0:
                    pe.wait_ge(down_read, n)
                its = inner_tiles(this)
                for tile in range(2):
                    toks = slice(tile * P, (tile + 1) * P)
                    for it, k in its:
                        last = matmul3(nc, down_bank[tile][:, :], act_w[0:k, HI, it, toks], act_w[0:k, LO, it, toks],
                                       d_w[0:k, HI, it, :], d_w[0:k, LO, it, :], it == 0, it == len(its) - 1)
                last.then_inc(down_done, 1)

            def count_tokens():
                m = member[:, :, :].rearrange("p t e -> p (t e)")
                pe.wait_ge(member_ready, 1)
                pe.wait_ge(tables_ready, 6)
                nc.tensor.matmul(flip_bank[0][:, 0:NT * XP], before[:, :], m, start=True, stop=True)
                nc.tensor.matmul(flip_bank[0][:, NT * XP:2 * NT * XP], ones[:, :], m, start=True,
                                 stop=True).then_inc(ranked, 1)
                pe.wait_ge(rank_read, 1)

            def step(n, phases, counting):
                _, before, this, after = phases
                widen(n, this, g_w, g_ready, gate_bank, silu_ready, gate_done)
                widen(n, this, u_w, u_ready, up_bank, act_ready, up_done)
                if counting:
                    count_tokens()
                if after == ROUTE:
                    flip(n + 1)
                if before is not None:
                    narrow(n - 1, before)

            runs(pe, step, lambda n: n == RANK_STEP)
            narrow(LAST, phase(LAST))

        @block.scalar
        def _(act):
            nc.scalar.preload_act_table(ACT.Silu)

            def weights_high(n, this, loaded, raw, w, users, hi):
                act.wait_ge(loaded, load_index(n, this) * 16 + 16)
                if not isinstance(n, int) or n > 0:
                    act.wait_ge(users, n)
                if raw is d_raw:
                    its = len(inner_tiles(this))
                    nc.scalar.activation(w[:, HI, 0:its, :], raw[:, 0:its, :], ACT.Copy).then_inc(hi, 1)
                else:
                    cols = width(this)
                    nc.scalar.activation(w[:, HI, :, 0:cols], raw[:, :, 0:cols], ACT.Copy).then_inc(hi, 1)

            def hT_high(n):
                act.wait_ge(flipped, n - R0 + 1)
                for k in range(2):
                    last = nc.scalar.activation(hT_of(n, HI, slice(2 * k, 2 * k + 2)), flip_bank[k][:, :], ACT.Copy)
                last.then_inc(hT_hi, 1)

            def act_high(n, this):
                act.wait_ge(act_ready, n + 1)
                if not isinstance(n, int) or n > 0:
                    act.wait_ge(down_done, n)
                for k, it in halves(this):
                    last = nc.scalar.activation(act_w[k, HI, it, :], act_full[k, it, :], ACT.Copy)
                last.then_inc(act_hi, 1)

            def silus(n, this):
                act.wait_ge(gate_done, n + 1)
                if not isinstance(n, int) or n > 0:
                    act.wait_ge(act_ready, n)
                for src, dst in both(gate_bank, silu, this):
                    last = nc.scalar.activation(dst, src, ACT.Silu)
                last.then_inc(silu_ready, 1)

            def results(n):
                act.wait_ge(down_done, n + 1)
                if not isinstance(n, int) or n > R0:
                    act.wait_ge(y_stored, 16 * (n - R0))
                nc.scalar.activation(y[:, 0, :], down_bank[0][:, :], ACT.Copy)
                nc.scalar.activation(y[:, 1, :], down_bank[1][:, :], ACT.Copy).then_inc(down_read, 1)

            def step(n, phases, own):
                before2, before, this, after = phases
                if before is not None:
                    act_high(n - 1, before)
                if fresh(before2, before):
                    weights_high(n - 1, before, d_loaded, d_raw, d_w, down_done, d_hi)
                silus(n, this)
                if fresh(this, after):
                    weights_high(n + 1, after, g_loaded, g_raw, g_w, gate_done, g_hi)
                if after == ROUTE:
                    hT_high(n + 1)
                if fresh(this, after):
                    weights_high(n + 1, after, u_loaded, u_raw, u_w, up_done, u_hi)
                if before == ROUTE:
                    results(n - 1)

            weights_high(0, 0, g_loaded, g_raw, g_w, gate_done, g_hi)
            weights_high(0, 0, u_loaded, u_raw, u_w, up_done, u_hi)
            runs(act, step)
            act_high(LAST, phase(LAST))

        @block.vector
        def _(dve):
            def weights_low(n, this, raw, w, hi, ready):
                dve.wait_ge(hi, load_index(n, this) + 1)
                if raw is d_raw:
                    part = slice(0, len(inner_tiles(this))), slice(0, E)
                else:
                    part = slice(0, EC), slice(0, width(this))
                nc.vector.tensor_tensor(w[:, LO, part[0], part[1]], raw[:, part[0], part[1]],
                                        w[:, HI, part[0], part[1]], ALU.subtract).then_inc(ready, 1)

            def hT_low(n):
                dve.wait_ge(hT_hi, n - R0 + 1)
                for k in range(2):
                    chunks = slice(2 * k, 2 * k + 2)
                    last = nc.vector.tensor_tensor(hT_of(n, LO, chunks), flip_bank[k][:, :], hT_of(n, HI, chunks),
                                                   ALU.subtract)
                last.then_inc(hT_ready, 1)

            def products(n, this):
                dve.wait_ge(silu_ready, n + 1)
                dve.wait_ge(up_done, n + 1)
                if not isinstance(n, int) or n > 0:
                    dve.wait_ge(act_split, n)
                for (src, full), (_, other) in zip(both(up_bank, act_full, this), both(up_bank, silu, this)):
                    last = nc.vector.tensor_tensor(full, src, other, ALU.mult)
                last.then_inc(act_ready, 1)

            def act_low(n, this):
                dve.wait_ge(act_hi, n + 1)
                for k, it in halves(this):
                    last = nc.vector.tensor_tensor(act_w[k, LO, it, :], act_full[k, it, :], act_w[k, HI, it, :],
                                                   ALU.subtract)
                last.then_inc(act_split, 1)

            def add_shared(n, this):
                dve.wait_ge(down_done, n + 1)
                for tile in range(2):
                    t = (n - start(this)) * 2 + tile
                    rows_of = x[:, bass.ds(t, 1), :].rearrange("p a e -> p (a e)")
                    last = nc.vector.scalar_tensor_tensor(rows_of, down_bank[tile][:, :],
                                                          shared_gate[:, bass.ds(t, 1)], rows_of, ALU.mult, ALU.add)
                last.then_inc(down_read, 1)

            def add_routed(t):
                dve.wait_ge(fetched, t * (16 * TOPK) + 16 * TOPK)
                rows_of = x[:, bass.ds(t, 1), :].rearrange("p a e -> p (a e)")
                for j in range(TOPK):
                    dve.wait_ge(gathered, TOPK * t + (j + SEED))
                    nc.vector.scalar_tensor_tensor(
                        rows_of, got[:, bass.ds(t % 2, 1), j, :].rearrange("p a e -> p (a e)"),
                        top_w[:, bass.ds(t, 1), j:j + 1].rearrange("p a j -> p (a j)"),
                        rows_of, ALU.mult, ALU.add).then_inc(gathered, 1)

            steps = [0]

            def chain(instruction):
                steps[0] += 1
                instruction.then_inc(route_step, 1)
                dve.wait_ge(route_step, steps[0])

            v = nc.vector

            def choose():
                chain(v.reduce_sum(total[:, :], exp_logits[:, :, :], AX_X))
                chain(v.reciprocal(total[:, :], total[:, :]))
                chain(v.tensor_tensor(probs[:, :, :], exp_logits[:, :, :],
                                      total[:, :].unsqueeze(2).to_broadcast([P, NT, XP]), ALU.mult))
                for t in range(NT):
                    ins = v.max(best[:, t, :], probs[:, t, :])
                chain(ins)
                chain(v.tensor_scalar(shared_gate[:, :], exp_gate[:, :], 1.0, None, ALU.add))
                chain(v.reciprocal(shared_gate[:, :], shared_gate[:, :]))

            def name_chosen():
                for t in range(NT):
                    ins = v.max_index(best_at[:, t, :], best[:, t, :], probs[:, t, :])
                chain(ins)
                chain(v.tensor_copy(chosen[:, :, :], best_at[:, :, 0:TOPK]))
                dve.wait_ge(tables_ready, 6)
                chain(v.tensor_tensor(onehot[:, :, :, :],
                                      chosen[:, :, :].unsqueeze(3).to_broadcast([P, NT, TOPK, XP]),
                                      expert_ids[:, :].unsqueeze(1).unsqueeze(1).to_broadcast([P, NT, TOPK, XP]),
                                      ALU.is_equal))
                with nc.allow_low_precision(reason="zeros and ones"):
                    v.reduce_sum(member[:, :, :], onehot[:, :, :, :].rearrange("p t k e -> p t e k"),
                                 AX_X).then_inc(member_ready, 1)

            def read_counts():
                dve.wait_ge(ranked, 1)
                v.tensor_copy(rank[:, :, :], flip_bank[0][:, 0:NT * XP].rearrange("p (t e) -> p t e", e=XP))
                v.tensor_copy(in_tile[:, :, :], flip_bank[0][:, NT * XP:2 * NT * XP].rearrange(
                    "p (t e) -> p t e", e=XP)).then_inc(rank_read, 1)
                dve.wait_ge(rank_read, 1)

            def count_prior():
                chain(v.memset(prior[:, 0, :], 0.0))
                for t in range(1, NT):
                    chain(v.tensor_tensor(prior[:, t, :], prior[:, t - 1, :], in_tile[:, t - 1, :], ALU.add))
                chain(v.tensor_tensor(count[:, :], prior[:, NT - 1, :], in_tile[:, NT - 1, :], ALU.add))

            def lay_out():
                chain(v.tensor_tensor(used[:, :, :], count[:, :].unsqueeze(2).to_broadcast([P, XP, N // TS]),
                                      tile_starts[:, :].unsqueeze(1).to_broadcast([P, XP, N // TS]), ALU.is_gt))
                chain(v.reduce_sum(tiles[:, :], used[:, :, :], AX_X))
                chain(v.tensor_tensor_scan(tiles_to[:, :], one_row[:, :], tiles[:, :], 0.0, ALU.mult, ALU.add))
                chain(v.tensor_tensor(base[:, :], tiles_to[:, :], tiles[:, :], ALU.subtract))
                chain(v.tensor_scalar(base[:, :], base[:, :], float(TS), None, ALU.mult))
                chain(v.tensor_tensor(place[:, :, :], rank[:, :, :], prior[:, :, :], ALU.add))
                chain(v.tensor_tensor(place[:, :, :], place[:, :, :],
                                      base[:, :].unsqueeze(1).to_broadcast([P, NT, XP]), ALU.add))

            def place_tokens():
                chain(v.tensor_tensor(picked[:, :, :, :], onehot[:, :, :, :],
                                      place[:, :, :].unsqueeze(2).to_broadcast([P, NT, TOPK, XP]), ALU.mult))
                chain(v.reduce_sum(place_k[:, :, :], picked[:, :, :, :], AX_X))
                v.tensor_copy(slot[:, :, :], place_k[:, :, :]).then_inc(slots_ready, 1)

            def name_owners():
                chain(v.tensor_tensor(past[:, :, :], tiles_to[:, :].unsqueeze(1).to_broadcast([P, ROUTED, XP]),
                                      tile_ids[:, :].unsqueeze(2).to_broadcast([P, ROUTED, XP]), ALU.is_le))
                chain(v.reduce_sum(owner[:, :], past[:, :, :], AX_X))
                chain(v.tensor_scalar(owner[:, :], owner[:, :], float(XP - 1), None, ALU.min))
                v.tensor_copy(expert_of[:, :], owner[:, :]).then_inc(owners_ready, 1)
                chain(v.reduce_sum(top_sum[:, :], best[:, :, 0:TOPK], AX_X))
                chain(v.tensor_scalar(top_sum[:, :], top_sum[:, :], 1e-9, None, ALU.max))
                chain(v.reciprocal(top_sum[:, :], top_sum[:, :]))
                chain(v.tensor_tensor(top_w[:, :, :], best[:, :, 0:TOPK],
                                      top_sum[:, :].unsqueeze(2).to_broadcast([P, NT, TOPK]), ALU.mult))

            routing = {0: choose, 1: name_chosen, 2: count_prior, 3: lay_out, 4: place_tokens, 5: name_owners}

            def step(n, phases, own):
                before2, before, this, after = phases
                if before is not None:
                    act_low(n - 1, before)
                if fresh(before2, before):
                    weights_low(n - 1, before, d_raw, d_w, d_hi, d_ready)
                if fresh(this, after):
                    weights_low(n + 1, after, g_raw, g_w, g_hi, g_ready)
                if own == RANK_STEP:
                    read_counts()
                products(n, this)
                if after == ROUTE:
                    hT_low(n + 1)
                if fresh(this, after):
                    weights_low(n + 1, after, u_raw, u_w, u_hi, u_ready)
                if isinstance(own, tuple):
                    dve.wait_ge(down_read, n - 1)
                    for tile in own:
                        add_routed(n - C0 + tile)
                    dve.wait_ge(gathered, TOPK * (n - C0) + (TOPK * (own[-1] + 1) + SEED))
                if before not in (None, ROUTE):
                    add_shared(n - 1, before)
                if own in routing:
                    routing[own]()

            dve.sem_inc(gathered, SEED)
            weights_low(0, 0, g_raw, g_w, g_hi, g_ready)
            weights_low(0, 0, u_raw, u_w, u_hi, u_ready)

            doubles = [C0 + 2 + 3 * d for d in range(NT - (STEPS - C0))]

            def own(n):
                if n in routing:
                    return n
                if n < C0:
                    return None
                before = sum(d < n for d in doubles)
                return (before, before + 1) if n in doubles else (before,)

            runs(dve, step, own)
            act_low(LAST, phase(LAST))
            add_shared(LAST, phase(LAST))


def program(nc, ins, out):
    xt_dram = nc.dram_tensor("xt_scratch", [B, P, 2, EC, S], F32, kind="Internal").ap()
    slot_rows = nc.dram_tensor("slot_rows", [SLOTS, E], F32, kind="Internal").ap()
    slot_out = nc.dram_tensor("slot_out", [ROUTED * TS, E], F32, kind="Internal").ap()
    with Space(nc, "all") as top:
        ident = top.sb("ident", [P, P])
        neg_half = top.sb("neg_half", [P, NT])
        x = top.sb("x", [P, NT, E])
        stats = top.sb("stats", [P, NT, 6])
        make_constants(nc, ident, neg_half)
        with Space(nc, "weights") as keep:
            xt = keep.sb("xt", [P, 2, EC, S], F32R)
            w_raw = keep.sb("w_raw", [P, 4, EC * HG * P])
            w = keep.sb("w", [P, 4, 2, EC * HG * P], F32R)
            with Space(nc, "whole") as s:
                xT = s.sb("xT", [P, 2, EC, N], F32R)
                first_layernorm(nc, x, stats, xT, xt, w, w_raw, ident, neg_half, ins["x"], xt_dram, ins["wqkv"])
            attention(nc, x, stats, xt, w, w_raw, ident, neg_half, xt_dram, ins["wqkv"], ins["wo"], ins["q_scale"],
                      ins["k_scale"], slot_rows)
        rows = top.sb("rows", [P, NT, E])
        exp_logits = top.sb("exp_logits", [P, NT, XP])
        exp_gate = top.sb("exp_gate", [P, NT])
        with Space(nc, "second") as s:
            xT = s.sb("xT", [P, 2, EC, N], F32R)
            retention(nc, x, stats, xT, rows, ident, neg_half, ins["ctxT"], ins["head_w"], ins["decayT"],
                      ins["gate_w"], ins["out_w"], ins["gamma"], ins["beta"], ins["router"], xt_dram,
                      exp_logits, exp_gate)
        experts(nc, x, rows, exp_logits, exp_gate, ident, xt_dram, slot_rows, slot_out,
                (ins["w_gate"], ins["sh_gate"]), (ins["w_up"], ins["sh_up"]), (ins["w_down"], ins["sh_down"]), out)


def decay_masks():
    heads = E // P
    gam = 1.0 - 2.0 ** (-5.0 - np.arange(heads))
    d = np.arange(S)[:, None] - np.arange(S)[None, :]
    m = np.where(d >= 0, gam[:, None, None] ** (-d[None].astype(float)), 0.0)
    m = m / np.sqrt(m.sum(axis=-1, keepdims=True)).transpose(0, 2, 1) / np.sqrt(P)
    return np.ascontiguousarray(m.transpose(0, 2, 1).reshape(heads, 2, P, S).transpose(0, 2, 1, 3)).astype(np.float32)


def kernel(**inputs):
    from concourse import bacc
    from concourse.bass_utils import run_bass_kernel_spmd

    a = {k: np.ascontiguousarray(v) for k, v in inputs.items()}
    qkv = np.stack([a[f"L0_attn_w{c}"].reshape(EC, P, G, HG * P) for c in "qkv"])
    def wide(w):
        return np.ascontiguousarray(w.reshape(-1, EC, P, w.shape[-1]).transpose(0, 2, 1, 3))

    def deep(w):
        padded = np.zeros((w.shape[0], WP, E), np.float32)
        padded[:, :w.shape[1]] = w
        return np.ascontiguousarray(padded.reshape(-1, 3, P, E).transpose(0, 2, 1, 3))

    def parts(w):
        padded = np.zeros((E, SHARED * WP), np.float32)
        padded[:, :WS] = w
        return np.ascontiguousarray(padded.reshape(E, SHARED, WP).transpose(1, 0, 2))

    down = np.zeros((SHARED * WP, E), np.float32)
    down[:WS] = a["L0_ffn_sh_down"]
    router = np.zeros((P, EC, W), np.float32)
    router[:, :, :XP] = a["L0_ffn_router_w"].reshape(XP, EC, P).transpose(2, 1, 0)
    router[:, :, XP] = a["L0_ffn_sh_gate_w"].reshape(EC, P).T
    arrays = {
        "x": a["x"],
        "wqkv": np.ascontiguousarray(qkv.transpose(3, 0, 2, 1, 4)).reshape(G, 3, P, EC * HG * P),
        "wo": a["L0_attn_wo"].reshape(G, HG, P, E),
        "q_scale": a["L0_attn_q_scale"],
        "k_scale": a["L0_attn_k_scale"],
        "ctxT": np.ascontiguousarray(a["ctx_2048"].reshape(N, EC, P).transpose(1, 2, 0)),
        "head_w": a["L0_xattn_Wh"],
        "decayT": decay_masks(),
        "gate_w": a["L0_xattn_wg_w"],
        "out_w": a["L0_xattn_wo_w"],
        "gamma": a["L0_xattn_gn_gamma"],
        "beta": a["L0_xattn_gn_beta"],
        "router": router,
        "w_gate": wide(a["L0_ffn_w_gate"]),
        "w_up": wide(a["L0_ffn_w_up"]),
        "w_down": deep(a["L0_ffn_w_down"]),
        "sh_gate": wide(parts(a["L0_ffn_sh_gate"])),
        "sh_up": wide(parts(a["L0_ffn_sh_up"])),
        "sh_down": deep(down.reshape(SHARED, WP, E)),
    }
    nc = bacc.Bacc("TRN2", target_bir_lowering=False, num_devices=1)
    ins = {k: nc.dram_tensor(f"in_{k}", v.shape, mybir.dt.from_np(v.dtype), kind="ExternalInput").ap()
           for k, v in arrays.items()}
    out = nc.dram_tensor("out", [B, S, E], F32, kind="ExternalOutput").ap()
    program(nc, ins, out)
    r = run_bass_kernel_spmd(nc, [{f"in_{k}": v for k, v in arrays.items()}], core_ids=[0])
    return r.results[0]["out"]
```
